# Optimizing a Trainium2 kernel written in Bass

```python
import numpy as np
import jax
import jax.numpy as jnp

def _softmax(x, axis=-1):
    return jax.nn.softmax(x, axis=axis)

def _gelu(x):
    return jax.nn.gelu(x, approximate=True)

def _silu(x):
    return jax.nn.silu(x)

def _sigmoid(x):
    return jax.nn.sigmoid(x)

def _layernorm(x, axis=-1, eps=1e-05):
    m = jnp.mean(x, axis=axis, keepdims=True)
    v = jnp.var(x, axis=axis, keepdims=True)
    return (x - m) / jnp.sqrt(v + eps)

def _scatter_add(tgt, idx, src, axis=0):
    return tgt.at[idx].add(src)

def _segment_sum(src, seg, n):
    return jax.ops.segment_sum(src, seg, n)
kernel_name = 'mk_perceiver_d2_seqx_r8_ca4995'

def setup_inputs(seed: int=0):
    np.random.seed(seed)
    _w = jnp.asarray

    def _rec_inputs():
        import jax
        import jax.numpy as jnp
        _rk = jax.random.key(seed)
        x = 0.002226 + 0.9996 * jax.random.normal(jax.random.fold_in(_rk, 1), (128, 32, 128), jnp.float32)
        _lenS = 32 - jax.random.randint(jax.random.fold_in(_rk, 7), (128,), 0, max(1, 32 // 4) + 1, jnp.int32)
        _lenS2 = 257 - jax.random.randint(jax.random.fold_in(_rk, 8), (128,), 0, max(1, 257 // 4) + 1, jnp.int32)
        _ctx_1024P = jax.random.normal(jax.random.fold_in(_rk, 11), (128, 16, 128), jnp.float32)
        _ctx_1024c = jax.random.dirichlet(jax.random.fold_in(_rk, 511), 0.3 * jnp.ones((16,), jnp.float32), (128, 257))
        _ctx_1024t = jnp.einsum('bsk,bkd->bsd', _ctx_1024c, _ctx_1024P)
        _ctx_1024t = _ctx_1024t * jax.lax.rsqrt(jnp.mean(jnp.square(_ctx_1024t)) + 1e-12) * 0.953939
        ctx_1024 = -0.000125008 + 0.999885 * (_ctx_1024t + 0.3 * jax.random.normal(jax.random.fold_in(_rk, 611), (128, 257, 128), jnp.float32))
        return (x, ctx_1024)
    x, ctx_1024 = _rec_inputs()

    def _L0_xattn_setup():
        import jax, jax.numpy as jnp
        import numpy as np
        B, M, N, DIM, DH, H = (8, 512, 64, 128, 128, 8)
        INNER = DH * H
        EPS = 1e-05

        def _layernorm(x, g, b):
            mu = jnp.mean(x, axis=-1, keepdims=True)
            var = jnp.var(x, axis=-1, keepdims=True)
            return (x - mu) * jax.lax.rsqrt(var + EPS) * g + b
        key = jax.random.key(seed)
        ks = jax.random.split(key, 8)
        sd = 0.02
        return {'x': jax.random.normal(ks[0], (B, M, DIM), jnp.float32), 'latents': jax.random.normal(ks[1], (B, N, DIM), jnp.float32), 'gamma_media': jnp.ones((DIM,), jnp.float32), 'beta_media': jnp.zeros((DIM,), jnp.float32), 'gamma_lat': jnp.ones((DIM,), jnp.float32), 'beta_lat': jnp.zeros((DIM,), jnp.float32), 'Wq': jax.random.normal(ks[2], (DIM, INNER), jnp.float32) * sd, 'bq': jnp.zeros((INNER,), jnp.float32), 'Wkv': jax.random.normal(ks[3], (DIM, 2 * INNER), jnp.float32) * sd, 'bkv': jnp.zeros((2 * INNER,), jnp.float32), 'Wo': jax.random.normal(ks[4], (INNER, DIM), jnp.float32) * sd, 'bo': jnp.zeros((DIM,), jnp.float32)}
    _L0_xattn_all = _L0_xattn_setup()
    _L0_xattn_in = {k: v for k, v in _L0_xattn_all.items() if k in ('gamma_media', 'beta_media', 'gamma_lat', 'beta_lat', 'Wq', 'bq', 'Wkv', 'bkv', 'Wo', 'bo')}
    del _L0_xattn_all

    def _L0_attn_setup():
        import jax, jax.numpy as jnp
        import numpy as np
        HEADS = 64
        DIM_HEAD = 64
        SCALE = DIM_HEAD ** (-0.5)
        EPS = 1e-06
        key = jax.random.key(seed)
        ks = jax.random.split(key, 6)
        b, s, dim = (2, 512, 128)
        inner = HEADS * DIM_HEAD
        std = 0.02
        return {'x': jax.random.normal(ks[0], (b, s, dim), dtype=jnp.float32), 'Wq': jax.random.normal(ks[1], (dim, inner), dtype=jnp.float32) * std, 'Wk': jax.random.normal(ks[2], (dim, inner), dtype=jnp.float32) * std, 'Wv': jax.random.normal(ks[3], (dim, inner), dtype=jnp.float32) * std, 'Wo': jax.random.normal(ks[4], (inner, dim), dtype=jnp.float32) * std, 'bo': jnp.zeros((dim,), dtype=jnp.float32)}
    _L0_attn_all = _L0_attn_setup()
    _L0_attn_in = {k: v for k, v in _L0_attn_all.items() if k in ('Wq', 'Wk', 'Wv', 'Wo', 'bo')}
    del _L0_attn_all

    def _L0_ffn_setup():
        import jax, jax.numpy as jnp
        import numpy as np
        THRESHOLD = 0.1
        key = jax.random.key(seed)
        k1, k2, k3 = jax.random.split(key, 3)
        B, S, D, E = (4, 512, 128, 8)
        inputs = jax.random.normal(k1, (B, S, D), dtype=jnp.float32)
        gate_w = jax.random.normal(k2, (D, E), dtype=jnp.float32) * 0.02
        gate_b = jnp.zeros((E,), dtype=jnp.float32)
        expert_w = jax.random.normal(k3, (E, D, D), dtype=jnp.float32) * 0.02
        expert_b = jnp.zeros((E, D), dtype=jnp.float32)
        return {'inputs': inputs, 'gate_w': gate_w, 'gate_b': gate_b, 'expert_w': expert_w, 'expert_b': expert_b}
    _L0_ffn_all = _L0_ffn_setup()
    _L0_ffn_in = {k: v for k, v in _L0_ffn_all.items() if k in ('gate_w', 'gate_b', 'expert_w', 'expert_b')}
    del _L0_ffn_all

    def _L1_xattn_setup():
        import jax, jax.numpy as jnp
        import numpy as np
        D = 128
        NUM_ITERS = 3
        EPS = 1e-06
        SCALE = D ** (-0.5)

        def rmsnorm(x, w, eps=EPS):
            return x * jax.lax.rsqrt(jnp.mean(x * x, axis=-1, keepdims=True) + eps) * w

        def gru_cell(x, h, wih, whh, bih, bhh):
            gx = x @ wih.T + bih
            gh = h @ whh.T + bhh
            xr, xz, xn = jnp.split(gx, 3, axis=-1)
            hr, hz, hn = jnp.split(gh, 3, axis=-1)
            r = jax.nn.sigmoid(xr + hr)
            z = jax.nn.sigmoid(xz + hz)
            n = jnp.tanh(xn + r * hn)
            return (1.0 - z) * n + z * h
        key = jax.random.key(seed)
        ks = jax.random.split(key, 8)
        B, K, M, d = (8, 64, 512, D)
        w_std = d ** (-0.5)
        return {'slots': jax.random.normal(ks[0], (B, K, d), jnp.float32), 'P': jax.random.normal(ks[1], (B, M, d), jnp.float32), 'Wq': jax.random.normal(ks[2], (d, d), jnp.float32) * w_std, 'Wk': jax.random.normal(ks[3], (d, d), jnp.float32) * w_std, 'Wv': jax.random.normal(ks[4], (d, d), jnp.float32) * w_std, 'gru_wih': jax.random.normal(ks[5], (3 * d, d), jnp.float32) * w_std, 'gru_whh': jax.random.normal(ks[6], (3 * d, d), jnp.float32) * w_std, 'gru_bih': jnp.zeros((3 * d,), jnp.float32), 'gru_bhh': jnp.zeros((3 * d,), jnp.float32), 'slot_norm_w': jnp.ones((d,), jnp.float32), 'input_norm_w': jnp.ones((d,), jnp.float32)}
    _L1_xattn_all = _L1_xattn_setup()
    _L1_xattn_in = {k: v for k, v in _L1_xattn_all.items() if k in ('Wq', 'Wk', 'Wv', 'gru_wih', 'gru_whh', 'gru_bih', 'gru_bhh', 'slot_norm_w', 'input_norm_w')}
    del _L1_xattn_all

    def _L1_attn_setup():
        import jax, jax.numpy as jnp
        import numpy as np
        HIDDEN = 128
        HEADS = 16
        HEAD_DIM = HIDDEN // HEADS
        ROPE_BASE = 10000.0

        def _rope_cos_sin(seq_len, dim):
            inv_freq = 1.0 / ROPE_BASE ** (jnp.arange(0, dim, 2, dtype=jnp.float32) / dim)
            t = jnp.arange(seq_len, dtype=jnp.float32)
            freqs = jnp.einsum('i,j->ij', t, inv_freq)
            emb = jnp.concatenate([freqs, freqs], axis=-1)
            return (jnp.cos(emb), jnp.sin(emb))

        def _apply_rope(x, cos, sin):
            x1, x2 = (x[..., 0::2], x[..., 1::2])
            c = cos[..., :x1.shape[-1]]
            s = sin[..., :x1.shape[-1]]
            return jnp.concatenate([x1 * c - x2 * s, x1 * s + x2 * c], axis=-1)
        key = jax.random.key(seed)
        ks = jax.random.split(key, 9)
        B, S = (4, 256)
        lim = 1.0 / np.sqrt(HIDDEN)

        def lin(kw, kb):
            W = jax.random.uniform(kw, (HIDDEN, HIDDEN), jnp.float32, -lim, lim)
            b = jax.random.uniform(kb, (HIDDEN,), jnp.float32, -lim, lim)
            return (W, b)
        Wq, bq = lin(ks[0], ks[1])
        Wk, bk = lin(ks[2], ks[3])
        Wv, bv = lin(ks[4], ks[5])
        Wo, bo = lin(ks[6], ks[7])
        x = jax.random.normal(ks[8], (B, S, HIDDEN), jnp.float32)
        return {'x': x, 'Wq': Wq, 'bq': bq, 'Wk': Wk, 'bk': bk, 'Wv': Wv, 'bv': bv, 'Wo': Wo, 'bo': bo}
    _L1_attn_all = _L1_attn_setup()
    _L1_attn_in = {k: v for k, v in _L1_attn_all.items() if k in ('Wq', 'bq', 'Wk', 'bk', 'Wv', 'bv', 'Wo', 'bo')}
    del _L1_attn_all

    def _L1_ffn_setup():
        import jax, jax.numpy as jnp
        import numpy as np
        NUM_EXPERTS = 8
        TOP_K = 2
        key = jax.random.key(seed)
        ks = jax.random.split(key, 4)
        B, S, H, F = (4, 512, 128, 512)
        x = jax.random.normal(ks[0], (B, S, H), dtype=jnp.float32)
        router_w = jax.random.normal(ks[1], (H, NUM_EXPERTS), dtype=jnp.float32) * 0.02
        w1 = jax.random.normal(ks[2], (H, F), dtype=jnp.float32) * 0.02
        b1 = jnp.zeros((F,), dtype=jnp.float32)
        w2 = jax.random.normal(ks[3], (F, H), dtype=jnp.float32) * 0.02
        b2 = jnp.zeros((H,), dtype=jnp.float32)
        return {'x': x, 'router_w': router_w, 'w1': w1, 'b1': b1, 'w2': w2, 'b2': b2}
    _L1_ffn_all = _L1_ffn_setup()
    _L1_ffn_in = {k: v for k, v in _L1_ffn_all.items() if k in ('router_w', 'w1', 'b1', 'w2', 'b2')}
    del _L1_ffn_all
    return {'x': x, 'ctx_1024': ctx_1024, 'L0_xattn_gamma_media': _L0_xattn_in['gamma_media'], 'L0_xattn_beta_media': _L0_xattn_in['beta_media'], 'L0_xattn_gamma_lat': _L0_xattn_in['gamma_lat'], 'L0_xattn_beta_lat': _L0_xattn_in['beta_lat'], 'L0_xattn_Wq': _L0_xattn_in['Wq'], 'L0_xattn_bq': _L0_xattn_in['bq'], 'L0_xattn_Wkv': _L0_xattn_in['Wkv'], 'L0_xattn_bkv': _L0_xattn_in['bkv'], 'L0_xattn_Wo': _L0_xattn_in['Wo'], 'L0_xattn_bo': _L0_xattn_in['bo'], 'L0_attn_Wq': _L0_attn_in['Wq'], 'L0_attn_Wk': _L0_attn_in['Wk'], 'L0_attn_Wv': _L0_attn_in['Wv'], 'L0_attn_Wo': _L0_attn_in['Wo'], 'L0_attn_bo': _L0_attn_in['bo'], 'L0_ffn_gate_w': _L0_ffn_in['gate_w'], 'L0_ffn_gate_b': _L0_ffn_in['gate_b'], 'L0_ffn_expert_w': _L0_ffn_in['expert_w'], 'L0_ffn_expert_b': _L0_ffn_in['expert_b'], 'L1_xattn_Wq': _L1_xattn_in['Wq'], 'L1_xattn_Wk': _L1_xattn_in['Wk'], 'L1_xattn_Wv': _L1_xattn_in['Wv'], 'L1_xattn_gru_wih': _L1_xattn_in['gru_wih'], 'L1_xattn_gru_whh': _L1_xattn_in['gru_whh'], 'L1_xattn_gru_bih': _L1_xattn_in['gru_bih'], 'L1_xattn_gru_bhh': _L1_xattn_in['gru_bhh'], 'L1_xattn_slot_norm_w': _L1_xattn_in['slot_norm_w'], 'L1_xattn_input_norm_w': _L1_xattn_in['input_norm_w'], 'L1_attn_Wq': _L1_attn_in['Wq'], 'L1_attn_bq': _L1_attn_in['bq'], 'L1_attn_Wk': _L1_attn_in['Wk'], 'L1_attn_bk': _L1_attn_in['bk'], 'L1_attn_Wv': _L1_attn_in['Wv'], 'L1_attn_bv': _L1_attn_in['bv'], 'L1_attn_Wo': _L1_attn_in['Wo'], 'L1_attn_bo': _L1_attn_in['bo'], 'L1_ffn_router_w': _L1_ffn_in['router_w'], 'L1_ffn_w1': _L1_ffn_in['w1'], 'L1_ffn_b1': _L1_ffn_in['b1'], 'L1_ffn_w2': _L1_ffn_in['w2'], 'L1_ffn_b2': _L1_ffn_in['b2']}

def reference(x, ctx_1024, L0_xattn_gamma_media, L0_xattn_beta_media, L0_xattn_gamma_lat, L0_xattn_beta_lat, L0_xattn_Wq, L0_xattn_bq, L0_xattn_Wkv, L0_xattn_bkv, L0_xattn_Wo, L0_xattn_bo, L0_attn_Wq, L0_attn_Wk, L0_attn_Wv, L0_attn_Wo, L0_attn_bo, L0_ffn_gate_w, L0_ffn_gate_b, L0_ffn_expert_w, L0_ffn_expert_b, L1_xattn_Wq, L1_xattn_Wk, L1_xattn_Wv, L1_xattn_gru_wih, L1_xattn_gru_whh, L1_xattn_gru_bih, L1_xattn_gru_bhh, L1_xattn_slot_norm_w, L1_xattn_input_norm_w, L1_attn_Wq, L1_attn_bq, L1_attn_Wk, L1_attn_bk, L1_attn_Wv, L1_attn_bv, L1_attn_Wo, L1_attn_bo, L1_ffn_router_w, L1_ffn_w1, L1_ffn_b1, L1_ffn_w2, L1_ffn_b2):
    import jax
    import jax.numpy as jnp

    def _L0_xattn_ref(x, latents, gamma_media, beta_media, gamma_lat, beta_lat, Wq, bq, Wkv, bkv, Wo, bo):
        import jax, jax.numpy as jnp
        import numpy as np
        B, M, N, DIM, DH, H = (8, 512, 64, 128, 128, 8)
        INNER = DH * H
        EPS = 1e-05

        def _layernorm(x, g, b):
            mu = jnp.mean(x, axis=-1, keepdims=True)
            var = jnp.var(x, axis=-1, keepdims=True)
            return (x - mu) * jax.lax.rsqrt(var + EPS) * g + b
        b = x.shape[0]
        xn = _layernorm(x, gamma_media, beta_media)
        ln = _layernorm(latents, gamma_lat, beta_lat)
        q = ln @ Wq + bq
        kv_input = jnp.concatenate([xn, ln], axis=1)
        kv = kv_input @ Wkv + bkv
        k, v = jnp.split(kv, 2, axis=-1)

        def to_heads(t):
            return t.reshape(b, t.shape[1], H, DH).transpose(0, 2, 1, 3)
        q, k, v = (to_heads(q), to_heads(k), to_heads(v))
        q = q * DH ** (-0.5)
        sim = jnp.einsum('bhid,bhjd->bhij', q, k)
        attn = jax.nn.softmax(sim, axis=-1)
        out = jnp.einsum('bhij,bhjd->bhid', attn, v)
        out = out.transpose(0, 2, 1, 3).reshape(b, -1, INNER)
        return out @ Wo + bo

    def _L0_attn_ref(x, Wq, Wk, Wv, Wo, bo):
        import jax, jax.numpy as jnp
        import numpy as np
        HEADS = 64
        DIM_HEAD = 64
        SCALE = DIM_HEAD ** (-0.5)
        EPS = 1e-06
        b, s, dim = x.shape
        h, dh = (HEADS, DIM_HEAD)
        q = (x @ Wq).reshape(b, s, h, dh)
        k = (x @ Wk).reshape(b, s, h, dh)
        v = (x @ Wv).reshape(b, s, h, dh)
        q = jax.nn.relu(q) * SCALE
        k = jax.nn.relu(k)
        kv = jnp.einsum('bsid,bsjd->bsdj', k, v)
        out = jnp.einsum('bsid,bsdj->bsij', q, kv)
        q_norm = jnp.einsum('bsid,bsd->bsi', q, k.sum(axis=2))
        out = out / (q_norm[..., None] + EPS)
        out = out.reshape(b, s, h * h)
        return out @ Wo + bo

    def _L0_ffn_ref(inputs, gate_w, gate_b, expert_w, expert_b):
        import jax, jax.numpy as jnp
        import numpy as np
        THRESHOLD = 0.1
        d = inputs.shape[-1]
        x = inputs.reshape(-1, d)
        gate_logits = jax.nn.softmax(x @ gate_w + gate_b, axis=-1)
        selected = (gate_logits >= THRESHOLD).astype(x.dtype)
        weights = gate_logits * selected
        wsum = jnp.sum(weights, axis=-1, keepdims=True)
        weights = weights / jnp.where(wsum == 0, jnp.ones_like(wsum), wsum)
        E = expert_w.shape[0]
        out = jnp.zeros((x.shape[0], expert_w.shape[-1]), dtype=x.dtype)
        for e in range(E):
            out = out + weights[:, e:e + 1] * (x @ expert_w[e] + expert_b[e])
        return out.reshape(*inputs.shape[:-1], out.shape[-1])

    def _L1_xattn_ref(slots, P, Wq, Wk, Wv, gru_wih, gru_whh, gru_bih, gru_bhh, slot_norm_w, input_norm_w):
        import jax, jax.numpy as jnp
        import numpy as np
        D = 128
        NUM_ITERS = 3
        EPS = 1e-06
        SCALE = D ** (-0.5)

        def rmsnorm(x, w, eps=EPS):
            return x * jax.lax.rsqrt(jnp.mean(x * x, axis=-1, keepdims=True) + eps) * w

        def gru_cell(x, h, wih, whh, bih, bhh):
            gx = x @ wih.T + bih
            gh = h @ whh.T + bhh
            xr, xz, xn = jnp.split(gx, 3, axis=-1)
            hr, hz, hn = jnp.split(gh, 3, axis=-1)
            r = jax.nn.sigmoid(xr + hr)
            z = jax.nn.sigmoid(xz + hz)
            n = jnp.tanh(xn + r * hn)
            return (1.0 - z) * n + z * h
        Pn = rmsnorm(P, input_norm_w)
        k_proj = Pn @ Wk.T
        v_proj = Pn @ Wv.T
        for _ in range(NUM_ITERS):
            sn = rmsnorm(slots, slot_norm_w)
            q_proj = sn @ Wq.T
            scores = jnp.einsum('bkd,bmd->bkm', q_proj, k_proj) * SCALE
            attn = jax.nn.softmax(scores, axis=-2)
            attn = attn / (jnp.sum(attn, axis=-1, keepdims=True) + EPS)
            updates = jnp.einsum('bkm,bmd->bkd', attn, v_proj)
            slots = gru_cell(updates, slots, gru_wih, gru_whh, gru_bih, gru_bhh)
        return slots

    def _L1_attn_ref(x, Wq, bq, Wk, bk, Wv, bv, Wo, bo):
        import jax, jax.numpy as jnp
        import numpy as np
        HIDDEN = 128
        HEADS = 16
        HEAD_DIM = HIDDEN // HEADS
        ROPE_BASE = 10000.0

        def _rope_cos_sin(seq_len, dim):
            inv_freq = 1.0 / ROPE_BASE ** (jnp.arange(0, dim, 2, dtype=jnp.float32) / dim)
            t = jnp.arange(seq_len, dtype=jnp.float32)
            freqs = jnp.einsum('i,j->ij', t, inv_freq)
            emb = jnp.concatenate([freqs, freqs], axis=-1)
            return (jnp.cos(emb), jnp.sin(emb))

        def _apply_rope(x, cos, sin):
            x1, x2 = (x[..., 0::2], x[..., 1::2])
            c = cos[..., :x1.shape[-1]]
            s = sin[..., :x1.shape[-1]]
            return jnp.concatenate([x1 * c - x2 * s, x1 * s + x2 * c], axis=-1)
        B, S, _ = x.shape
        scale = HEAD_DIM ** (-0.5)

        def proj(W, b):
            y = jnp.einsum('bsd,ed->bse', x, W) + b
            return y.reshape(B, S, HEADS, HEAD_DIM).transpose(0, 2, 1, 3)
        q = proj(Wq, bq)
        k = proj(Wk, bk)
        v = proj(Wv, bv)
        cos, sin = _rope_cos_sin(S, HEAD_DIM)
        cos = cos[None, None]
        sin = sin[None, None]
        q = _apply_rope(q, cos, sin) * scale
        k = _apply_rope(k, cos, sin)
        attn = jnp.einsum('bhsd,bhtd->bhst', q, k)
        attn = jax.nn.softmax(attn, axis=-1)
        out = jnp.einsum('bhst,bhtd->bhsd', attn, v)
        out = out.transpose(0, 2, 1, 3).reshape(B, S, HIDDEN)
        return jnp.einsum('bsd,ed->bse', out, Wo) + bo

    def _L1_ffn_ref(x, router_w, w1, b1, w2, b2):
        import jax, jax.numpy as jnp
        import numpy as np
        NUM_EXPERTS = 8
        TOP_K = 2
        B, S, H = x.shape
        xt = x.reshape(-1, H)
        router_logits = jnp.matmul(xt, router_w)
        router_probs = jax.nn.softmax(router_logits, axis=-1)
        top_k_probs, top_k_indices = jax.lax.top_k(router_probs, TOP_K)
        top_k_probs = top_k_probs / jnp.sum(top_k_probs, axis=-1, keepdims=True)
        one_hot = jax.nn.one_hot(top_k_indices, NUM_EXPERTS, dtype=xt.dtype)
        combine = jnp.einsum('tk,tke->te', top_k_probs, one_hot)
        expert_out = jnp.matmul(jax.nn.gelu(jnp.matmul(xt, w1) + b1), w2) + b2
        out = expert_out * jnp.sum(combine, axis=-1, keepdims=True)
        return out.reshape(B, S, H)
    x = x + _L0_xattn_ref(ctx_1024, _layernorm(x, axis=-1), L0_xattn_gamma_media, L0_xattn_beta_media, L0_xattn_gamma_lat, L0_xattn_beta_lat, L0_xattn_Wq, L0_xattn_bq, L0_xattn_Wkv, L0_xattn_bkv, L0_xattn_Wo, L0_xattn_bo)
    x = x + _L0_attn_ref(_layernorm(x, axis=-1), L0_attn_Wq, L0_attn_Wk, L0_attn_Wv, L0_attn_Wo, L0_attn_bo)
    x = x + _L0_ffn_ref(_layernorm(x, axis=-1), L0_ffn_gate_w, L0_ffn_gate_b, L0_ffn_expert_w, L0_ffn_expert_b)
    x = x + _L1_xattn_ref(_layernorm(x, axis=-1), ctx_1024, L1_xattn_Wq, L1_xattn_Wk, L1_xattn_Wv, L1_xattn_gru_wih, L1_xattn_gru_whh, L1_xattn_gru_bih, L1_xattn_gru_bhh, L1_xattn_slot_norm_w, L1_xattn_input_norm_w)
    x = x + _L1_attn_ref(_layernorm(x, axis=-1), L1_attn_Wq, L1_attn_bq, L1_attn_Wk, L1_attn_bk, L1_attn_Wv, L1_attn_bv, L1_attn_Wo, L1_attn_bo)
    x = x + _L1_ffn_ref(_layernorm(x, axis=-1), L1_ffn_router_w, L1_ffn_w1, L1_ffn_b1, L1_ffn_w2, L1_ffn_b2)
    return x

_drawn_inputs = setup_inputs


def setup_inputs(seed=0):
    import zlib

    import numpy as np

    out = dict(_drawn_inputs(seed))
    spreads = {'L0_xattn_gamma_media': (1.0, 0.6),
     'L0_xattn_beta_media': (0.0, 0.705),
     'L0_xattn_gamma_lat': (1.0, 0.6),
     'L0_xattn_beta_lat': (0.0, 0.8),
     'L0_xattn_bq': (0.0, 2.0),
     'L0_xattn_bkv': (0.0, 0.1),
     'L0_xattn_bo': (0.0, 0.1),
     'L0_attn_bo': (0.0, 0.1),
     'L0_ffn_gate_b': (0.0, 0.269),
     'L0_ffn_expert_b': (0.0, 0.1),
     'L1_xattn_gru_bih': (0.0, 0.1),
     'L1_xattn_gru_bhh': (0.0, 0.1),
     'L1_xattn_slot_norm_w': (1.0, 0.6),
     'L1_xattn_input_norm_w': (1.0, 0.2),
     'L1_ffn_b1': (0.0, 0.426),
     'L1_ffn_b2': (0.0, 0.1)}
    factors = {'L0_xattn_Wq': 8.0,
     'L0_attn_Wk': 22.711,
     'L1_attn_Wq': 3.712,
     'L1_attn_bq': 8.0,
     'L1_attn_Wk': 3.688,
     'L1_attn_bk': 8.0,
     'L1_ffn_router_w': 64.0}
    for name, (base, spread) in spreads.items():
        noise = np.random.default_rng([zlib.crc32(name.encode()), seed]).standard_normal(out[name].shape)
        drawn = base * np.exp(spread * noise) if base else spread * noise
        out[name] = jnp.asarray(drawn.astype(out[name].dtype))
    for name, factor in factors.items():
        out[name] = (out[name] * factor).astype(out[name].dtype)
    return out
```

```python
from contextlib import ExitStack

import numpy as np

import concourse.bass as bass
from concourse import mybir

F32 = mybir.dt.float32
ALU = mybir.AluOpType
ACT = mybir.ActivationFunctionType
AX = mybir.AxisListType.X

P = 128
D = 128
B = 128
S = 32
M = 257
TOK = B * S
CH = 512
NCH = TOK // CH
BPC = CH // S

XH = 8
XROWS = 97
XLAT = M - 2 * XROWS
XKEYS = M + S
XK = [XROWS, XROWS, S + XLAT]
LH = 64
LD = 64
LT = 256
LHALF = LT // 2
NLC = TOK // LT
E = 8
ITERS = 3
ST = 86
SK = [86, 86, 85]
RH = 16
RD = 8
FF = 512

VECS = ["g_media", "b_media", "g_lat", "b_lat"] + [f"bq{h}" for h in range(8)] + [f"bv{h}" for h in range(8)] + [
    "x_bo", "a_bo", "slot_w", "input_w", "bih_r", "bih_z", "bih_n", "bhh_r", "bhh_z", "bhh_n",
    "r_bqa", "r_bqb", "r_bka", "r_bkb", "r_bv", "r_bo", "f_b1_0", "f_b1_1", "f_b1_2", "f_b1_3", "f_b2",
]
VCOL = {n: i for i, n in enumerate(VECS)}


def run_steps(eng, step, total, unroll):
    for n in range(unroll):
        step(n, n % unroll)
    with eng.Fori(unroll, total - 2 * unroll + 1, unroll) as base:
        for k in range(unroll):
            step(base + k, k)
    for n in range(total - unroll, total):
        step(n, n % unroll)


def inside(n, total):
    return not isinstance(n, int) or 0 <= n < total


class Core:
    pass


def layer_norm(core, tag, src, dst, eps, gamma=None, beta=None):
    nc = core.nc
    s = core.norm_sems
    mean_ready, centred_ready, square_ready = s["mean_ready"], s["centred_ready"], s["square_ready"]
    var_ready, log_ready, rstd_ready, normed = s["var_ready"], s["log_ready"], s["rstd_ready"], s["normed"]
    done = core.norms[0] * NCH
    core.norms[0] += 1
    banks = core.banks
    with ExitStack() as ctx:
        def sb(name, shape):
            return ctx.enter_context(nc.sbuf_tensor(f"{tag}_{name}", shape, F32))

        centred = sb("centred", [P, 2, CH])
        square = sb("square", [P, 2, CH])
        logvar = sb("logvar", [P, 2, CH])
        rstd = sb("rstd", [P, 2, CH])
        block = ctx.enter_context(nc.Block())

        @block.tensor
        def _(pe):
            with pe.Fori(0, NCH - 1, 2) as c0:
                for u in range(2):
                    pe.matmul(banks[u][:, :], core.mean_mat[:, :], src[:, bass.ds((c0 + u) * CH, CH)],
                              start=True, stop=True).then_inc(mean_ready, 1)
                for u in range(2):
                    pe.wait_ge(square_ready, done + c0 + u + 1)
                    pe.matmul(banks[2 + u][:, :], core.mean_mat[:, :], square[:, u, :],
                              start=True, stop=True).then_inc(var_ready, 1)

        @block.vector
        def _(dve):
            with dve.Fori(0, NCH - 1, 2) as c0:
                dve.wait_ge(normed, done + c0)
                for u in range(2):
                    dve.wait_ge(mean_ready, done + c0 + u + 1)
                    dve.tensor_tensor(centred[:, u, :], src[:, bass.ds((c0 + u) * CH, CH)], banks[u][:, :],
                                      ALU.subtract).then_inc(centred_ready, 1)
                for u in range(2):
                    dve.wait_ge(rstd_ready, done + c0 + u + 1)
                    out = dst[:, bass.ds((c0 + u) * CH, CH)]
                    dve.tensor_tensor(out, centred[:, u, :], rstd[:, u, :], ALU.mult).then_inc(normed, 1)
                if gamma is not None:
                    for u in range(2):
                        dve.wait_ge(normed, done + c0 + u + 1)
                        out = dst[:, bass.ds((c0 + u) * CH, CH)]
                        dve.tensor_scalar(out, out, gamma, beta, ALU.mult, ALU.add)

        @block.scalar
        def _(act):
            with act.Fori(0, NCH - 1, 2) as c0:
                act.wait_ge(rstd_ready, done + c0)
                for u in range(2):
                    act.wait_ge(centred_ready, done + c0 + u + 1)
                    act.activation(square[:, u, :], centred[:, u, :], ACT.Square).then_inc(square_ready, 1)
                for u in range(2):
                    act.wait_ge(var_ready, done + c0 + u + 1)
                    act.activation(logvar[:, u, :], banks[2 + u][:, :], ACT.Ln,
                                   bias=core.eps_col(eps)).then_inc(log_ready, 1)
                for u in range(2):
                    act.wait_ge(log_ready, done + c0 + u + 1)
                    act.activation(rstd[:, u, :], logvar[:, u, :], ACT.Exp, scale=-0.5).then_inc(rstd_ready, 1)


def load_residual(core):
    nc = core.nc
    loaded = core.sem("residual_loaded")
    eps_set = core.sem("eps_set")
    with nc.Block() as block:
        @block.sync
        def _(sp):
            sp.dma_start(core.ident[:, :], core.d["ident"]).then_inc(loaded, 16)
            sp.dma_start(core.mean_mat[:, :], core.d["mean_mat"]).then_inc(loaded, 16)
            sp.dma_start(core.vecs[:, :], core.d["vecs"]).then_inc(loaded, 16)
            sp.dma_start(core.xT[:, :], core.d["xT"]).then_inc(loaded, 16)
            sp.wait_ge(loaded, 64)

        @block.vector
        def _(dve):
            dve.memset(core.eps5[:, :], 1e-5)
            dve.memset(core.eps6[:, :], 1e-6).then_inc(eps_set, 1)


def store_residual(core):
    nc = core.nc
    stored = core.sem("residual_stored")
    with nc.Block() as block:
        @block.sync
        def _(sp):
            sp.dma_start(core.d["out"], core.xT[:, :]).then_inc(stored, 16)
            sp.wait_ge(stored, 16)


def cross_attention(core):
    nc, sem, banks, xT, ident = core.nc, core.sem, core.banks, core.xT, core.ident
    scale = float(D) ** -0.5
    CALL = XH * S

    with ExitStack() as ctx:
        def sb(name, shape):
            return ctx.enter_context(nc.sbuf_tensor(f"x_{name}_sb", shape, F32))

        latT = sb("latT", [P, TOK])
        qk_w = sb("qk_w", [P, XH, D])
        vo_w = sb("vo_w", [P, XH, D])
        qk_b = sb("qk_b", [P, XH])
        vo_b = sb("vo_b", [P, 1])

        layer_norm(core, "x_ln0", xT, latT, 1e-5)
        layer_norm(core, "x_ln1", latT, latT, 1e-5, core.vec("g_lat"), core.vec("b_lat"))

        w_loaded = sem("x_w_loaded")
        w_prod = sem("x_w_prod")
        w_done = sem("x_w_done")
        with ExitStack() as wctx:
            wq = wctx.enter_context(nc.sbuf_tensor("x_wq_sb", [P, XH, D], F32))
            wk = wctx.enter_context(nc.sbuf_tensor("x_wk_sb", [P, XH, D], F32))
            wv = wctx.enter_context(nc.sbuf_tensor("x_wv_sb", [P, XH, D], F32))
            wo = wctx.enter_context(nc.sbuf_tensor("x_wo_sb", [P, XH, D], F32))
            block = wctx.enter_context(nc.Block())

            @block.sync
            def _(sp):
                for t, n in ((wq, "x_wqT"), (wk, "x_wkT"), (wv, "x_wvT"), (wo, "x_wo")):
                    sp.dma_start(t[:, :, :], core.d[n]).then_inc(w_loaded, 16)

            @block.tensor
            def _(pe):
                pe.wait_ge(w_loaded, 64)
                for h in range(XH):
                    pe.matmul(banks[h // 4][:, (h % 4) * D:(h % 4 + 1) * D], wq[:, h, :], wk[:, h, :],
                              start=True, stop=True)
                    pe.matmul(banks[2 + h // 4][:, (h % 4) * D:(h % 4 + 1) * D], wv[:, h, :], wo[:, h, :],
                              start=True, stop=True)
                    pe.matmul(banks[4][:, h:h + 1], wk[:, h, :], core.vec(f"bq{h}"), start=True, stop=True)
                for h in range(XH):
                    last = pe.matmul(banks[5][:, 0:1], wo[:, h, :], core.vec(f"bv{h}"),
                                     start=(h == 0), stop=(h == XH - 1))
                last.then_inc(w_prod, 1)

            @block.vector
            def _(dve):
                dve.wait_ge(w_prod, 1)
                for g in range(2):
                    dve.tensor_scalar(qk_w[:, 4 * g:4 * g + 4, :],
                                      banks[g][:, :].rearrange("p (h d) -> p h d", h=4), scale, None, ALU.mult)
                    dve.tensor_copy(vo_w[:, 4 * g:4 * g + 4, :],
                                    banks[2 + g][:, :].rearrange("p (h d) -> p h d", h=4))
                dve.tensor_scalar(qk_b[:, :], banks[4][:, 0:XH], scale, None, ALU.mult)
                dve.tensor_tensor(vo_b[:, :], banks[5][:, 0:1], core.vec("x_bo"), ALU.add).then_inc(w_done, 1)

        G = sb("G", [P, B, XH, S])
        g_ready = sem("x_g_ready")
        g_kept = sem("x_g_kept")
        with nc.Block() as block:
            @block.tensor
            def _(pe):
                with pe.Fori(0, NCH) as c:
                    pe.wait_ge(g_kept, c * XH)
                    for h in range(XH):
                        pe.matmul(banks[h][:, :], qk_w[:, h, :], latT[:, bass.ds(c * CH, CH)],
                                  start=True, stop=True).then_inc(g_ready, 1)

            @block.scalar
            def _(act):
                with act.Fori(0, NCH) as c:
                    for h in range(XH):
                        act.wait_ge(g_ready, c * XH + h + 1)
                        act.activation(G[:, bass.ds(c * BPC, BPC), h, :],
                                       banks[h][:, :].rearrange("p (b i) -> p b i", i=S),
                                       ACT.Identity, bias=qk_b[:, h:h + 1]).then_inc(g_kept, 1)

        with ExitStack() as bctx:
            cross_attention_batches(core, bctx, latT, G, CALL)

        y_ready = sem("x_y_ready")
        y_added = sem("x_y_added")
        with nc.Block() as block:
            @block.tensor
            def _(pe):
                with pe.Fori(0, NCH - 1, 2) as c0:
                    for u in range(2):
                        pe.wait_ge(y_added, c0)
                        for h in range(XH):
                            last = pe.matmul(banks[u][:, :], vo_w[:, h, :], G[:, bass.ds((c0 + u) * BPC, BPC), h, :],
                                             start=(h == 0), stop=(h == XH - 1))
                        last.then_inc(y_ready, 1)

            @block.vector
            def _(dve):
                with dve.Fori(0, NCH - 1, 2) as c0:
                    for u in range(2):
                        dve.wait_ge(y_ready, c0 + u + 1)
                        x = xT[:, bass.ds((c0 + u) * CH, CH)]
                        dve.scalar_tensor_tensor(x, banks[u][:, :], vo_b[:, 0:1], x, ALU.add,
                                                 ALU.add).then_inc(y_added, 1)


def cross_attention_batches(core, ctx, latT, G, CALL):
    nc, sem, banks, ident = core.nc, core.sem, core.banks, core.ident
    U = 4

    def sb(name, shape):
        return ctx.enter_context(nc.sbuf_tensor(f"x_{name}_sb", shape, F32))

    raw = [sb(f"raw{k}", [XROWS, 3, D]) for k in range(U)]
    xhat = sb("xhat", [XROWS, 3, D])
    scaled = sb("scaled", [XROWS, 3, D])
    keys = [sb(f"keys{k}", [XROWS, 3, D]) for k in range(U)]
    keysT = [sb(f"keysT{k}", [P, XKEYS]) for k in range(2)]
    lat = [sb(f"lat{k}", [P, S]) for k in range(2)]
    query = [sb(f"query{k}", [P, CALL]) for k in range(U)]
    probs = [sb(f"probs{k}", [P, 2, XKEYS]) for k in range(2)]
    probsT = sb("probsT", [P, 3, CALL])
    stats = sb("stats", [XROWS, 3, 6])
    meanvar = [sb(f"meanvar{k}", [XROWS, 3, 2]) for k in range(2)]
    vareps = sb("vareps", [XROWS, 3])
    rstd = [sb(f"rstd{k}", [XROWS, 3]) for k in range(2)]
    minus_half = sb("minus_half", [XROWS, 3])
    eps = sb("eps", [XROWS, 3])
    negmax = [sb(f"negmax{k}", [P, 2]) for k in range(2)]
    total = [sb(f"total{k}", [P, 2]) for k in range(2)]
    rtotal = [sb(f"rtotal{k}", [P, 2]) for k in range(2)]
    g_row = sb("g_row", [XROWS, D])
    b_row = sb("b_row", [XROWS, D])

    cleared = sem("x_cleared")
    rows_loaded = sem("x_rows_loaded")
    raw_loaded = [sem(f"x_raw_loaded{k}") for k in range(U)]
    query_loaded = [sem(f"x_query_loaded{k}") for k in range(U)]
    stats_ready = sem("x_stats_ready")
    meanvar_ready = sem("x_meanvar_ready")
    vareps_ready = sem("x_vareps_ready")
    rstd_ready = sem("x_rstd_ready")
    xhat_ready = sem("x_xhat_ready")
    scaled_ready = sem("x_scaled_ready")
    media_ready = sem("x_media_ready")
    lat_ready = sem("x_lat_ready")
    lat_turned = sem("x_lat_turned")
    keys_ready = sem("x_keys_ready")
    keys_turned = sem("x_keys_turned")
    keysT_ready = sem("x_keysT_ready")
    scores_ready = sem("x_scores_ready")
    max_ready = sem("x_max_ready")
    probs_ready = sem("x_probs_ready")
    rtotal_ready = sem("x_rtotal_ready")
    normp_ready = sem("x_normp_ready")
    probs_turned = sem("x_probs_turned")
    probsT_low = sem("x_probsT_low")
    probsT_high = sem("x_probsT_high")
    mix_ready = sem("x_mix_ready")
    mix_kept = sem("x_mix_kept")

    turn_bank = [banks[0], banks[1]]
    score_bank = [banks[2], banks[3]]
    pT_low, pT_high, mix_bank = banks[4], banks[5], banks[6]

    block = ctx.enter_context(nc.Block())

    @block.sync
    def _(sp):
        sp.wait_ge(cleared, 1)
        sp.dma_start(g_row[:, :], core.d["g_media_rows"]).then_inc(rows_loaded, 16)
        sp.dma_start(b_row[:, :], core.d["b_media_rows"]).then_inc(rows_loaded, 16)

        def load(n, k):
            ctx_n = core.d["ctx"][bass.ds(n, 1), :, :]
            sp.dma_start(raw[k][:, 0:2, :],
                         ctx_n[:, 0:2 * XROWS, :].rearrange("b (t p) d -> p (b t) d", p=XROWS)).then_inc(raw_loaded[k], 16)
            sp.dma_start(raw[k][S:S + XLAT, 2, :],
                         ctx_n[:, 2 * XROWS:M, :].rearrange("b p d -> (b p) d")).then_inc(raw_loaded[k], 16)
            sp.dma_start(query[k][:, :], G[:, bass.ds(n, 1), :, :].rearrange("p b h i -> p (b h i)")).then_inc(query_loaded[k], 16)

        for k in range(U):
            load(k, k)
        with sp.Fori(0, B - 2 * U + 1, U) as base:
            for k in range(U):
                sp.wait_ge(scores_ready, 2 * (base + k) + 2)
                load(base + k + U, k)

    @block.vector
    def _(dve):
        for k in range(U):
            dve.memset(raw[k][:, 2, :], 0.0)
        dve.memset(minus_half[:, :], -0.5)
        dve.memset(eps[:, :], 1e-5).then_inc(cleared, 1)

        def moments(n, k):
            if isinstance(n, int):
                dve.wait_ge(raw_loaded[k], 32 * (n // U + 1))
            else:
                dve.wait_ge(raw_loaded[k], 32 * ((n - k) // U) + 32)
            for t in range(3):
                last = dve.bn_stats(stats[:, t, :], raw[k][:, t, :])
            last.then_inc(stats_ready, 1)

        def mean_variance(n, k):
            for t in range(3):
                last = dve.bn_aggr(meanvar[k % 2][:, t, :], stats[:, t, :])
            last.then_inc(meanvar_ready, 1)

        def normalise(n, k):
            dve.wait_ge(rstd_ready, n + 1)
            for t in range(3):
                last = dve.tensor_scalar(xhat[:, t, :], raw[k][:, t, :], meanvar[k % 2][:, t, 0:1],
                                         rstd[k % 2][:, t:t + 1], ALU.subtract, ALU.mult)
            last.then_inc(xhat_ready, 1)

        def step(n, k):
            if inside(n - 1, B):
                dve.wait_ge(probs_turned, n)
                dve.tensor_copy(probsT[0:XK[2], 2, :], pT_high[0:XK[2], 0:CALL]).then_inc(probsT_high, 1)
            if inside(n + 1, B):
                dve.wait_ge(media_ready, n + 2)
                dve.wait_ge(lat_turned, n + 2)
                dve.tensor_copy(keys[(k + 1) % U][0:S, 2, :], turn_bank[(k + 1) % 2][0:S, 0:D]).then_inc(keys_ready, 1)
            if inside(n, B):
                for f in range(2):
                    dve.wait_ge(scores_ready, 2 * n + f + 1)
                    dve.tensor_reduce(negmax[k % 2][:, f:f + 1], score_bank[f][:, 0:XKEYS], AX, ALU.max,
                                      negate=True).then_inc(max_ready, 1)
            if inside(n + 2, B):
                moments(n + 2, (k + 2) % U)
            if inside(n + 2, B):
                dve.wait_ge(stats_ready, n + 3)
            if inside(n, B):
                dve.wait_ge(probs_ready, 2 * n + 2)
                dve.reciprocal(rtotal[k % 2][:, :], total[k % 2][:, :]).then_inc(rtotal_ready, 1)
            if inside(n + 2, B):
                mean_variance(n + 2, (k + 2) % U)
            if inside(n, B):
                dve.wait_ge(rtotal_ready, n + 1)
                for f in range(2):
                    dve.tensor_scalar(probs[k % 2][:, f, :], probs[k % 2][:, f, :], rtotal[k % 2][:, f:f + 1],
                                      None, ALU.mult).then_inc(normp_ready, 1)
            if inside(n + 2, B):
                normalise(n + 2, (k + 2) % U)

        for n in (0, 1):
            moments(n, n)
            dve.wait_ge(stats_ready, n + 1)
            mean_variance(n, n)
            normalise(n, n)
        dve.wait_ge(media_ready, 1)
        dve.wait_ge(lat_turned, 1)
        dve.tensor_copy(keys[0][0:S, 2, :], turn_bank[0][0:S, 0:D]).then_inc(keys_ready, 1)
        run_steps(dve, step, B, U)
        step(B, 0)

    @block.gpsimd
    def _(pool):
        def variance(n, k):
            pool.wait_ge(meanvar_ready, n + 1)
            pool.tensor_tensor(vareps[:, :], meanvar[k % 2][:, :, 1], eps[:, :], ALU.add).then_inc(vareps_ready, 1)
            pool.wait_ge(vareps_ready, n + 1)
            pool.tensor_tensor(rstd[k % 2][:, :], vareps[:, :], minus_half[:, :], ALU.pow).then_inc(rstd_ready, 1)

        def affine(n, k):
            pool.wait_ge(xhat_ready, n + 1)
            pool.tensor_copy(lat[k % 2][:, :], latT[:, bass.ds(n * S, S)]).then_inc(lat_ready, 1)
            g = g_row[:, :].unsqueeze(1).to_broadcast([XROWS, 3, D])
            b = b_row[:, :].unsqueeze(1).to_broadcast([XROWS, 3, D])
            pool.tensor_tensor(scaled[:, :, :], xhat[:, :, :], g, ALU.mult).then_inc(scaled_ready, 1)
            pool.wait_ge(scaled_ready, n + 1)
            pool.tensor_tensor(keys[k][:, :, :], scaled[:, :, :], b, ALU.add).then_inc(media_ready, 1)

        def step(n, k):
            if inside(n + 2, B):
                variance(n + 2, (k + 2) % U)
                affine(n + 2, (k + 2) % U)

        pool.wait_ge(rows_loaded, 32)
        for n in (0, 1):
            variance(n, n)
            affine(n, n)
        run_steps(pool, step, B, U)

    @block.tensor
    def _(pe):
        def turn_latents(n, k):
            pe.wait_ge(lat_ready, n + 1)
            pe.transpose(turn_bank[k % 2][0:S, 0:D], lat[k % 2][:, :], ident[:, :]).then_inc(lat_turned, 1)

        def turn_keys(n, k):
            pe.wait_ge(keys_ready, n + 1)
            for t in range(3):
                last = pe.transpose(turn_bank[k % 2][:, D + t * XROWS:D + t * XROWS + XK[t]],
                                    keys[k][0:XK[t], t, :], ident[0:XK[t], 0:XK[t]])
            last.then_inc(keys_turned, 1)

        def scores(n, k):
            pe.wait_ge(keysT_ready, n + 1)
            if isinstance(n, int):
                pe.wait_ge(query_loaded[k], 16 * (n // U + 1))
            else:
                pe.wait_ge(query_loaded[k], 16 * ((n - k) // U) + 16)
            for f in range(2):
                pe.matmul(score_bank[f][:, 0:XKEYS], query[k][:, f * P:(f + 1) * P], keysT[k % 2][:, :],
                          start=True, stop=True).then_inc(scores_ready, 1)

        def turn_probs(n, k):
            pe.wait_ge(normp_ready, 2 * n + 2)
            for t in range(3):
                for f in range(2):
                    out = pT_low[:, t * CALL:] if t < 2 else pT_high
                    last = pe.transpose(out[0:XK[t], f * P:(f + 1) * P],
                                        probs[k % 2][:, f, t * XROWS:t * XROWS + XK[t]], ident[:, :])
            last.then_inc(probs_turned, 1)

        def mix(n, k):
            pe.wait_ge(probsT_low, n + 1)
            pe.wait_ge(probsT_high, n + 1)
            for t in range(3):
                last = pe.matmul(mix_bank[:, 0:CALL], keys[k][0:XK[t], t, :], probsT[0:XK[t], t, :],
                                 start=(t == 0), stop=(t == 2))
            last.then_inc(mix_ready, 1)

        def step(n, k):
            if inside(n - 1, B):
                turn_probs(n - 1, (k - 1) % U)
            if inside(n + 1, B):
                turn_latents(n + 1, (k + 1) % U)
            if inside(n, B):
                scores(n, k)
            if inside(n + 1, B):
                turn_keys(n + 1, (k + 1) % U)
            if inside(n - 1, B):
                mix(n - 1, (k - 1) % U)

        turn_latents(0, 0)
        turn_keys(0, 0)
        run_steps(pe, step, B, U)
        step(B, 0)

    @block.scalar
    def _(act):
        def keep_keysT(n, k):
            act.wait_ge(keys_turned, n + 1)
            act.copy(keysT[k % 2][:, :], turn_bank[k % 2][:, D:D + XKEYS]).then_inc(keysT_ready, 1)

        def step(n, k):
            if inside(n - 1, B):
                act.wait_ge(probs_turned, n)
                act.copy(probsT[0:XROWS, 0:2, :],
                         pT_low[0:XROWS, 0:2 * CALL].rearrange("p (t c) -> p t c", t=2)).then_inc(probsT_low, 1)
            if inside(n, B):
                for f in range(2):
                    act.wait_ge(max_ready, 2 * n + f + 1)
                    act.activation(probs[k % 2][:, f, :], score_bank[f][:, 0:XKEYS], ACT.Exp,
                                   bias=negmax[k % 2][:, f:f + 1],
                                   accum_out=total[k % 2][:, f:f + 1]).then_inc(probs_ready, 1)
            if inside(n + 1, B):
                keep_keysT(n + 1, (k + 1) % U)
            if inside(n - 1, B):
                act.wait_ge(mix_ready, n)
                act.copy(G[:, bass.ds(n - 1, 1), :, :].rearrange("p b h i -> p (b h i)"),
                         mix_bank[:, 0:CALL]).then_inc(mix_kept, 1)

        keep_keysT(0, 0)
        run_steps(act, step, B, U)
        step(B, 0)


def linear_attention(core):
    linear_attention_sums(core)
    core.xT_guard.__exit__(None, None, None)
    with ExitStack() as ctx:
        linear_attention_tokens(core, ctx)
    hold_residual(core, "xT_again_sb")
    reloaded = core.sem("a_x_reloaded")
    with core.nc.Block() as block:
        @block.sync
        def _(sp):
            sp.dma_start(core.xT[:, :], core.d["a_x2"]).then_inc(reloaded, 16)
            sp.wait_ge(reloaded, 16)


def linear_attention_sums(core):
    nc, sem, banks = core.nc, core.sem, core.banks
    d = core.d
    with ExitStack() as ctx:
        def sb(name, shape):
            return ctx.enter_context(nc.sbuf_tensor(f"a_{name}_sb", shape, F32))

        xn = sb("xn", [P, TOK])
        wk = sb("wk", [P, LH * LD])
        fold = sb("fold", [P, LD])
        acc = [sb(f"acc{u}", [P, CH]) for u in range(2)]
        ksum = sb("ksum", [P, NLC, LHALF])
        layer_norm(core, "a_ln", core.xT, xn, 1e-5)
        PAIRS = LH // 2

        w_loaded = sem("a_wk_loaded")
        k_ready = sem("a_k_ready")
        k_added = sem("a_k_added")
        fold_ready = sem("a_fold_ready")
        ksum_kept = sem("a_ksum_kept")
        spilled = sem("a_spilled")
        block = ctx.enter_context(nc.Block())

        @block.sync
        def _(sp):
            sp.dma_start(wk[:, :], d["a_wk"]).then_inc(w_loaded, 16)
            sp.dma_start(fold[:, :], d["a_fold"]).then_inc(w_loaded, 16)
            sp.dma_start(d["a_x"], core.xT[:, :]).then_inc(spilled, 16)
            sp.dma_start(d["a_xn"], xn[:, :]).then_inc(spilled, 16)
            sp.wait_ge(ksum_kept, NCH)
            sp.dma_start(d["a_ks"], ksum[:, :, :].rearrange("p c t -> p (c t)")).then_inc(spilled, 16)
            sp.wait_ge(spilled, 48)

        @block.tensor
        def _(pe):
            pe.wait_ge(w_loaded, 32)
            with pe.Fori(0, NCH) as c:
                pe.wait_ge(ksum_kept, c)
                for h in range(PAIRS):
                    if h >= 6:
                        pe.wait_ge(k_added, c * PAIRS + h - 5)
                    pe.matmul(banks[h % 6][:, :], wk[:, h * P:(h + 1) * P], xn[:, bass.ds(c * CH, CH)],
                              start=True, stop=True).then_inc(k_ready, 1)
                pe.wait_ge(k_added, c * PAIRS + PAIRS)
                for sub in range(CH // LT):
                    for half in range(2):
                        at = sub * LT + half * LHALF
                        for u in range(2):
                            last = pe.matmul(banks[6][half * LD:half * LD + LD, sub * LHALF:(sub + 1) * LHALF],
                                             fold[:, :], acc[u][:, at:at + LHALF], start=(u == 0), stop=(u == 1))
                last.then_inc(fold_ready, 1)

        @block.vector
        def _(dve):
            with dve.Fori(0, NCH) as c:
                dve.wait_ge(fold_ready, c)
                for h in range(PAIRS):
                    dve.wait_ge(k_ready, c * PAIRS + h + 1)
                    if h < 2:
                        dve.tensor_scalar(acc[h][:, :], banks[h][:, :], 0.0, None, ALU.max).then_inc(k_added, 1)
                    else:
                        dve.wait_ge(k_added, c * PAIRS + h - 1)
                        dve.scalar_tensor_tensor(acc[h % 2][:, :], banks[h % 6][:, :], 0.0, acc[h % 2][:, :],
                                                 ALU.max, ALU.add).then_inc(k_added, 1)
                dve.wait_ge(fold_ready, c + 1)
                dve.tensor_copy(ksum[:, bass.ds(c * (CH // LT), CH // LT), :],
                                banks[6][:, 0:LT].rearrange("p (s t) -> p s t", s=CH // LT)).then_inc(ksum_kept, 1)


def linear_attention_tokens(core, ctx):
    nc, sem, banks, d = core.nc, core.sem, core.banks, core.d

    def sb(name, shape):
        return ctx.enter_context(nc.sbuf_tensor(f"a_{name}_sb", shape, F32))

    wq = sb("wq", [P, LH * LD])
    wv = sb("wv", [P, LH * LD])
    wo = sb("wo", [P, LH, 2, D])
    q = sb("q", [P, LHALF, LH])
    v = sb("v", [P, LHALF, 2, LH + 1])
    xnc = [sb(f"xnc{k}", [P, LT]) for k in range(2)]
    xc = [sb(f"xc{k}", [P, LT]) for k in range(2)]
    ksc = [sb(f"ksc{k}", [P, LHALF]) for k in range(2)]
    norm = [sb(f"norm{k}", [P, 8]) for k in range(2)]
    rnorm = [sb(f"rnorm{k}", [P, 8]) for k in range(2)]
    out = q[:, :, :].rearrange("p (m a) j -> p m a j", a=2)

    HB = 4
    NB = LH // HB
    NG = LHALF // 8
    G = 4

    w_loaded = sem("a_w_loaded")
    chunk_loaded = [sem(f"a_chunk_loaded{k}") for k in range(2)]
    cleared = sem("a_cleared")
    ones_set = sem("a_ones_set")
    v_ready = sem("a_v_ready")
    v_low = sem("a_v_low")
    v_high = sem("a_v_high")
    q_ready = sem("a_q_ready")
    q_kept = sem("a_q_kept")
    out_ready = sem("a_out_ready")
    norm_ready = sem("a_norm_ready")
    rnorm_ready = sem("a_rnorm_ready")
    out_kept = sem("a_out_kept")
    y_ready = sem("a_y_ready")
    y_half = sem("a_y_half")
    y_added = sem("a_y_added")
    stored = [sem(f"a_stored{k}") for k in range(2)]

    pair = [(banks[0], banks[1]), (banks[2], banks[3])]
    y_bank = [banks[4], banks[5]]
    block = ctx.enter_context(nc.Block())

    def wait_slot(eng, s, c, k, per):
        if isinstance(c, int):
            eng.wait_ge(s[k], per * (c // 2 + 1))
        else:
            eng.wait_ge(s[k], per * ((c - k) // 2) + per)

    @block.sync
    def _(sp):
        sp.dma_start(wq[:, :], d["a_wq"]).then_inc(w_loaded, 16)
        sp.dma_start(wv[:, :], d["a_wv"]).then_inc(w_loaded, 16)
        sp.wait_ge(cleared, 1)
        sp.dma_start(wo[0:LD, :, 0, :], d["a_wo"]).then_inc(w_loaded, 16)
        sp.dma_start(wo[LD:P, :, 1, :], d["a_wo"]).then_inc(w_loaded, 16)

        def load(c, k):
            sp.dma_start(xnc[k][:, :], d["a_xn"][:, bass.ds(c * LT, LT)]).then_inc(chunk_loaded[k], 16)
            sp.dma_start(xc[k][:, :], d["a_x"][:, bass.ds(c * LT, LT)]).then_inc(chunk_loaded[k], 16)
            sp.dma_start(ksc[k][:, :], d["a_ks"][:, bass.ds(c * LHALF, LHALF)]).then_inc(chunk_loaded[k], 16)

        def step(c, k):
            if inside(c + 1, NLC):
                if inside(c - 1, NLC):
                    wait_slot(sp, stored, c - 1, 1 - k, 16)
                load(c + 1, 1 - k)
            sp.wait_ge(y_added, c + 1)
            sp.dma_start(d["a_x2"][:, bass.ds(c * LT, LT)], xc[k][:, :]).then_inc(stored[k], 16)

        load(0, 0)
        run_steps(sp, step, NLC, 2)
        for k in range(2):
            sp.wait_ge(stored[k], 16 * NLC // 2)

    @block.gpsimd
    def _(pool):
        pool.memset(wo[LD:P, :, 0, :], 0.0)
        pool.memset(wo[0:LD, :, 1, :], 0.0).then_inc(cleared, 1)

    @block.tensor
    def _(pe):
        pe.wait_ge(w_loaded, 64)
        pe.wait_ge(ones_set, 2)

        def step(c, k):
            wait_slot(pe, chunk_loaded, c, k, 48)
            for g in range(NB):
                bank = banks[g % 4]
                if g >= 4:
                    pe.wait_ge(v_low, c * NB + g - 3)
                    pe.wait_ge(v_high, c * NB + g - 3)
                for j in range(HB):
                    h = g * HB + j
                    for half in range(2):
                        last = pe.matmul(bank[half * LD:half * LD + LD, j * LHALF:(j + 1) * LHALF],
                                         wv[:, h * LD:(h + 1) * LD], xnc[k][:, half * LHALF:(half + 1) * LHALF],
                                         start=True, stop=True)
                last.then_inc(v_ready, 1)
            for g in range(NB):
                bank = banks[4 + g % 4]
                if g >= 4:
                    pe.wait_ge(q_kept, c * NB + g - 3)
                elif g == 0:
                    pe.wait_ge(y_added, c)
                for j in range(HB):
                    h = g * HB + j
                    for half in range(2):
                        last = pe.matmul(bank[half * LD:half * LD + LD, j * LHALF:(j + 1) * LHALF],
                                         wq[:, h * LD:(h + 1) * LD], xnc[k][:, half * LHALF:(half + 1) * LHALF],
                                         start=True, stop=True)
                last.then_inc(q_ready, 1)
            pe.wait_ge(v_low, c * NB + NB)
            pe.wait_ge(v_high, c * NB + NB)
            pe.wait_ge(q_kept, c * NB + NB)
            for g in range(NG):
                if g >= 2:
                    pe.wait_ge(out_kept, c * NG + g - 1)
                for m in range(4):
                    for par in range(2):
                        n = 8 * g + 2 * m + par
                        bank = pair[g % 2][m // 2]
                        at = (m % 2) * 2 * (LH + 1)
                        last = pe.matmul(bank[par * LH:par * LH + LH, at:at + 2 * (LH + 1)],
                                         q[:, n, :], v[:, n, :, :].rearrange("p a j -> p (a j)"), start=True, stop=True)
                last.then_inc(out_ready, 1)
            pe.wait_ge(out_kept, c * NG + NG)
            for par in range(2):
                for j in range(LH):
                    last = pe.matmul(y_bank[par][:, 0:LHALF], wo[:, j, par, :], out[:, :, :, j],
                                     start=(j == 0), stop=(j == LH - 1))
                last.then_inc(y_ready, 1)

        run_steps(pe, step, NLC, 2)

    @block.scalar
    def _(act):
        def step(c, k):
            for g in range(NB):
                act.wait_ge(v_ready, c * NB + g + 1)
                act.copy(v[0:LD, :, 0, g * HB:(g + 1) * HB].rearrange("p n j -> p j n"),
                         banks[g % 4][0:LD, :].rearrange("p (j n) -> p j n", j=HB)).then_inc(v_low, 1)

        run_steps(act, step, NLC, 2)

    @block.vector
    def _(dve):
        dve.memset(v[:, :, :, :], 0.0).then_inc(ones_set, 1)
        dve.wait_ge(ones_set, 1)
        dve.memset(v[0:LD, :, 0, LH:LH + 1], 1.0)
        dve.memset(v[LD:P, :, 1, LH:LH + 1], 1.0).then_inc(ones_set, 1)

        def step(c, k):
            for g in range(NB):
                dve.wait_ge(v_ready, c * NB + g + 1)
                dve.tensor_copy(v[LD:P, :, 1, g * HB:(g + 1) * HB].rearrange("p n j -> p j n"),
                                banks[g % 4][LD:P, :].rearrange("p (j n) -> p j n", j=HB)).then_inc(v_high, 1)
            wait_slot(dve, chunk_loaded, c, k, 48)
            for g in range(NB):
                dve.wait_ge(q_ready, c * NB + g + 1)
                dve.scalar_tensor_tensor(q[:, :, g * HB:(g + 1) * HB].rearrange("p n i -> p i n"),
                                         banks[4 + g % 4][:, :].rearrange("p (i n) -> p i n", i=HB), 0.0,
                                         ksc[k][:, :].unsqueeze(1).to_broadcast([P, HB, LHALF]),
                                         ALU.max, ALU.mult).then_inc(q_kept, 1)
            for g in range(NG):
                w = g % 2
                b0 = pair_view(w)
                dve.wait_ge(out_ready, c * NG + g + 1)
                dve.tensor_scalar(norm[w][:, :].rearrange("p (b m) -> p b m", b=2), b0[:, :, :, LH], 1e-6, None,
                                  ALU.add).then_inc(norm_ready, 1)
                dve.wait_ge(norm_ready, c * NG + g + 1)
                dve.reciprocal(rnorm[w][:, :], norm[w][:, :]).then_inc(rnorm_ready, 1)
                dve.wait_ge(rnorm_ready, c * NG + g + 1)
                dve.tensor_tensor(
                    out[:, 4 * g:4 * g + 4, :, :].rearrange("p (b m) a j -> p b (m a) j", b=2),
                    b0[:, :, :, 0:LH],
                    rnorm[w][:, :].rearrange("p (b m) -> p b m", b=2).unsqueeze(3).to_broadcast([P, 2, 4, LH]),
                    ALU.mult).then_inc(out_kept, 1)
            for par in range(2):
                dve.wait_ge(y_ready, 2 * c + par + 1)
                x = xc[k][:, :].rearrange("p (a m o) -> p m a o", a=2, o=2)[:, :, :, par]
                ins = dve.scalar_tensor_tensor(x, y_bank[par][:, 0:LHALF].rearrange("p (m a) -> p m a", a=2),
                                               core.vec("a_bo"), x, ALU.add, ALU.add)
            ins.then_inc(y_added, 1)

        def pair_view(w):
            both = core.all_banks[:, 2 * w:2 * w + 2, 0:4 * (LH + 1)]
            return both.rearrange("p b (m j) -> p b m j", j=LH + 1)

        run_steps(dve, step, NLC, 2)


def experts(core):
    nc, sem, banks, xT, ident, d = core.nc, core.sem, core.banks, core.xT, core.ident, core.d
    with ExitStack() as ctx:
        def sb(name, shape):
            return ctx.enter_context(nc.sbuf_tensor(f"e_{name}_sb", shape, F32))

        xn = sb("xn", [P, TOK])
        layer_norm(core, "e_ln", xT, xn, 1e-5)
        tile = [sb(f"tile{k}", [P, P]) for k in range(2)]
        w = sb("w", [P, E, D])
        gate = sb("gate", [P, E])
        gate_b = sb("gate_b", [P, E])
        bias = sb("bias", [E, D])
        logit = sb("logit", [P, E])
        negmax = sb("negmax", [P, 1])
        ex = sb("ex", [P, E])
        total = sb("total", [P, 1])
        rtotal = sb("rtotal", [P, 1])
        prob = sb("prob", [P, E])
        kept = sb("kept", [P, E])
        ksum = sb("ksum", [P, 1])
        guard = sb("guard", [P, 1])
        rksum = sb("rksum", [P, 1])
        weight = sb("weight", [P, E])
        weightT = sb("weightT", [E, P])
        acc = [sb(f"acc{k}", [P, D]) for k in range(2)]

        loaded = sem("e_loaded")
        tile_ready = sem("e_tile_ready")
        mm_ready = sem("e_mm_ready")
        small = sem("e_small")
        exp_ready = sem("e_exp_ready")
        weight_ready = sem("e_weight_ready")
        acc_step = sem("e_acc_step")
        wT_turned = sem("e_wT_turned")
        wT_ready = sem("e_wT_ready")
        y_ready = sem("e_y_ready")
        y_added = sem("e_y_added")
        guard_ready = sem("e_guard_ready")
        rksum_ready = sem("e_rksum_ready")
        N = TOK // P
        block = ctx.enter_context(nc.Block())

        @block.sync
        def _(sp):
            sp.dma_start(w[:, :, :], d["e_w"]).then_inc(loaded, 16)
            sp.dma_start(gate[:, :], d["e_gate"]).then_inc(loaded, 16)
            sp.dma_start(gate_b[:, :], d["e_gate_b"]).then_inc(loaded, 16)
            sp.dma_start(bias[:, :], d["e_bias"]).then_inc(loaded, 16)

        @block.scalar
        def _(act):
            def step(n, k):
                if inside(n + 1, N):
                    if inside(n - 1, N):
                        act.wait_ge(mm_ready, n)
                    act.copy(tile[1 - k][:, :], xn[:, bass.ds((n + 1) * P, P)]).then_inc(tile_ready, 1)
                act.wait_ge(small, 5 * n + 2)
                act.activation(ex[:, :], logit[:, :], ACT.Exp, bias=negmax[:, :],
                               accum_out=total[:, :]).then_inc(exp_ready, 1)
                act.wait_ge(wT_turned, n + 1)
                act.copy(weightT[:, :], banks[6][0:E, 0:P]).then_inc(wT_ready, 1)

            act.copy(tile[0][:, :], xn[:, 0:P]).then_inc(tile_ready, 1)
            run_steps(act, step, N, 2)

        @block.tensor
        def _(pe):
            pe.wait_ge(loaded, 64)

            def products(n, k):
                pe.wait_ge(tile_ready, n + 1)
                pe.matmul(banks[4 + k][:, 0:E], tile[k][:, :], gate[:, :], start=True, stop=True)
                for half in range(2):
                    last = pe.matmul(banks[2 * k + half][:, :], tile[k][:, :],
                                     w[:, 4 * half:4 * half + 4, :].rearrange("p e c -> p (e c)"), start=True, stop=True)
                last.then_inc(mm_ready, 1)

            def step(n, k):
                if inside(n + 1, N):
                    products(n + 1, 1 - k)
                pe.wait_ge(weight_ready, n + 1)
                pe.transpose(banks[6][0:E, 0:P], weight[:, :], ident[:, :]).then_inc(wT_turned, 1)
                pe.wait_ge(acc_step, (n + 1) * E)
                pe.wait_ge(wT_ready, n + 1)
                pe.matmul(banks[7][:, 0:P], acc[k][:, :], ident[:, :], start=True, stop=False)
                pe.matmul(banks[7][:, 0:P], bias[:, :], weightT[:, :], start=False, stop=True).then_inc(y_ready, 1)

            products(0, 0)
            run_steps(pe, step, N, 2)

        @block.vector
        def _(dve):
            dve.wait_ge(loaded, 64)

            def step(n, k):
                base = 5 * n
                dve.wait_ge(mm_ready, n + 1)
                dve.tensor_tensor(logit[:, :], banks[4 + k][:, 0:E], gate_b[:, :], ALU.add).then_inc(small, 1)
                dve.wait_ge(small, base + 1)
                dve.tensor_reduce(negmax[:, :], logit[:, :], AX, ALU.max, negate=True).then_inc(small, 1)
                dve.wait_ge(exp_ready, n + 1)
                dve.reciprocal(rtotal[:, :], total[:, :]).then_inc(small, 1)
                dve.wait_ge(small, base + 3)
                dve.tensor_scalar(prob[:, :], ex[:, :], rtotal[:, 0:1], None, ALU.mult).then_inc(small, 1)
                dve.wait_ge(small, base + 4)
                dve.scalar_tensor_tensor(kept[:, :], prob[:, :], 0.1, prob[:, :], ALU.is_ge, ALU.mult,
                                         accum_out=ksum[:, :]).then_inc(small, 1)
                dve.wait_ge(small, base + 5)
                dve.scalar_tensor_tensor(guard[:, :], ksum[:, :], 0.0, ksum[:, :], ALU.is_equal,
                                         ALU.add).then_inc(guard_ready, 1)
                dve.wait_ge(guard_ready, n + 1)
                dve.reciprocal(rksum[:, :], guard[:, :]).then_inc(rksum_ready, 1)
                dve.wait_ge(rksum_ready, n + 1)
                dve.tensor_scalar(weight[:, :], kept[:, :], rksum[:, 0:1], None, ALU.mult).then_inc(weight_ready, 1)
                dve.wait_ge(weight_ready, n + 1)
                for e in range(E):
                    bank = banks[2 * k + e // 4][:, (e % 4) * D:(e % 4 + 1) * D]
                    if e == 0:
                        dve.tensor_scalar(acc[k][:, :], bank, weight[:, 0:1], None, ALU.mult).then_inc(acc_step, 1)
                    else:
                        dve.wait_ge(acc_step, n * E + e)
                        dve.scalar_tensor_tensor(acc[k][:, :], bank, weight[:, e:e + 1], acc[k][:, :], ALU.mult,
                                                 ALU.add).then_inc(acc_step, 1)
                dve.wait_ge(acc_step, n * E + E)
                dve.wait_ge(y_ready, n + 1)
                x = xT[:, bass.ds(n * P, P)]
                dve.tensor_tensor(x, x, banks[7][:, 0:P], ALU.add).then_inc(y_added, 1)
                dve.wait_ge(y_added, n + 1)

            run_steps(dve, step, N, 2)


def slot_attention(core):
    nc, sem, banks, xT, d = core.nc, core.sem, core.banks, core.xT, core.d
    with ExitStack() as ctx:
        def sb(name, shape):
            return ctx.enter_context(nc.sbuf_tensor(f"s_{name}_sb", shape, F32))

        slots = sb("slots", [P, TOK])
        qk_w = sb("qk_w", [P, D])
        in_w = sb("in_w", [P, 3, D])
        hh_w = sb("hh_w", [P, 3, D])
        key_scale = sb("key_scale", [P, 1])
        half_b = sb("half_b", [P, 2])
        sum_b = sb("sum_b", [P, 2])

        layer_norm(core, "s_ln", xT, slots, 1e-5)
        w_loaded = sem("s_w_loaded")
        w_prod = sem("s_w_prod")
        sum_ready = sem("s_sum_ready")
        with ExitStack() as wctx:
            wq, wk, wv = [wctx.enter_context(nc.sbuf_tensor(f"s_w{n}_sb", [P, D], F32)) for n in "qkv"]
            ih = wctx.enter_context(nc.sbuf_tensor("s_ih_sb", [P, 3, D], F32))
            block = wctx.enter_context(nc.Block())

            @block.sync
            def _(sp):
                for t, n in ((wq, "s_wq"), (wk, "s_wk"), (wv, "s_wv")):
                    sp.dma_start(t[:, :], d[n]).then_inc(w_loaded, 16)
                sp.dma_start(ih[:, :, :], d["s_ihT"]).then_inc(w_loaded, 16)
                sp.dma_start(hh_w[:, :, :], d["s_hhT"]).then_inc(w_loaded, 16)
                sp.wait_ge(w_loaded, 80)

            @block.tensor
            def _(pe):
                pe.wait_ge(w_loaded, 80)
                pe.matmul(banks[0][:, 0:D], wq[:, :], wk[:, :], start=True, stop=True)
                pe.matmul(banks[1][:, 0:3 * D], wv[:, :], ih[:, :, :].rearrange("p g c -> p (g c)"),
                          start=True, stop=True).then_inc(w_prod, 1)

            @block.vector
            def _(dve):
                for g, n in enumerate("rz"):
                    ins = dve.tensor_tensor(sum_b[:, g:g + 1], core.vec(f"bih_{n}"), core.vec(f"bhh_{n}"), ALU.add)
                ins.then_inc(sum_ready, 1)
                dve.tensor_scalar(key_scale[:, :], core.vec("input_w"), float(D) ** -0.5, None, ALU.mult)
                dve.wait_ge(sum_ready, 1)
                dve.tensor_scalar(half_b[:, :], sum_b[:, :], 0.5, None, ALU.mult)
                dve.wait_ge(w_prod, 1)
                dve.tensor_scalar(qk_w[:, :], banks[0][:, 0:D], core.vec("slot_w"), None, ALU.mult)
                dve.tensor_scalar(in_w[:, :, :], banks[1][:, 0:3 * D].rearrange("p (g c) -> p g c", g=3),
                                  core.vec("input_w"), None, ALU.mult)

        with ExitStack() as rctx:
            slot_rounds(core, rctx, slots, qk_w, in_w, hh_w, key_scale, half_b)


def slot_rounds(core, ctx, slots, qk_w, in_w, hh_w, key_scale, half_b):
    nc, sem, banks, xT, ident, d = core.nc, core.sem, core.banks, core.xT, core.ident, core.d
    GB = BPC
    Q = GB // 4
    R = 4
    SC = 3 * ST

    def sb(name, shape):
        return ctx.enter_context(nc.sbuf_tensor(f"s_{name}_sb", shape, F32))

    raw = [sb(f"raw{k}", [ST, 3, D]) for k in range(R)]
    junk = sb("junk", [ST, 3, D])
    sumsq = [sb(f"sumsq{k}", [ST, 3]) for k in range(R)]
    shifted = sb("shifted", [ST, 3])
    krstd = [sb(f"krstd{k}", [ST, 3]) for k in range(2)]
    minus_half = sb("minus_half", [P, 4])
    eps_sum = sb("eps_sum", [ST, 3])
    keys = [sb(f"keys{p}", [ST, GB, 3, D + 1]) for p in range(2)]
    keysT = [sb(f"keysT{p}", [P, GB, SC]) for p in range(2)]
    sq = sb("sq", [P, CH])
    mean_sq = sb("mean_sq", [P, Q])
    srstd = sb("srstd", [P, Q])
    query = sb("query", [P, CH])
    score = [sb(f"score{u}", [P, SC]) for u in range(2)]
    big = [sb(f"big{u}", [ST, 12]) for u in range(2)]
    less = [sb(f"less{u}", [ST, 12, S]) for u in range(2)]
    total = [sb(f"total{u}", [ST, 12]) for u in range(2)]
    rtotal = [sb(f"rtotal{u}", [ST, 12]) for u in range(2)]
    attn = [sb(f"attn{u}", [ST, 12, S]) for u in range(2)]
    mass = [sb(f"mass{u}", [P, 1]) for u in range(2)]
    rmass = [sb(f"rmass{u}", [P, 1]) for u in range(2)]
    update = [sb(f"update{u}", [P, D]) for u in range(2)]
    updT = sb("updT", [P, CH])
    gate_r = sb("gate_r", [P, CH])
    gate_z = sb("gate_z", [P, CH])
    cand_in = sb("cand_in", [P, CH])
    cand = sb("cand", [P, CH])
    diff = sb("diff", [P, CH])

    cleared = sem("s_cleared")
    raw_loaded = [sem(f"s_raw_loaded{k}") for k in range(R)]
    sumsq_ready = sem("s_sumsq_ready")
    shifted_ready = sem("s_shifted_ready")
    krstd_ready = sem("s_krstd_ready")
    keys_ready = sem("s_keys_ready")
    keys_turned = sem("s_keys_turned")
    keysT_ready = sem("s_keysT_ready")
    sq_ready = sem("s_sq_ready")
    msq_ready = sem("s_msq_ready")
    mean_kept = sem("s_mean_kept")
    srstd_ready = sem("s_srstd_ready")
    query_ready = sem("s_query_ready")
    query_kept = sem("s_query_kept")
    score_ready = sem("s_score_ready")
    score_kept = sem("s_score_kept")
    score_turned = sem("s_score_turned")
    big_ready = sem("s_big_ready")
    less_ready = sem("s_less_ready")
    exp_ready = sem("s_exp_ready")
    total_ready = sem("s_total_ready")
    rtotal_ready = sem("s_rtotal_ready")
    attn_ready = sem("s_attn_ready")
    mix_ready = sem("s_mix_ready")
    mass_ready = sem("s_mass_ready")
    rmass_ready = sem("s_rmass_ready")
    update_ready = sem("s_update_ready")
    update_turned = sem("s_update_turned")
    updT_ready = sem("s_updT_ready")
    gates_ready = sem("s_gates_ready")
    tanh_ready = sem("s_tanh_ready")
    reset_ready = sem("s_reset_ready")
    cand_step = sem("s_cand_step")
    cand_ready = sem("s_cand_ready")
    mix_step = sem("s_mix_step")
    slots_ready = sem("s_slots_ready")
    x_added = sem("s_x_added")

    def spread(it, q):
        i = it * Q + q
        return range(i * GB // (ITERS * Q), (i + 1) * GB // (ITERS * Q))

    def landed(eng, n, k):
        if isinstance(n, int):
            eng.wait_ge(raw_loaded[k], 32 * (n // R + 1))
        else:
            eng.wait_ge(raw_loaded[k], 32 * ((n - k) // R) + 32)

    block = ctx.enter_context(nc.Block())

    @block.sync
    def _(sp):
        sp.wait_ge(cleared, 1)

        def load(n, k):
            ctx_n = d["ctx"][bass.ds(n, 1), :, :]
            sp.dma_start(raw[k][:, 0:2, :],
                         ctx_n[:, 0:2 * ST, :].rearrange("b (t p) d -> p (b t) d", p=ST)).then_inc(raw_loaded[k], 16)
            sp.dma_start(raw[k][0:SK[2], 2, :],
                         ctx_n[:, 2 * ST:M, :].rearrange("b p d -> (b p) d")).then_inc(raw_loaded[k], 16)

        for k in range(R):
            load(k, k)
        with sp.Fori(0, B - 2 * R + 1, R) as base:
            for k in range(R):
                sp.wait_ge(keys_ready, base + k + 1)
                load(base + k + R, k)

    @block.gpsimd
    def _(pool):
        def key_norm(n, k):
            pool.wait_ge(krstd_ready, n)
            pool.wait_ge(sumsq_ready, n + 1)
            pool.tensor_tensor(shifted[:, :], sumsq[k % R][:, :], eps_sum[:, :], ALU.add).then_inc(shifted_ready, 1)
            pool.wait_ge(shifted_ready, n + 1)
            pool.tensor_tensor(krstd[k % 2][:, :], shifted[:, :], minus_half[0:ST, 0:3], ALU.pow).then_inc(krstd_ready, 1)

        def step(g, p):
            for it in range(ITERS):
                pool.wait_ge(mean_kept, g * ITERS + it + 1)
                pool.tensor_tensor(srstd[:, :], mean_sq[:, :], minus_half[:, :], ALU.pow).then_inc(srstd_ready, 1)
                for q in range(Q):
                    if inside(g + 1, NCH):
                        for b in spread(it, q):
                            key_norm((g + 1) * GB + b, b)

        pool.wait_ge(cleared, 1)
        for b in range(GB):
            key_norm(b, b)
        run_steps(pool, step, NCH, 2)

    @block.tensor
    def _(pe):
        def turn_keys(n, p, b):
            pe.wait_ge(keys_ready, n + 1)
            if isinstance(n, int):
                if n > 0:
                    pe.wait_ge(keysT_ready, n)
            else:
                pe.wait_ge(keysT_ready, n)
            for t in range(3):
                last = pe.transpose(banks[3][:, t * ST:(t + 1) * ST], keys[p][:, b, t, 0:D], ident[0:ST, 0:ST])
            last.then_inc(keys_turned, 1)

        def scores(r, p, q):
            for j in range(4):
                last = pe.matmul(banks[2][j * S:(j + 1) * S, 0:SC], query[:, (4 * q + j) * S:(4 * q + j + 1) * S],
                                 keysT[p][:, 4 * q + j, :], start=True, stop=True)
            last.then_inc(score_ready, 1)

        def turn_scores(r, q):
            pe.wait_ge(score_kept, r * Q + q + 1)
            for t in range(3):
                last = pe.transpose(banks[4 + q % 2][0:ST, t * P:(t + 1) * P],
                                    score[q % 2][:, t * ST:(t + 1) * ST], ident[:, :])
            last.then_inc(score_turned, 1)

        def mix(r, p, q):
            pe.wait_ge(attn_ready, r * Q + q + 1)
            pe.wait_ge(update_ready, r * Q + q)
            for t in range(3):
                for j in range(4):
                    last = pe.matmul(banks[6][j * S:(j + 1) * S, 0:D + 1], attn[q % 2][0:SK[t], t * 4 + j, :],
                                     keys[p][0:SK[t], 4 * q + j, t, :], start=(t == 0), stop=(t == 2))
            last.then_inc(mix_ready, 1)

        def turn_update(r, q):
            pe.wait_ge(update_ready, r * Q + q + 1)
            pe.transpose(banks[7][:, q * P:(q + 1) * P], update[q % 2][:, :], ident[:, :]).then_inc(update_turned, 1)

        def step(g, p):
            sl = slots[:, bass.ds(g * CH, CH)]
            pe.wait_ge(keysT_ready, g * GB + GB)
            for it in range(ITERS):
                r = g * ITERS + it
                pe.wait_ge(slots_ready, r)
                pe.matmul(banks[1][:, :], qk_w[:, :], sl, start=True, stop=True).then_inc(query_ready, 1)
                pe.wait_ge(sq_ready, r + 1)
                for q in range(Q):
                    last = pe.matmul(banks[0][:, q:q + 1], sq[:, q * P:(q + 1) * P], core.mean_mat[:, 0:1],
                                     start=True, stop=True)
                last.then_inc(msq_ready, 1)
                pe.wait_ge(query_kept, r + 1)
                for q in range(Q + 2):
                    if q < Q:
                        scores(r, p, q)
                        turn_scores(r, q)
                    if 0 <= q - 1 < Q:
                        mix(r, p, q - 1)
                    if q < Q and inside(g + 1, NCH):
                        for b in spread(it, q):
                            turn_keys((g + 1) * GB + b, 1 - p, b)
                    if 0 <= q - 2:
                        turn_update(r, q - 2)
                pe.wait_ge(mean_kept, r + 1)
                for n, bank in ((0, 0), (1, 1)):
                    pe.matmul(banks[bank][:, :], hh_w[:, n, :], sl, start=True, stop=False)
                pe.matmul(banks[4][:, :], hh_w[:, 2, :], sl, start=True, stop=True)
                pe.wait_ge(updT_ready, r + 1)
                for n, bank in ((0, 0), (1, 1)):
                    pe.matmul(banks[bank][:, :], in_w[:, n, :], updT[:, :], start=False, stop=True)
                pe.matmul(banks[2][:, :], in_w[:, 2, :], updT[:, :], start=True, stop=True).then_inc(gates_ready, 1)

        for b in range(GB):
            turn_keys(b, 0, b)
        run_steps(pe, step, NCH, 2)

    @block.scalar
    def _(act):
        def squares(n, k):
            landed(act, n, k % R)
            for t in range(3):
                last = act.activation(junk[:, t, :], raw[k % R][:, t, :], ACT.Square,
                                      accum_out=sumsq[k % R][:, t:t + 1])
            last.then_inc(sumsq_ready, 1)
            act.wait_ge(sumsq_ready, n + 1)

        def keep_keysT(n, p, b):
            act.wait_ge(keys_turned, n + 1)
            act.copy(keysT[p][:, b, :], banks[3][:, 0:SC]).then_inc(keysT_ready, 1)

        def step(g, p):
            for it in range(ITERS):
                r = g * ITERS + it
                act.wait_ge(query_ready, r + 1)
                act.activation(query[:, :], banks[1][:, :], ACT.Copy, scale=key_scale[:, 0:1]).then_inc(query_kept, 1)
                act.wait_ge(srstd_ready, r + 1)
                for q in range(Q):
                    act.wait_ge(score_ready, r * Q + q + 1)
                    act.activation(score[q % 2][:, :], banks[2][:, 0:SC], ACT.Copy,
                                   scale=srstd[:, q:q + 1]).then_inc(score_kept, 1)
                    if inside(g + 1, NCH):
                        for b in spread(it, q):
                            squares((g + 1) * GB + b, b)
                    act.wait_ge(less_ready, r * Q + q + 1)
                    act.activation(less[q % 2][:, :, :], less[q % 2][:, :, :], ACT.Exp).then_inc(exp_ready, 1)
                    if inside(g + 1, NCH):
                        for b in spread(it, q):
                            keep_keysT((g + 1) * GB + b, 1 - p, b)
                act.wait_ge(update_turned, r * Q + Q)
                act.copy(updT[:, :], banks[7][:, :]).then_inc(updT_ready, 1)
                act.wait_ge(gates_ready, r + 1)
                act.activation(gate_r[:, :], banks[0][:, :], ACT.Tanh, scale=0.5, bias=half_b[:, 0:1]).then_inc(tanh_ready, 1)
                act.activation(gate_z[:, :], banks[1][:, :], ACT.Tanh, scale=0.5, bias=half_b[:, 1:2]).then_inc(tanh_ready, 1)
                act.wait_ge(cand_step, 2 * r + 2)
                act.activation(cand[:, :], cand_in[:, :], ACT.Tanh, bias=core.vec("bih_n")).then_inc(cand_ready, 1)

        for b in range(GB):
            squares(b, b)
            keep_keysT(b, 0, b)
        run_steps(act, step, NCH, 2)

    @block.vector
    def _(dve):
        dve.memset(minus_half[:, :], -0.5)
        dve.memset(eps_sum[:, :], 1e-6 * D)
        for p in range(2):
            dve.memset(keys[p][:, :, :, D:D + 1], 1.0)
        for k in range(R):
            ins = dve.memset(raw[k][:, 2, :], 0.0)
        ins.then_inc(cleared, 1)

        def scale_keys(n, p, b):
            dve.wait_ge(krstd_ready, n + 1)
            for t in range(3):
                last = dve.tensor_scalar(keys[p][:, b, t, 0:D], raw[b % R][:, t, :], krstd[b % 2][:, t:t + 1],
                                         float(D) ** 0.5, ALU.mult, ALU.mult)
            last.then_inc(keys_ready, 1)

        def take_update(r, q):
            u = q % 2
            dve.wait_ge(mix_ready, r * Q + q + 1)
            dve.tensor_scalar(mass[u][:, :], banks[6][:, D:D + 1], 1e-6, None, ALU.add).then_inc(mass_ready, 1)
            dve.wait_ge(mass_ready, r * Q + q + 1)
            dve.reciprocal(rmass[u][:, :], mass[u][:, :]).then_inc(rmass_ready, 1)
            dve.wait_ge(rmass_ready, r * Q + q + 1)
            dve.tensor_scalar(update[u][:, :], banks[6][:, 0:D], rmass[u][:, 0:1], None, ALU.mult).then_inc(update_ready, 1)

        def step(g, p):
            sl = slots[:, bass.ds(g * CH, CH)]
            for it in range(ITERS):
                r = g * ITERS + it
                dve.wait_ge(msq_ready, r)
                dve.tensor_tensor(sq[:, :], sl, sl, ALU.mult).then_inc(sq_ready, 1)
                dve.wait_ge(msq_ready, r + 1)
                dve.tensor_scalar(mean_sq[:, :], banks[0][:, 0:Q], 1e-6, None, ALU.add).then_inc(mean_kept, 1)
                for q in range(Q + 1):
                    if q < Q:
                        u = q % 2
                        turned = banks[4 + u][0:ST, 0:3 * P].rearrange("p (g k) -> p g k", k=S)
                        dve.wait_ge(score_turned, r * Q + q + 1)
                        dve.tensor_reduce(big[u][:, :], turned, AX, ALU.max).then_inc(big_ready, 1)
                        dve.wait_ge(big_ready, r * Q + q + 1)
                        dve.tensor_tensor(less[u][:, :, :], turned, big[u][:, :].unsqueeze(2).to_broadcast([ST, 12, S]),
                                          ALU.subtract).then_inc(less_ready, 1)
                    if q < Q and inside(g + 1, NCH):
                        for b in spread(it, q):
                            scale_keys((g + 1) * GB + b, 1 - p, b)
                    if q >= 1:
                        take_update(r, q - 1)
                    if q < Q:
                        dve.wait_ge(exp_ready, r * Q + q + 1)
                        dve.tensor_reduce(total[u][:, :], less[u][:, :, :], AX, ALU.add).then_inc(total_ready, 1)
                        dve.wait_ge(total_ready, r * Q + q + 1)
                        dve.reciprocal(rtotal[u][:, :], total[u][:, :]).then_inc(rtotal_ready, 1)
                        dve.wait_ge(rtotal_ready, r * Q + q + 1)
                        dve.tensor_tensor(attn[u][:, :, :], less[u][:, :, :],
                                          rtotal[u][:, :].unsqueeze(2).to_broadcast([ST, 12, S]),
                                          ALU.mult).then_inc(attn_ready, 1)
                dve.wait_ge(tanh_ready, 2 * r + 1)
                dve.tensor_scalar(gate_r[:, :], gate_r[:, :], 0.5, 0.5, ALU.mult, ALU.add).then_inc(reset_ready, 1)
                dve.wait_ge(reset_ready, r + 1)
                dve.scalar_tensor_tensor(cand_in[:, :], banks[4][:, :], core.vec("bhh_n"), gate_r[:, :], ALU.add,
                                         ALU.mult).then_inc(cand_step, 1)
                dve.wait_ge(cand_step, 2 * r + 1)
                dve.tensor_tensor(cand_in[:, :], cand_in[:, :], banks[2][:, :], ALU.add).then_inc(cand_step, 1)
                dve.wait_ge(tanh_ready, 2 * r + 2)
                dve.tensor_scalar(gate_z[:, :], gate_z[:, :], 0.5, 0.5, ALU.mult, ALU.add).then_inc(mix_step, 1)
                dve.wait_ge(cand_ready, r + 1)
                dve.tensor_tensor(diff[:, :], sl, cand[:, :], ALU.subtract).then_inc(mix_step, 1)
                dve.wait_ge(mix_step, 3 * r + 2)
                dve.tensor_tensor(diff[:, :], diff[:, :], gate_z[:, :], ALU.mult).then_inc(mix_step, 1)
                dve.wait_ge(mix_step, 3 * r + 3)
                dve.tensor_tensor(sl, diff[:, :], cand[:, :], ALU.add).then_inc(slots_ready, 1)
                dve.wait_ge(slots_ready, r + 1)
            x = xT[:, bass.ds(g * CH, CH)]
            dve.tensor_tensor(x, x, sl, ALU.add).then_inc(x_added, 1)

        for b in range(GB):
            scale_keys(b, 0, b)
        run_steps(dve, step, NCH, 2)


def rotary_attention(core):
    nc, sem, banks, xT, d = core.nc, core.sem, core.banks, core.xT, core.d
    with ExitStack() as ctx:
        def sb(name, shape):
            return ctx.enter_context(nc.sbuf_tensor(f"r_{name}_sb", shape, F32))

        xn = sb("xn", [P, TOK])
        layer_norm(core, "r_ln", xT, xn, 1e-5)
        w = sb("w", [P, 6, D])
        turn = sb("turn", [P, 4, S])
        own_head = sb("own_head", [P, RH])
        own_batch = sb("own_batch", [P, 4])
        own_quarter = sb("own_quarter", [P, 4])
        out_b = sb("out_b", [P, 1])
        xt = [sb(f"xt{p}", [P, CH]) for p in range(2)]
        part = [sb(f"part{u}", [P, BPC, S]) for u in range(2)]
        qT = [sb(f"qT{p}", [P, CH]) for p in range(2)]
        kT = [sb(f"kT{p}", [P, CH]) for p in range(2)]
        spread = [sb(f"spread{u}", [P, 4, RH, S]) for u in range(2)]
        big = [sb(f"big{u}", [P, RH]) for u in range(2)]
        less = [sb(f"less{u}", [P, RH, S]) for u in range(2)]
        total = [sb(f"total{u}", [P, RH]) for u in range(2)]
        rtotal = [sb(f"rtotal{u}", [P, RH]) for u in range(2)]
        attn = [sb(f"attn{u}", [P, RH * S]) for u in range(2)]
        attnT = [sb(f"attnT{u}", [P, RH * S]) for u in range(2)]
        vals = [sb(f"vals{u}", [P, 4, D]) for u in range(2)]
        own = [sb(f"own{u}", [P, 4, S, 4]) for u in range(2)]
        oT = sb("oT", [P, CH])

        loaded = sem("r_loaded")
        bias_prod = sem("r_bias_prod")
        bias_ready = sem("r_bias_ready")
        xt_ready = sem("r_xt_ready")
        proj_ready = sem("r_proj_ready")
        part_ready = sem("r_part_ready")
        turned_ready = sem("r_turned_ready")
        spread_ready = sem("r_spread_ready")
        score_ready = sem("r_score_ready")
        big_ready = sem("r_big_ready")
        less_ready = sem("r_less_ready")
        exp_ready = sem("r_exp_ready")
        total_ready = sem("r_total_ready")
        rtotal_ready = sem("r_rtotal_ready")
        attn_ready = sem("r_attn_ready")
        attnT_ready = sem("r_attnT_ready")
        v_ready = sem("r_v_ready")
        vals_ready = sem("r_vals_ready")
        mix_ready = sem("r_mix_ready")
        own_ready = sem("r_own_ready")
        o_ready = sem("r_o_ready")
        y_ready = sem("r_y_ready")
        y_added = sem("r_y_added")
        Q = 4

        def at_least(eng, s, count):
            if not isinstance(count, int) or count > 0:
                eng.wait_ge(s, count)

        block = ctx.enter_context(nc.Block())

        @block.sync
        def _(sp):
            sp.dma_start(w[:, :, :], d["r_w"]).then_inc(loaded, 16)
            sp.dma_start(turn[:, :, :], d["r_turn"]).then_inc(loaded, 16)
            sp.dma_start(own_head[:, :], d["r_own_head"]).then_inc(loaded, 16)
            sp.dma_start(own_batch[:, :], d["r_own_batch"]).then_inc(loaded, 16)
            sp.dma_start(own_quarter[:, :], d["r_own_quarter"]).then_inc(loaded, 16)

        @block.gpsimd
        def _(pool):
            pool.wait_ge(loaded, 80)

            def step(c, p):
                pool.wait_ge(turned_ready, 2 * c + 2)
                for q in range(Q):
                    at_least(pool, score_ready, c * Q + q - 1)
                    for j in range(4):
                        k = kT[p][:, (4 * q + j) * S:(4 * q + j + 1) * S].unsqueeze(1).to_broadcast([P, RH, S])
                        m = own_head[:, :].unsqueeze(2).to_broadcast([P, RH, S])
                        pool.tensor_tensor(spread[q % 2][:, j, :, :], k, m, ALU.mult).then_inc(spread_ready, 1)

            run_steps(pool, step, NCH, 2)

        @block.tensor
        def _(pe):
            pe.wait_ge(loaded, 80)
            pe.matmul(banks[7][:, 0:1], w[:, 5, :], core.vec("r_bv"), start=True, stop=True).then_inc(bias_prod, 1)

            def project(c, which):
                at_least(pe, turned_ready, 2 * c + which)
                for half in range(2):
                    last = pe.matmul(banks[5 + half][:, :], w[:, 2 * which + half, :], xn[:, bass.ds(c * CH, CH)],
                                     start=True, stop=True)
                last.then_inc(proj_ready, 1)

            def values(c, p):
                pe.wait_ge(xt_ready, c + 1)
                at_least(pe, vals_ready, c * Q)
                for q in range(Q):
                    last = pe.matmul(banks[4][:, q * P:(q + 1) * P], xt[p][:, q * P:(q + 1) * P], w[:, 4, :],
                                     start=True, stop=True)
                last.then_inc(v_ready, 1)

            def scores(c, p, q):
                n = c * Q + q
                at_least(pe, less_ready, n - 1)
                for j in range(4):
                    pe.wait_ge(spread_ready, 4 * n + j + 1)
                    last = pe.matmul(banks[q % 2][j * S:(j + 1) * S, :], qT[p][:, (4 * q + j) * S:(4 * q + j + 1) * S],
                                     spread[q % 2][:, j, :, :].rearrange("p h t -> p (h t)"), start=True, stop=True)
                last.then_inc(score_ready, 1)

            def mix(c, q):
                n = c * Q + q
                pe.wait_ge(attnT_ready, n + 1)
                pe.wait_ge(vals_ready, n + 1)
                for j in range(4):
                    for g in range(4):
                        last = pe.matmul(banks[2 + q % 2][g * S:(g + 1) * S, j * P:(j + 1) * P],
                                         vals[q % 2][:, j, g * S:(g + 1) * S], attnT[q % 2][:, g * P:(g + 1) * P],
                                         start=True, stop=True)
                last.then_inc(mix_ready, 1)

            def step(c, p):
                for q in range(Q + 1):
                    if q < Q:
                        scores(c, p, q)
                    if q >= 1:
                        mix(c, q - 1)
                    if inside(c + 1, NCH):
                        if q == 0:
                            project(c + 1, 0)
                        if q == 2:
                            project(c + 1, 1)
                        if q == 4:
                            values(c + 1, 1 - p)
                pe.wait_ge(o_ready, c * Q + Q)
                pe.wait_ge(bias_ready, 1)
                pe.matmul(banks[7][:, :], w[:, 5, :], oT[:, :], start=True, stop=True).then_inc(y_ready, 1)

            project(0, 0)
            project(0, 1)
            values(0, 0)
            run_steps(pe, step, NCH, 2)

        @block.scalar
        def _(act):
            def copy_tile(c, p):
                act.copy(xt[p][:, :], xn[:, bass.ds(c * CH, CH)]).then_inc(xt_ready, 1)

            def step(c, p):
                for q in range(Q):
                    act.wait_ge(less_ready, c * Q + q + 1)
                    act.activation(less[q % 2][:, :, :], less[q % 2][:, :, :], ACT.Exp).then_inc(exp_ready, 1)
                    if q == 0 and inside(c + 1, NCH):
                        act.wait_ge(v_ready, c + 1)
                        copy_tile(c + 1, 1 - p)

            copy_tile(0, 0)
            run_steps(act, step, NCH, 2)

        @block.vector
        def _(dve):
            dve.wait_ge(loaded, 80)
            dve.wait_ge(bias_prod, 1)
            dve.tensor_tensor(out_b[:, :], banks[7][:, 0:1], core.vec("r_bo"), ALU.add).then_inc(bias_ready, 1)

            def rotate(c, p, which):
                n = 2 * c + which
                dve.wait_ge(proj_ready, n + 1)
                at_least(dve, turned_ready, n)
                names = ("r_bqa", "r_bqb") if which == 0 else ("r_bka", "r_bkb")
                for half in range(2):
                    last = dve.scalar_tensor_tensor(
                        part[half][:, :, :], banks[5 + half][:, :].rearrange("p (b s) -> p b s", s=S),
                        core.vec(names[half]), turn[:, 2 * which + half, :].unsqueeze(1).to_broadcast([P, BPC, S]),
                        ALU.add, ALU.mult)
                last.then_inc(part_ready, 1)
                dve.wait_ge(part_ready, n + 1)
                dst = (qT, kT)[which][p]
                dve.tensor_tensor(dst[:, :].rearrange("p (b s) -> p b s", s=S), part[0][:, :, :], part[1][:, :, :],
                                  ALU.add).then_inc(turned_ready, 1)

            def take(c, q):
                n = c * Q + q
                u = q % 2
                dve.wait_ge(mix_ready, n + 1)
                dve.tensor_tensor(own[u][:, :, :, :].rearrange("p b s h -> p b h s"),
                                  banks[2 + u][:, :].rearrange("p (b h s) -> p b h s", b=4, h=4),
                                  own_quarter[:, :].unsqueeze(1).unsqueeze(3).to_broadcast([P, 4, 4, S]),
                                  ALU.mult).then_inc(own_ready, 1)
                if q == 0:
                    at_least(dve, y_ready, c)
                dve.wait_ge(own_ready, n + 1)
                dve.tensor_reduce(oT[:, q * P:(q + 1) * P].rearrange("p (b s) -> p b s", b=4), own[u][:, :, :, :], AX,
                                  ALU.add).then_inc(o_ready, 1)

            def step(c, p):
                for q in range(Q + 1):
                    n = c * Q + q
                    u = q % 2
                    if q < Q:
                        dve.wait_ge(score_ready, n + 1)
                        s = banks[u][:, :].rearrange("p (h t) -> p h t", t=S)
                        dve.tensor_reduce(big[u][:, :], s, AX, ALU.max).then_inc(big_ready, 1)
                        dve.wait_ge(big_ready, n + 1)
                        dve.tensor_tensor(less[u][:, :, :], s, big[u][:, :].unsqueeze(2).to_broadcast([P, RH, S]),
                                          ALU.subtract).then_inc(less_ready, 1)
                        dve.wait_ge(v_ready, c + 1)
                        dve.tensor_tensor(vals[u][:, :, :],
                                          banks[4][:, q * P:(q + 1) * P].unsqueeze(1).to_broadcast([P, 4, D]),
                                          own_batch[:, :].unsqueeze(2).to_broadcast([P, 4, D]),
                                          ALU.mult).then_inc(vals_ready, 1)
                    if q >= 1:
                        take(c, q - 1)
                    if q < Q:
                        dve.wait_ge(exp_ready, n + 1)
                        dve.tensor_reduce(total[u][:, :], less[u][:, :, :], AX, ALU.add).then_inc(total_ready, 1)
                        dve.wait_ge(total_ready, n + 1)
                        dve.reciprocal(rtotal[u][:, :], total[u][:, :]).then_inc(rtotal_ready, 1)
                        dve.wait_ge(rtotal_ready, n + 1)
                        dve.tensor_tensor(attn[u][:, :].rearrange("p (h t) -> p h t", t=S), less[u][:, :, :],
                                          rtotal[u][:, :].unsqueeze(2).to_broadcast([P, RH, S]),
                                          ALU.mult).then_inc(attn_ready, 1)
                        dve.wait_ge(attn_ready, n + 1)
                        dve.transpose(attnT[u][:, :], attn[u][:, :]).then_inc(attnT_ready, 1)
                    if inside(c + 1, NCH):
                        if q == 1:
                            rotate(c + 1, 1 - p, 0)
                        if q == 3:
                            rotate(c + 1, 1 - p, 1)
                dve.wait_ge(y_ready, c + 1)
                x = xT[:, bass.ds(c * CH, CH)]
                dve.scalar_tensor_tensor(x, banks[7][:, :], out_b[:, 0:1], x, ALU.add, ALU.add).then_inc(y_added, 1)
                dve.wait_ge(y_added, c + 1)

            rotate(0, 0, 0)
            rotate(0, 0, 1)
            run_steps(dve, step, NCH, 2)


def mlp(core):
    nc, sem, banks, xT, ident, d = core.nc, core.sem, core.banks, core.xT, core.ident, core.d
    T = CH // P
    FT = FF // P
    with ExitStack() as ctx:
        def sb(name, shape):
            return ctx.enter_context(nc.sbuf_tensor(f"f_{name}_sb", shape, F32))

        xn = sb("xn", [P, TOK])
        layer_norm(core, "f_ln", xT, xn, 1e-5)
        tile = sb("tile", [P, CH])
        w1 = sb("w1", [P, FF])
        w2 = sb("w2", [P, FT, D])
        router = sb("router", [P, E])
        hidden = sb("hidden", [P, FT, CH])
        shifted = sb("shifted", [P, T, E])
        top_ex = sb("top_ex", [P, T, E])
        top = sb("top", [P, T, 2])
        big = sb("big", [P, T])
        negmax = sb("negmax", [P, T])
        ex = sb("ex", [P, T, E])
        total = sb("total", [P, T])
        rtotal = sb("rtotal", [P, T])
        pair = sb("pair", [P, T])
        rpair = sb("rpair", [P, T])
        share = sb("share", [P, T, 2])
        factor = sb("factor", [P, T])
        rows = sb("rows", [P, T, P])
        ones = sb("ones", [P, P])
        factorT = sb("factorT", [P, CH])
        mixed = sb("mixed", [P, CH])

        loaded = sem("f_loaded")
        ones_set = sem("f_ones_set")
        tile_ready = sem("f_tile_ready")
        logit_ready = sem("f_logit_ready")
        small = sem("f_small")
        exp_ready = sem("f_exp_ready")
        rows_ready = sem("f_rows_ready")
        hidden_ready = sem("f_hidden_ready")
        gelu_ready = sem("f_gelu_ready")
        factor_turned = sem("f_factor_turned")
        factor_ready = sem("f_factor_ready")
        y_ready = sem("f_y_ready")
        y_scaled = sem("f_y_scaled")
        y_added = sem("f_y_added")
        factor_sum = sem("f_factor_sum")
        block = ctx.enter_context(nc.Block())

        @block.sync
        def _(sp):
            sp.dma_start(w1[:, :], d["f_w1"]).then_inc(loaded, 16)
            sp.dma_start(w2[:, :, :], d["f_w2"]).then_inc(loaded, 16)
            sp.dma_start(router[:, :], d["f_router"]).then_inc(loaded, 16)

        @block.gpsimd
        def _(pool):
            with pool.Fori(0, NCH) as c:
                pool.wait_ge(logit_ready, c)
                pool.tensor_copy(tile[:, :], xn[:, bass.ds(c * CH, CH)]).then_inc(tile_ready, 1)

        @block.tensor
        def _(pe):
            pe.wait_ge(loaded, 48)
            with pe.Fori(0, NCH) as c:
                pe.wait_ge(tile_ready, c + 1)
                for t in range(T):
                    last = pe.matmul(banks[0][:, t * E:(t + 1) * E], tile[:, t * P:(t + 1) * P], router[:, :],
                                     start=True, stop=True)
                last.then_inc(logit_ready, 1)
                for f in range(FT):
                    pe.matmul(banks[1 + f][:, :], w1[:, f * P:(f + 1) * P], xn[:, bass.ds(c * CH, CH)],
                              start=True, stop=True).then_inc(hidden_ready, 1)
                for f in range(FT):
                    pe.wait_ge(gelu_ready, c * FT + f + 1)
                    last = pe.matmul(banks[5][:, :], w2[:, f, :], hidden[:, f, :], start=(f == 0), stop=(f == FT - 1))
                last.then_inc(y_ready, 1)
                pe.wait_ge(rows_ready, c + 1)
                for t in range(T):
                    last = pe.transpose(banks[6][:, t * P:(t + 1) * P], rows[:, t, :], ident[:, :])
                last.then_inc(factor_turned, 1)
                pe.wait_ge(y_scaled, c + 1)

        @block.scalar
        def _(act):
            with act.Fori(0, NCH) as c:
                act.wait_ge(small, c * 9 + 3)
                act.activation(ex[:, :, :], shifted[:, :, :], ACT.Exp).then_inc(exp_ready, 1)
                for f in range(FT):
                    act.wait_ge(hidden_ready, c * FT + f + 1)
                    act.activation(hidden[:, f, :], banks[1 + f][:, :], ACT.Gelu_apprx_tanh,
                                   bias=core.vec(f"f_b1_{f}")).then_inc(gelu_ready, 1)
                act.wait_ge(factor_turned, c + 1)
                act.copy(factorT[:, :], banks[6][:, :]).then_inc(factor_ready, 1)

        @block.vector
        def _(dve):
            dve.memset(ones[:, :], 1.0).then_inc(ones_set, 1)
            dve.wait_ge(ones_set, 1)
            with dve.Fori(0, NCH) as c:
                count = [0]

                def after(ins):
                    count[0] += 1
                    ins.then_inc(small, 1)
                    dve.wait_ge(small, c * 9 + count[0])

                dve.wait_ge(logit_ready, c + 1)
                logits = banks[0][:, 0:T * E].rearrange("p (t e) -> p t e", t=T)
                after(dve.tensor_reduce(big[:, :], logits, AX, ALU.max))
                after(dve.tensor_scalar(negmax[:, :], big[:, :], -1.0, None, ALU.mult))
                after(dve.tensor_tensor(shifted[:, :, :], logits,
                                        negmax[:, :].unsqueeze(2).to_broadcast([P, T, E]), ALU.add))
                dve.wait_ge(exp_ready, c + 1)
                dve.tensor_reduce(total[:, :], ex[:, :, :], AX, ALU.add)
                for t in range(T):
                    last = dve.max(top_ex[:, t, :], ex[:, t, :])
                after(last)
                after(dve.reciprocal(rtotal[:, :], total[:, :]))
                after(dve.tensor_tensor(top[:, :, :], top_ex[:, :, 0:2],
                                        rtotal[:, :].unsqueeze(2).to_broadcast([P, T, 2]), ALU.mult))
                after(dve.tensor_reduce(pair[:, :], top[:, :, :], AX, ALU.add))
                after(dve.reciprocal(rpair[:, :], pair[:, :]))
                after(dve.tensor_tensor(share[:, :, :], top[:, :, :],
                                        rpair[:, :].unsqueeze(2).to_broadcast([P, T, 2]), ALU.mult))
                dve.tensor_reduce(factor[:, :], share[:, :, :], AX, ALU.add).then_inc(factor_sum, 1)
                dve.wait_ge(factor_sum, c + 1)
                for t in range(T):
                    last = dve.tensor_scalar(rows[:, t, :], ones[:, :], factor[:, t:t + 1], None, ALU.mult)
                last.then_inc(rows_ready, 1)
                dve.wait_ge(y_ready, c + 1)
                dve.wait_ge(factor_ready, c + 1)
                dve.scalar_tensor_tensor(mixed[:, :], banks[5][:, :], core.vec("f_b2"), factorT[:, :], ALU.add,
                                         ALU.mult).then_inc(y_scaled, 1)
                dve.wait_ge(y_scaled, c + 1)
                x = xT[:, bass.ds(c * CH, CH)]
                dve.tensor_tensor(x, x, mixed[:, :], ALU.add).then_inc(y_added, 1)
                dve.wait_ge(y_added, c + 1)


STAGES = [cross_attention, linear_attention, experts, slot_attention, rotary_attention, mlp]


def hold_residual(core, name):
    core.xT_guard = core.nc.sbuf_tensor(name, [P, TOK], F32)
    core.xT = core.xT_guard.__enter__()


def run_stage(core, stage):
    nc, used, outer = core.nc, [], core.sem
    with ExitStack() as ctx:
        def sem(name):
            used.append(ctx.enter_context(nc.semaphore(name)))
            return used[-1]

        core.sem = sem
        stage(core)
        core.sem = outer
        with nc.Block() as block:
            @block.sync
            def _(sp):
                for s in used:
                    sp.sem_clear(s)


def build(nc, d, stages):
    core = Core()
    core.nc, core.d = nc, d
    with ExitStack() as ctx:
        core.sem = lambda name: ctx.enter_context(nc.semaphore(name))
        core.norms = [0]
        core.norm_sems = {n: core.sem(f"ln_{n}") for n in (
            "mean_ready", "centred_ready", "square_ready", "var_ready", "log_ready", "rstd_ready", "normed")}
        core.all_banks = ctx.enter_context(nc.psum_tensor("banks", [P, 8, 512], F32))
        core.banks = [core.all_banks[:, i, :] for i in range(8)]
        core.ident = ctx.enter_context(nc.sbuf_tensor("ident_sb", [P, P], F32))
        core.mean_mat = ctx.enter_context(nc.sbuf_tensor("mean_mat_sb", [P, P], F32))
        core.vecs = ctx.enter_context(nc.sbuf_tensor("vecs_sb", [P, len(VECS)], F32))
        core.eps5 = ctx.enter_context(nc.sbuf_tensor("eps5", [P, 1], F32))
        core.eps6 = ctx.enter_context(nc.sbuf_tensor("eps6", [P, 1], F32))
        scratch = lambda name, cols: nc.dram_tensor(name, (P, cols), F32, kind="Internal").ap()
        d["a_x"], d["a_x2"], d["a_xn"] = scratch("a_x", TOK), scratch("a_x2", TOK), scratch("a_xn", TOK)
        d["a_ks"] = scratch("a_ks", TOK // 2)
        core.vec = lambda name: core.vecs[:, VCOL[name]:VCOL[name] + 1]
        core.eps_col = lambda eps: (core.eps5 if eps == 1e-5 else core.eps6)[:, 0:1]
        hold_residual(core, "xT_sb")
        load_residual(core)
        for stage in stages:
            run_stage(core, stage)
        store_residual(core)
        core.xT_guard.__exit__(None, None, None)


def lay_out(inputs):
    i = {k: np.asarray(v) for k, v in inputs.items()}
    c = np.ascontiguousarray
    wkv = i["L0_xattn_Wkv"]
    heads = lambda w: c(w.reshape(D, XH, D).transpose(2, 1, 0))
    even = np.array([RD * h + 2 * (r % (RD // 2)) for h in range(RH) for r in range(RD)])
    a = {
        "xT": c(i["x"].reshape(TOK, D).T),
        "ctx": i["ctx_1024"],
        "ident": np.eye(P, dtype=np.float32),
        "mean_mat": np.full((P, P), 1.0 / D, np.float32),
        "g_media_rows": c(np.broadcast_to(i["L0_xattn_gamma_media"], (XROWS, D))),
        "b_media_rows": c(np.broadcast_to(i["L0_xattn_beta_media"], (XROWS, D))),
        "x_wqT": heads(i["L0_xattn_Wq"]),
        "x_wkT": heads(wkv[:, :XH * D]),
        "x_wvT": heads(wkv[:, XH * D:]),
        "x_wo": c(i["L0_xattn_Wo"].reshape(XH, D, D).transpose(1, 0, 2)),
    }
    bih, bhh = i["L1_xattn_gru_bih"].reshape(3, D), i["L1_xattn_gru_bhh"].reshape(3, D)
    cols = [i["L0_xattn_gamma_media"], i["L0_xattn_beta_media"], i["L0_xattn_gamma_lat"], i["L0_xattn_beta_lat"]]
    cols += list(i["L0_xattn_bq"].reshape(XH, D)) + list(i["L0_xattn_bkv"][XH * D:].reshape(XH, D))
    cols += [i["L0_xattn_bo"], i["L0_attn_bo"], i["L1_xattn_slot_norm_w"], i["L1_xattn_input_norm_w"], *bih, *bhh]
    cols += [i["L1_attn_bq"][even], i["L1_attn_bq"][even + 1], i["L1_attn_bk"][even], i["L1_attn_bk"][even + 1]]
    cols += [i["L1_attn_bv"], i["L1_attn_bo"], *i["L1_ffn_b1"].reshape(4, D), i["L1_ffn_b2"]]
    a["vecs"] = c(np.stack(cols, axis=1))
    more_arrays(i, a, c, even)
    return a


def more_arrays(i, a, c, even):
    a["a_wq"], a["a_wk"], a["a_wv"] = i["L0_attn_Wq"], i["L0_attn_Wk"], i["L0_attn_Wv"]
    a["a_wo"] = c(i["L0_attn_Wo"].reshape(LH, LH, D))
    a["a_fold"] = c(np.tile(np.eye(LD, dtype=np.float32), (2, 1))) * np.float32(LD ** -0.5)
    a["e_w"] = c(i["L0_ffn_expert_w"].transpose(1, 0, 2))
    a["e_gate"] = i["L0_ffn_gate_w"]
    a["e_gate_b"] = c(np.broadcast_to(i["L0_ffn_gate_b"], (P, E)))
    a["e_bias"] = i["L0_ffn_expert_b"]
    a["f_w1"] = i["L1_ffn_w1"]
    a["f_w2"] = c(i["L1_ffn_w2"].reshape(FF // P, P, D).transpose(1, 0, 2))
    a["f_router"] = i["L1_ffn_router_w"]
    a["s_wq"], a["s_wk"], a["s_wv"] = i["L1_xattn_Wq"], i["L1_xattn_Wk"], i["L1_xattn_Wv"]
    a["s_ihT"] = c(i["L1_xattn_gru_wih"].reshape(3, D, D).transpose(2, 0, 1))
    a["s_hhT"] = c(i["L1_xattn_gru_whh"].reshape(3, D, D).transpose(2, 0, 1))
    w = [i["L1_attn_Wq"][even], i["L1_attn_Wq"][even + 1], i["L1_attn_Wk"][even], i["L1_attn_Wk"][even + 1]]
    a["r_w"] = c(np.stack([m.T for m in w + [i["L1_attn_Wv"], i["L1_attn_Wo"]]], axis=1))
    freq = (1.0 / 10000.0 ** (np.arange(0, RD, 2) / RD)).astype(np.float32)
    angle = np.outer(freq, np.arange(S, dtype=np.float32)).astype(np.float32)
    cos, sin = np.cos(angle), np.sin(angle)
    first, second = np.concatenate([cos, sin]), np.concatenate([-sin, cos])
    turn = np.stack([first * RD ** -0.5, second * RD ** -0.5, first, second], axis=1)
    a["r_turn"] = np.tile(turn, (RH, 1, 1)).astype(np.float32)
    rows = np.arange(P)
    a["r_own_head"] = (rows[:, None] // RD == np.arange(RH)).astype(np.float32)
    a["r_own_batch"] = (rows[:, None] // S == np.arange(4)).astype(np.float32)
    a["r_own_quarter"] = (rows[:, None] // RD % 4 == np.arange(4)).astype(np.float32)


def kernel(**inputs):
    import concourse.bacc as bacc
    from concourse.bass_utils import run_bass_kernel_spmd

    nc = bacc.Bacc("TRN2", target_bir_lowering=False, num_devices=1)
    arrays = lay_out(inputs)
    d = {n: nc.dram_tensor(n, a.shape, mybir.dt.from_np(a.dtype), kind="ExternalInput").ap() for n, a in arrays.items()}
    d["out"] = nc.dram_tensor("out", (D, TOK), F32, kind="ExternalOutput").ap()
    build(nc, d, STAGES)
    got = run_bass_kernel_spmd(nc, [arrays], core_ids=[0]).results[0]["out"]
    return np.ascontiguousarray(np.asarray(got).T).reshape(B, S, D)
```

```python
from contextlib import ExitStack

import numpy as np

import concourse.bass as bass
from concourse import mybir

F32 = mybir.dt.float32
ALU = mybir.AluOpType
ACT = mybir.ActivationFunctionType
AX = mybir.AxisListType.X

P = 128
D = 128
B = 128
S = 32
M = 257
TOK = B * S
CH = 512
NCH = TOK // CH
BPC = CH // S

XH = 8
XROWS = 97
XLAT = M - 2 * XROWS
XKEYS = M + S
XK = [XROWS, XROWS, S + XLAT]
LH = 64
LD = 64
LT = 256
LHALF = LT // 2
NLC = TOK // LT
E = 8
ITERS = 3
ST = 86
SK = [86, 86, 85]
RH = 16
RD = 8
FF = 512

VECS = ["g_media", "b_media", "g_lat", "b_lat"] + [f"bq{h}" for h in range(8)] + [f"bv{h}" for h in range(8)] + [
    "x_bo", "a_bo", "slot_w", "input_w", "bih_r", "bih_z", "bih_n", "bhh_r", "bhh_z", "bhh_n",
    "r_bqa", "r_bqb", "r_bka", "r_bkb", "r_bv", "r_bo", "f_b1_0", "f_b1_1", "f_b1_2", "f_b1_3", "f_b2",
]
VCOL = {n: i for i, n in enumerate(VECS)}


def run_steps(eng, step, total, unroll):
    for n in range(unroll):
        step(n, n % unroll)
    with eng.Fori(unroll, total - 2 * unroll + 1, unroll) as base:
        for k in range(unroll):
            step(base + k, k)
    for n in range(total - unroll, total):
        step(n, n % unroll)


def inside(n, total):
    return not isinstance(n, int) or 0 <= n < total


LN_EXP_SET = "natural_log_exp_and_others"


class Core:
    pass


def layer_norm(core, tag, src, dst, eps, gamma=None, beta=None, beside=None):
    nc = core.nc
    s = core.norm_sems
    mean_ready, centred_ready, square_ready = s["mean_ready"], s["centred_ready"], s["square_ready"]
    var_ready, log_ready, rstd_ready, normed = s["var_ready"], s["log_ready"], s["rstd_ready"], s["normed"]
    done = core.norms[0] * NCH
    core.norms[0] += 1
    banks = core.banks
    with ExitStack() as ctx:
        def sb(name, shape):
            return ctx.enter_context(nc.sbuf_tensor(f"{tag}_{name}", shape, F32))

        centred = sb("centred", [P, 2, CH])
        square = sb("square", [P, 2, CH])
        logvar = sb("logvar", [P, 2, CH])
        rstd = sb("rstd", [P, 2, CH])
        block = ctx.enter_context(nc.Block())

        if beside is not None:
            @block.sync
            def _(sp):
                beside(sp)

        @block.tensor
        def _(pe):
            def mean(c, u):
                if inside(c - 2, NCH):
                    pe.wait_ge(centred_ready, done + c - 1)
                pe.matmul(banks[u][:, :], core.mean_mat[:, :], src[:, bass.ds(c * CH, CH)],
                          start=True, stop=True).then_inc(mean_ready, 1)

            def step(c, u):
                if inside(c + 1, NCH):
                    mean(c + 1, 1 - u)
                pe.wait_ge(square_ready, done + c + 1)
                if inside(c - 2, NCH):
                    pe.wait_ge(log_ready, done + c - 1)
                pe.matmul(banks[2 + u][:, :], core.mean_mat[:, :], square[:, u, :],
                          start=True, stop=True).then_inc(var_ready, 1)

            mean(0, 0)
            run_steps(pe, step, NCH, 2)

        @block.vector
        def _(dve):
            def centre(c, u):
                dve.wait_ge(mean_ready, done + c + 1)
                if inside(c - 2, NCH):
                    dve.wait_ge(normed, done + c - 1)
                dve.tensor_tensor(centred[:, u, :], src[:, bass.ds(c * CH, CH)], banks[u][:, :],
                                  ALU.subtract).then_inc(centred_ready, 1)

            def step(c, u):
                if inside(c + 1, NCH):
                    centre(c + 1, 1 - u)
                out = dst[:, bass.ds(c * CH, CH)]
                dve.wait_ge(rstd_ready, done + c + 1)
                dve.tensor_tensor(out, centred[:, u, :], rstd[:, u, :], ALU.mult).then_inc(normed, 1)
                if gamma is not None:
                    dve.wait_ge(normed, done + c + 1)
                    dve.tensor_scalar(out, out, gamma, beta, ALU.mult, ALU.add)

            centre(0, 0)
            run_steps(dve, step, NCH, 2)

        @block.scalar
        def _(act):
            def squares(c, u):
                act.wait_ge(centred_ready, done + c + 1)
                if inside(c - 2, NCH):
                    act.wait_ge(var_ready, done + c - 1)
                act.activation(square[:, u, :], centred[:, u, :], ACT.Square).then_inc(square_ready, 1)

            def step(c, u):
                if inside(c + 1, NCH):
                    squares(c + 1, 1 - u)
                act.wait_ge(var_ready, done + c + 1)
                act.activation(logvar[:, u, :], banks[2 + u][:, :], ACT.Ln, bias=core.eps_col(eps)).then_inc(log_ready, 1)
                act.wait_ge(log_ready, done + c + 1)
                if inside(c - 2, NCH):
                    act.wait_ge(normed, done + c - 1)
                act.activation(rstd[:, u, :], logvar[:, u, :], ACT.Exp, scale=-0.5).then_inc(rstd_ready, 1)

            act.preload_act_table_set(LN_EXP_SET)
            squares(0, 0)
            run_steps(act, step, NCH, 2)


def load_residual(core):
    nc = core.nc
    loaded = core.sem("residual_loaded")
    eps_set = core.sem("eps_set")
    with nc.Block() as block:
        @block.sync
        def _(sp):
            sp.dma_start(core.ident[:, :], core.d["ident"]).then_inc(loaded, 16)
            sp.dma_start(core.mean_mat[:, :], core.d["mean_mat"]).then_inc(loaded, 16)
            sp.dma_start(core.vecs[:, :], core.d["vecs"]).then_inc(loaded, 16)
            sp.dma_start(core.xT[:, :], core.d["xT"]).then_inc(loaded, 16)
            sp.wait_ge(loaded, 64)

        @block.vector
        def _(dve):
            dve.memset(core.eps5[:, :], 1e-5)
            dve.memset(core.eps6[:, :], 1e-6).then_inc(eps_set, 1)


def store_residual(core):
    nc = core.nc
    stored = core.sem("residual_stored")
    with nc.Block() as block:
        @block.sync
        def _(sp):
            sp.dma_start(core.d["out"], core.xT[:, :]).then_inc(stored, 16)
            sp.wait_ge(stored, 16)


def cross_attention(core):
    nc, sem, banks, xT, ident = core.nc, core.sem, core.banks, core.xT, core.ident
    scale = float(D) ** -0.5
    CALL = XH * S

    with ExitStack() as ctx:
        def sb(name, shape):
            return ctx.enter_context(nc.sbuf_tensor(f"x_{name}_sb", shape, F32))

        latT = sb("latT", [P, TOK])
        qk_w = sb("qk_w", [P, XH, D])
        vo_w = sb("vo_w", [P, XH, D])
        qk_b = sb("qk_b", [P, XH])
        vo_b = sb("vo_b", [P, 1])

        w_loaded = sem("x_w_loaded")
        w_prod = sem("x_w_prod")
        w_done = sem("x_w_done")
        with ExitStack() as wctx:
            wq = wctx.enter_context(nc.sbuf_tensor("x_wq_sb", [P, XH, D], F32))
            wk = wctx.enter_context(nc.sbuf_tensor("x_wk_sb", [P, XH, D], F32))
            wv = wctx.enter_context(nc.sbuf_tensor("x_wv_sb", [P, XH, D], F32))
            wo = wctx.enter_context(nc.sbuf_tensor("x_wo_sb", [P, XH, D], F32))

            def load_weights(sp):
                for t, n in ((wq, "x_wqT"), (wk, "x_wkT"), (wv, "x_wvT"), (wo, "x_wo")):
                    sp.dma_start(t[:, :, :], core.d[n]).then_inc(w_loaded, 16)

            layer_norm(core, "x_ln0", xT, latT, 1e-5, beside=load_weights)
            layer_norm(core, "x_ln1", latT, latT, 1e-5, core.vec("g_lat"), core.vec("b_lat"))
            block = wctx.enter_context(nc.Block())

            @block.tensor
            def _(pe):
                pe.wait_ge(w_loaded, 64)
                for h in range(XH):
                    pe.matmul(banks[h // 4][:, (h % 4) * D:(h % 4 + 1) * D], wq[:, h, :], wk[:, h, :],
                              start=True, stop=True)
                    pe.matmul(banks[2 + h // 4][:, (h % 4) * D:(h % 4 + 1) * D], wv[:, h, :], wo[:, h, :],
                              start=True, stop=True)
                    pe.matmul(banks[4][:, h:h + 1], wk[:, h, :], core.vec(f"bq{h}"), start=True, stop=True)
                for h in range(XH):
                    last = pe.matmul(banks[5][:, 0:1], wo[:, h, :], core.vec(f"bv{h}"),
                                     start=(h == 0), stop=(h == XH - 1))
                last.then_inc(w_prod, 1)

            @block.vector
            def _(dve):
                dve.wait_ge(w_prod, 1)
                for g in range(2):
                    dve.tensor_scalar(qk_w[:, 4 * g:4 * g + 4, :],
                                      banks[g][:, :].rearrange("p (h d) -> p h d", h=4), scale, None, ALU.mult)
                    dve.tensor_copy(vo_w[:, 4 * g:4 * g + 4, :],
                                    banks[2 + g][:, :].rearrange("p (h d) -> p h d", h=4))
                dve.tensor_scalar(qk_b[:, :], banks[4][:, 0:XH], scale, None, ALU.mult)
                dve.tensor_tensor(vo_b[:, :], banks[5][:, 0:1], core.vec("x_bo"), ALU.add).then_inc(w_done, 1)

        G = sb("G", [P, B, XH, S])
        with ExitStack() as bctx:
            cross_attention_batches(core, bctx, latT, G, qk_w, qk_b, CALL)

        y_ready = sem("x_y_ready")
        y_added = sem("x_y_added")
        with nc.Block() as block:
            @block.tensor
            def _(pe):
                with pe.Fori(0, NCH - 1, 2) as c0:
                    for u in range(2):
                        pe.wait_ge(y_added, c0)
                        for h in range(XH):
                            last = pe.matmul(banks[u][:, :], vo_w[:, h, :], G[:, bass.ds((c0 + u) * BPC, BPC), h, :],
                                             start=(h == 0), stop=(h == XH - 1))
                        last.then_inc(y_ready, 1)

            @block.vector
            def _(dve):
                with dve.Fori(0, NCH - 1, 2) as c0:
                    for u in range(2):
                        dve.wait_ge(y_ready, c0 + u + 1)
                        x = xT[:, bass.ds((c0 + u) * CH, CH)]
                        dve.scalar_tensor_tensor(x, banks[u][:, :], vo_b[:, 0:1], x, ALU.add,
                                                 ALU.add).then_inc(y_added, 1)


def cross_attention_batches(core, ctx, latT, G, qk_w, qk_b, CALL):
    nc, sem, banks, ident = core.nc, core.sem, core.banks, core.ident
    U = 4

    def sb(name, shape):
        return ctx.enter_context(nc.sbuf_tensor(f"x_{name}_sb", shape, F32))

    raw = [sb(f"raw{k}", [XROWS, 3, D]) for k in range(U)]
    xhat = sb("xhat", [XROWS, 3, D])
    scaled = sb("scaled", [XROWS, 3, D])
    keys = [sb(f"keys{k}", [XROWS, 3, D]) for k in range(U)]
    keysT = [sb(f"keysT{k}", [P, XKEYS]) for k in range(2)]
    lat = [sb(f"lat{k}", [P, S]) for k in range(2)]
    query = [sb(f"query{k}", [P, CALL]) for k in range(U)]
    probs = [sb(f"probs{k}", [P, 2, XKEYS]) for k in range(2)]
    probsT = sb("probsT", [P, 3, CALL])
    stats = sb("stats", [XROWS, 3, 6])
    meanvar = [sb(f"meanvar{k}", [XROWS, 3, 2]) for k in range(2)]
    vareps = sb("vareps", [XROWS, 3])
    rstd = [sb(f"rstd{k}", [XROWS, 3]) for k in range(2)]
    minus_half = sb("minus_half", [XROWS, 3])
    eps = sb("eps", [XROWS, 3])
    negmax = [sb(f"negmax{k}", [P, 2]) for k in range(2)]
    total = [sb(f"total{k}", [P, 2]) for k in range(2)]
    rtotal = [sb(f"rtotal{k}", [P, 2]) for k in range(2)]
    g_row = sb("g_row", [XROWS, D])
    b_row = sb("b_row", [XROWS, D])

    cleared = sem("x_cleared")
    rows_loaded = sem("x_rows_loaded")
    raw_loaded = [sem(f"x_raw_loaded{k}") for k in range(U)]
    query_loaded = [sem(f"x_query_loaded{k}") for k in range(U)]
    stats_ready = sem("x_stats_ready")
    meanvar_ready = sem("x_meanvar_ready")
    vareps_ready = sem("x_vareps_ready")
    rstd_ready = sem("x_rstd_ready")
    xhat_ready = sem("x_xhat_ready")
    scaled_ready = sem("x_scaled_ready")
    media_ready = sem("x_media_ready")
    lat_ready = sem("x_lat_ready")
    lat_turned = sem("x_lat_turned")
    keys_ready = sem("x_keys_ready")
    keys_turned = sem("x_keys_turned")
    keysT_ready = sem("x_keysT_ready")
    scores_ready = sem("x_scores_ready")
    max_ready = sem("x_max_ready")
    probs_ready = sem("x_probs_ready")
    rtotal_ready = sem("x_rtotal_ready")
    normp_ready = sem("x_normp_ready")
    probs_turned = sem("x_probs_turned")
    probsT_low = sem("x_probsT_low")
    probsT_high = sem("x_probsT_high")
    mix_ready = sem("x_mix_ready")
    mix_kept = sem("x_mix_kept")

    turn_bank = [banks[0], banks[1]]
    score_bank = [banks[2], banks[3]]
    pT_low, pT_high, mix_bank = banks[4], banks[5][:, 0:CALL], banks[6][:, 0:CALL]

    g_ready = sem("x_g_ready")
    g_kept = sem("x_g_kept")


    def load_media(sp, n, k):
        ctx_n = core.d["ctx"][bass.ds(n, 1), :, :]
        sp.dma_start(raw[k][:, 0:2, :],
                     ctx_n[:, 0:2 * XROWS, :].rearrange("b (t p) d -> p (b t) d", p=XROWS)).then_inc(raw_loaded[k], 16)
        sp.dma_start(raw[k][S:S + XLAT, 2, :],
                     ctx_n[:, 2 * XROWS:M, :].rearrange("b p d -> (b p) d")).then_inc(raw_loaded[k], 16)

    with nc.Block() as block:
        @block.vector
        def _(dve):
            for k in range(U):
                dve.memset(raw[k][:, 2, :], 0.0)
            dve.memset(minus_half[:, :], -0.5)
            dve.memset(eps[:, :], 1e-5).then_inc(cleared, 1)

        @block.sync
        def _(sp):
            sp.wait_ge(cleared, 1)
            for k in range(U):
                load_media(sp, k, k)
            sp.dma_start(g_row[:, :], core.d["g_media_rows"]).then_inc(rows_loaded, 16)
            sp.dma_start(b_row[:, :], core.d["b_media_rows"]).then_inc(rows_loaded, 16)

        @block.tensor
        def _(pe):
            with pe.Fori(0, NCH) as c:
                pe.wait_ge(g_kept, c * XH)
                for h in range(XH):
                    pe.matmul(banks[h][:, :], qk_w[:, h, :], latT[:, bass.ds(c * CH, CH)],
                              start=True, stop=True).then_inc(g_ready, 1)

        @block.scalar
        def _(act):
            with act.Fori(0, NCH) as c:
                for h in range(XH):
                    act.wait_ge(g_ready, c * XH + h + 1)
                    act.activation(G[:, bass.ds(c * BPC, BPC), h, :],
                                   banks[h][:, :].rearrange("p (b i) -> p b i", i=S),
                                   ACT.Identity, bias=qk_b[:, h:h + 1]).then_inc(g_kept, 1)

    block = ctx.enter_context(nc.Block())

    @block.sync
    def _(sp):
        def load_query(n, k):
            sp.dma_start(query[k][:, :],
                         G[:, bass.ds(n, 1), :, :].rearrange("p b h i -> p (b h i)")).then_inc(query_loaded[k], 16)

        def step(n, k):
            if inside(n + U, B):
                sp.wait_ge(xhat_ready, n + 1)
                load_media(sp, n + U, k)
            if inside(n + U - 2, B):
                if inside(n - 2, B):
                    sp.wait_ge(scores_ready, 2 * (n - 2) + 2)
                load_query(n + U - 2, (k - 2) % U)

        for k in range(U - 2):
            load_query(k, k)
        run_steps(sp, step, B, U)

    @block.vector
    def _(dve):
        def moments(n, k):
            if isinstance(n, int):
                dve.wait_ge(raw_loaded[k], 32 * (n // U + 1))
            else:
                dve.wait_ge(raw_loaded[k], 32 * ((n - k) // U) + 32)
            if inside(n - 1, B):
                dve.wait_ge(meanvar_ready, n)
            for t in range(3):
                last = dve.bn_stats(stats[:, t, :], raw[k][:, t, :])
            last.then_inc(stats_ready, 1)

        def mean_variance(n, k):
            for t in range(3):
                last = dve.bn_aggr(meanvar[k % 2][:, t, :], stats[:, t, :])
            last.then_inc(meanvar_ready, 1)

        def normalise(n, k):
            dve.wait_ge(rstd_ready, n + 1)
            if inside(n - 1, B):
                dve.wait_ge(scaled_ready, n)
            for t in range(3):
                last = dve.tensor_scalar(xhat[:, t, :], raw[k][:, t, :], meanvar[k % 2][:, t, 0:1],
                                         rstd[k % 2][:, t:t + 1], ALU.subtract, ALU.mult)
            last.then_inc(xhat_ready, 1)

        def add_latents(n, k):
            dve.wait_ge(media_ready, n + 1)
            dve.wait_ge(lat_turned, n + 1)
            dve.tensor_copy(keys[k][0:S, 2, :], turn_bank[k % 2][0:S, 0:D]).then_inc(keys_ready, 1)

        def step(n, k):
            if inside(n + 2, B):
                normalise(n + 2, (k + 2) % U)
            if inside(n + 1, B):
                add_latents(n + 1, (k + 1) % U)
            if inside(n + 3, B):
                moments(n + 3, (k + 3) % U)
                dve.wait_ge(stats_ready, n + 4)
            if inside(n - 1, B):
                dve.wait_ge(probs_ready, 2 * n)
                dve.reciprocal(rtotal[(k - 1) % 2][:, :], total[(k - 1) % 2][:, :]).then_inc(rtotal_ready, 1)
            if inside(n + 3, B):
                mean_variance(n + 3, (k + 3) % U)
            if inside(n - 1, B):
                dve.wait_ge(rtotal_ready, n)
                for f in range(2):
                    dve.tensor_scalar(probs[(k - 1) % 2][:, f, :], probs[(k - 1) % 2][:, f, :],
                                      rtotal[(k - 1) % 2][:, f:f + 1], None, ALU.mult).then_inc(normp_ready, 1)
            if inside(n, B):
                for f in range(2):
                    dve.wait_ge(scores_ready, 2 * n + f + 1)
                    dve.tensor_reduce(negmax[k % 2][:, f:f + 1], score_bank[f][:, 0:XKEYS], AX, ALU.max,
                                      negate=True).then_inc(max_ready, 1)

        for n in range(3):
            moments(n, n)
            dve.wait_ge(stats_ready, n + 1)
            mean_variance(n, n)
            if n < 2:
                normalise(n, n)
        add_latents(0, 0)
        run_steps(dve, step, B, U)
        step(B, 0)

    @block.gpsimd
    def _(pool):
        def variance(n, k):
            pool.wait_ge(meanvar_ready, n + 1)
            pool.tensor_tensor(vareps[:, :], meanvar[k % 2][:, :, 1], eps[:, :], ALU.add).then_inc(vareps_ready, 1)
            pool.wait_ge(vareps_ready, n + 1)
            pool.tensor_tensor(rstd[k % 2][:, :], vareps[:, :], minus_half[:, :], ALU.pow).then_inc(rstd_ready, 1)

        def take_latents(n, k):
            if inside(n - 2, B):
                pool.wait_ge(lat_turned, n - 1)
            pool.tensor_copy(lat[k % 2][:, :], latT[:, bass.ds(n * S, S)]).then_inc(lat_ready, 1)

        def scale(n, k):
            pool.wait_ge(xhat_ready, n + 1)
            g = g_row[:, :].unsqueeze(1).to_broadcast([XROWS, 3, D])
            if inside(n - 1, B):
                pool.wait_ge(media_ready, n)
            pool.tensor_tensor(scaled[:, :, :], xhat[:, :, :], g, ALU.mult).then_inc(scaled_ready, 1)

        def shift(n, k):
            b = b_row[:, :].unsqueeze(1).to_broadcast([XROWS, 3, D])
            pool.wait_ge(scaled_ready, n + 1)
            if inside(n - U, B):
                pool.wait_ge(mix_ready, n - U + 1)
            pool.tensor_tensor(keys[k][:, :, :], scaled[:, :, :], b, ALU.add).then_inc(media_ready, 1)

        def step(n, k):
            if inside(n + 3, B):
                take_latents(n + 3, (k + 3) % U)
            if inside(n + 2, B):
                scale(n + 2, (k + 2) % U)
            if inside(n + 3, B):
                variance(n + 3, (k + 3) % U)
            if inside(n + 2, B):
                shift(n + 2, (k + 2) % U)

        pool.wait_ge(rows_loaded, 32)
        for n in range(3):
            take_latents(n, n)
        variance(0, 0)
        scale(0, 0)
        shift(0, 0)
        variance(1, 1)
        scale(1, 1)
        shift(1, 1)
        variance(2, 2)
        run_steps(pool, step, B, U)

    @block.tensor
    def _(pe):
        def turn_latents(n, k):
            pe.wait_ge(lat_ready, n + 1)
            pe.transpose(turn_bank[k % 2][0:S, 0:D], lat[k % 2][:, :], ident[:, :]).then_inc(lat_turned, 1)

        def turn_keys(n, k):
            pe.wait_ge(keys_ready, n + 1)
            for t in range(3):
                last = pe.transpose(turn_bank[k % 2][:, D + t * XROWS:D + t * XROWS + XK[t]],
                                    keys[k][0:XK[t], t, :], ident[0:XK[t], 0:XK[t]])
            last.then_inc(keys_turned, 1)

        def scores(n, k):
            pe.wait_ge(keysT_ready, n + 1)
            if isinstance(n, int):
                pe.wait_ge(query_loaded[k], 16 * (n // U + 1))
            else:
                pe.wait_ge(query_loaded[k], 16 * ((n - k) // U) + 16)
            if inside(n - 1, B):
                pe.wait_ge(probs_ready, 2 * n)
            for f in range(2):
                pe.matmul(score_bank[f][:, 0:XKEYS], query[k][:, f * P:(f + 1) * P], keysT[k % 2][:, :],
                          start=True, stop=True).then_inc(scores_ready, 1)

        def turn_probs(n, k):
            pe.wait_ge(normp_ready, 2 * n + 2)
            for t in range(3):
                for f in range(2):
                    out = pT_low[:, t * CALL:] if t < 2 else pT_high
                    last = pe.transpose(out[0:XK[t], f * P:(f + 1) * P],
                                        probs[k % 2][:, f, t * XROWS:t * XROWS + XK[t]], ident[:, :])
            last.then_inc(probs_turned, 1)

        def mix(n, k):
            pe.wait_ge(probsT_low, n + 1)
            pe.wait_ge(probsT_high, n + 1)
            if inside(n - 1, B):
                pe.wait_ge(mix_kept, n)
            for t in range(3):
                last = pe.matmul(mix_bank, keys[k][0:XK[t], t, :], probsT[0:XK[t], t, :],
                                 start=(t == 0), stop=(t == 2))
            last.then_inc(mix_ready, 1)

        def step(n, k):
            if inside(n, B):
                scores(n, k)
            if inside(n + 2, B):
                turn_latents(n + 2, (k + 2) % U)
            if inside(n + 1, B):
                turn_keys(n + 1, (k + 1) % U)
            if inside(n - 2, B):
                mix(n - 2, (k - 2) % U)
            if inside(n - 1, B):
                turn_probs(n - 1, (k - 1) % U)

        turn_latents(0, 0)
        turn_latents(1, 1)
        turn_keys(0, 0)
        run_steps(pe, step, B, U)
        step(B, 0)
        step(B + 1, 1)

    @block.scalar
    def _(act):
        def keep_keysT(n, k):
            act.wait_ge(keys_turned, n + 1)
            act.copy(keysT[k % 2][:, :], turn_bank[k % 2][:, D:D + XKEYS]).then_inc(keysT_ready, 1)

        def step(n, k):
            if inside(n + 1, B):
                keep_keysT(n + 1, (k + 1) % U)
            if inside(n, B):
                for f in range(2):
                    act.wait_ge(max_ready, 2 * n + f + 1)
                    act.activation(probs[k % 2][:, f, :], score_bank[f][:, 0:XKEYS], ACT.Exp,
                                   bias=negmax[k % 2][:, f:f + 1],
                                   accum_out=total[k % 2][:, f:f + 1]).then_inc(probs_ready, 1)
            if inside(n - 2, B):
                act.wait_ge(mix_ready, n - 1)
                act.copy(G[:, bass.ds(n - 2, 1), :, :].rearrange("p b h i -> p (b h i)"), mix_bank).then_inc(mix_kept, 1)
            if inside(n - 1, B):
                act.wait_ge(probs_turned, n)
                act.copy(probsT[0:XROWS, 0:2, :],
                         pT_low[0:XROWS, 0:2 * CALL].rearrange("p (t c) -> p t c", t=2)).then_inc(probsT_low, 1)
                act.copy(probsT[0:XK[2], 2, :], pT_high[0:XK[2], :]).then_inc(probsT_high, 1)

        keep_keysT(0, 0)
        run_steps(act, step, B, U)
        step(B, 0)
        step(B + 1, 1)


def linear_attention(core):
    linear_attention_sums(core)
    core.xT_guard.__exit__(None, None, None)
    with ExitStack() as ctx:
        linear_attention_tokens(core, ctx)
    hold_residual(core, "xT_again_sb")
    reloaded = core.sem("a_x_reloaded")
    with core.nc.Block() as block:
        @block.sync
        def _(sp):
            sp.dma_start(core.xT[:, :], core.d["a_x2"]).then_inc(reloaded, 16)
            sp.wait_ge(reloaded, 16)


def linear_attention_sums(core):
    nc, sem, banks = core.nc, core.sem, core.banks
    d = core.d
    with ExitStack() as ctx:
        def sb(name, shape):
            return ctx.enter_context(nc.sbuf_tensor(f"a_{name}_sb", shape, F32))

        xn = sb("xn", [P, TOK])
        wk = sb("wk", [P, LH * LD])
        fold = sb("fold", [P, LD])
        acc = [sb(f"acc{u}", [P, CH]) for u in range(2)]
        ksum = sb("ksum", [P, NLC, LHALF])
        layer_norm(core, "a_ln", core.xT, xn, 1e-5)
        PAIRS = LH // 2

        w_loaded = sem("a_wk_loaded")
        k_ready = sem("a_k_ready")
        k_added = sem("a_k_added")
        fold_ready = sem("a_fold_ready")
        ksum_kept = sem("a_ksum_kept")
        spilled = sem("a_spilled")
        block = ctx.enter_context(nc.Block())

        @block.sync
        def _(sp):
            sp.dma_start(wk[:, :], d["a_wk"]).then_inc(w_loaded, 16)
            sp.dma_start(fold[:, :], d["a_fold"]).then_inc(w_loaded, 16)
            sp.dma_start(d["a_x"], core.xT[:, :]).then_inc(spilled, 16)
            sp.dma_start(d["a_xn"], xn[:, :]).then_inc(spilled, 16)
            sp.wait_ge(ksum_kept, NCH)
            sp.dma_start(d["a_ks"], ksum[:, :, :].rearrange("p c t -> p (c t)")).then_inc(spilled, 16)
            sp.wait_ge(spilled, 48)

        @block.tensor
        def _(pe):
            pe.wait_ge(w_loaded, 32)
            with pe.Fori(0, NCH) as c:
                pe.wait_ge(ksum_kept, c)
                for h in range(PAIRS):
                    if h >= 6:
                        pe.wait_ge(k_added, c * PAIRS + h - 5)
                    pe.matmul(banks[h % 6][:, :], wk[:, h * P:(h + 1) * P], xn[:, bass.ds(c * CH, CH)],
                              start=True, stop=True).then_inc(k_ready, 1)
                pe.wait_ge(k_added, c * PAIRS + PAIRS)
                for sub in range(CH // LT):
                    for half in range(2):
                        at = sub * LT + half * LHALF
                        for u in range(2):
                            last = pe.matmul(banks[6][half * LD:half * LD + LD, sub * LHALF:(sub + 1) * LHALF],
                                             fold[:, :], acc[u][:, at:at + LHALF], start=(u == 0), stop=(u == 1))
                last.then_inc(fold_ready, 1)

        @block.vector
        def _(dve):
            with dve.Fori(0, NCH) as c:
                dve.wait_ge(fold_ready, c)
                for h in range(PAIRS):
                    dve.wait_ge(k_ready, c * PAIRS + h + 1)
                    if h < 2:
                        dve.tensor_scalar(acc[h][:, :], banks[h][:, :], 0.0, None, ALU.max).then_inc(k_added, 1)
                    else:
                        dve.wait_ge(k_added, c * PAIRS + h - 1)
                        dve.scalar_tensor_tensor(acc[h % 2][:, :], banks[h % 6][:, :], 0.0, acc[h % 2][:, :],
                                                 ALU.max, ALU.add).then_inc(k_added, 1)
                dve.wait_ge(fold_ready, c + 1)
                dve.tensor_copy(ksum[:, bass.ds(c * (CH // LT), CH // LT), :],
                                banks[6][:, 0:LT].rearrange("p (s t) -> p s t", s=CH // LT)).then_inc(ksum_kept, 1)


def linear_attention_tokens(core, ctx):
    nc, sem, banks, d = core.nc, core.sem, core.banks, core.d

    def sb(name, shape):
        return ctx.enter_context(nc.sbuf_tensor(f"a_{name}_sb", shape, F32))

    wq = sb("wq", [P, LH * LD])
    wv = sb("wv", [P, LH * LD])
    wo = sb("wo", [P, LH, 2, D])
    q = sb("q", [P, LHALF, LH])
    v = sb("v", [P, LHALF, 2, LH + 1])
    xnc = [sb(f"xnc{k}", [P, LT]) for k in range(2)]
    xc = [sb(f"xc{k}", [P, LT]) for k in range(2)]
    ksc = [sb(f"ksc{k}", [P, LHALF]) for k in range(2)]
    norm = [sb(f"norm{k}", [P, 8]) for k in range(2)]
    rnorm = [sb(f"rnorm{k}", [P, 8]) for k in range(2)]
    out = q[:, :, :].rearrange("p (m a) j -> p m a j", a=2)

    HB = 4
    NB = LH // HB
    NG = LHALF // 8
    G = 4

    w_loaded = sem("a_w_loaded")
    chunk_loaded = [sem(f"a_chunk_loaded{k}") for k in range(2)]
    cleared = sem("a_cleared")
    ones_set = sem("a_ones_set")
    v_ready = sem("a_v_ready")
    v_low = sem("a_v_low")
    v_high = sem("a_v_high")
    q_ready = sem("a_q_ready")
    q_kept = sem("a_q_kept")
    out_ready = sem("a_out_ready")
    norm_ready = sem("a_norm_ready")
    rnorm_ready = sem("a_rnorm_ready")
    out_kept = sem("a_out_kept")
    y_ready = sem("a_y_ready")
    y_half = sem("a_y_half")
    y_added = sem("a_y_added")
    stored = [sem(f"a_stored{k}") for k in range(2)]

    pair = [(banks[0], banks[1]), (banks[2], banks[3])]
    y_bank = [banks[4], banks[5]]
    block = ctx.enter_context(nc.Block())

    def wait_slot(eng, s, c, k, per):
        if isinstance(c, int):
            eng.wait_ge(s[k], per * (c // 2 + 1))
        else:
            eng.wait_ge(s[k], per * ((c - k) // 2) + per)

    @block.sync
    def _(sp):
        sp.dma_start(wq[:, :], d["a_wq"]).then_inc(w_loaded, 16)
        sp.dma_start(wv[:, :], d["a_wv"]).then_inc(w_loaded, 16)
        sp.wait_ge(cleared, 1)
        sp.dma_start(wo[0:LD, :, 0, :], d["a_wo"]).then_inc(w_loaded, 16)
        sp.dma_start(wo[LD:P, :, 1, :], d["a_wo"]).then_inc(w_loaded, 16)

        def load(c, k):
            sp.dma_start(xnc[k][:, :], d["a_xn"][:, bass.ds(c * LT, LT)]).then_inc(chunk_loaded[k], 16)
            sp.dma_start(xc[k][:, :], d["a_x"][:, bass.ds(c * LT, LT)]).then_inc(chunk_loaded[k], 16)
            sp.dma_start(ksc[k][:, :], d["a_ks"][:, bass.ds(c * LHALF, LHALF)]).then_inc(chunk_loaded[k], 16)

        def step(c, k):
            if inside(c + 1, NLC):
                if inside(c - 1, NLC):
                    wait_slot(sp, stored, c - 1, 1 - k, 16)
                load(c + 1, 1 - k)
            sp.wait_ge(y_added, c + 1)
            sp.dma_start(d["a_x2"][:, bass.ds(c * LT, LT)], xc[k][:, :]).then_inc(stored[k], 16)

        load(0, 0)
        run_steps(sp, step, NLC, 2)
        for k in range(2):
            sp.wait_ge(stored[k], 16 * NLC // 2)

    @block.gpsimd
    def _(pool):
        pool.memset(wo[LD:P, :, 0, :], 0.0)
        pool.memset(wo[0:LD, :, 1, :], 0.0).then_inc(cleared, 1)

    @block.tensor
    def _(pe):
        pe.wait_ge(w_loaded, 64)
        pe.wait_ge(ones_set, 2)

        def step(c, k):
            wait_slot(pe, chunk_loaded, c, k, 48)
            for g in range(NB):
                bank = banks[g % 4]
                if g >= 4:
                    pe.wait_ge(v_low, c * NB + g - 3)
                    pe.wait_ge(v_high, c * NB + g - 3)
                for j in range(HB):
                    h = g * HB + j
                    for half in range(2):
                        last = pe.matmul(bank[half * LD:half * LD + LD, j * LHALF:(j + 1) * LHALF],
                                         wv[:, h * LD:(h + 1) * LD], xnc[k][:, half * LHALF:(half + 1) * LHALF],
                                         start=True, stop=True)
                last.then_inc(v_ready, 1)
            for g in range(NB):
                bank = banks[4 + g % 4]
                if g >= 4:
                    pe.wait_ge(q_kept, c * NB + g - 3)
                elif g == 0:
                    pe.wait_ge(y_added, c)
                for j in range(HB):
                    h = g * HB + j
                    for half in range(2):
                        last = pe.matmul(bank[half * LD:half * LD + LD, j * LHALF:(j + 1) * LHALF],
                                         wq[:, h * LD:(h + 1) * LD], xnc[k][:, half * LHALF:(half + 1) * LHALF],
                                         start=True, stop=True)
                last.then_inc(q_ready, 1)
            pe.wait_ge(v_low, c * NB + NB)
            pe.wait_ge(v_high, c * NB + NB)
            pe.wait_ge(q_kept, c * NB + NB)
            for g in range(NG):
                if g >= 2:
                    pe.wait_ge(out_kept, c * NG + g - 1)
                for m in range(4):
                    for par in range(2):
                        n = 8 * g + 2 * m + par
                        bank = pair[g % 2][m // 2]
                        at = (m % 2) * 2 * (LH + 1)
                        last = pe.matmul(bank[par * LH:par * LH + LH, at:at + 2 * (LH + 1)],
                                         q[:, n, :], v[:, n, :, :].rearrange("p a j -> p (a j)"), start=True, stop=True)
                last.then_inc(out_ready, 1)
            pe.wait_ge(out_kept, c * NG + NG)
            for par in range(2):
                for j in range(LH):
                    last = pe.matmul(y_bank[par][:, 0:LHALF], wo[:, j, par, :], out[:, :, :, j],
                                     start=(j == 0), stop=(j == LH - 1))
                last.then_inc(y_ready, 1)

        run_steps(pe, step, NLC, 2)

    @block.scalar
    def _(act):
        def step(c, k):
            for g in range(NB):
                act.wait_ge(v_ready, c * NB + g + 1)
                act.copy(v[0:LD, :, 0, g * HB:(g + 1) * HB].rearrange("p n j -> p j n"),
                         banks[g % 4][0:LD, :].rearrange("p (j n) -> p j n", j=HB)).then_inc(v_low, 1)

        run_steps(act, step, NLC, 2)

    @block.vector
    def _(dve):
        dve.memset(v[:, :, :, :], 0.0).then_inc(ones_set, 1)
        dve.wait_ge(ones_set, 1)
        dve.memset(v[0:LD, :, 0, LH:LH + 1], 1.0)
        dve.memset(v[LD:P, :, 1, LH:LH + 1], 1.0).then_inc(ones_set, 1)

        def step(c, k):
            for g in range(NB):
                dve.wait_ge(v_ready, c * NB + g + 1)
                dve.tensor_copy(v[LD:P, :, 1, g * HB:(g + 1) * HB].rearrange("p n j -> p j n"),
                                banks[g % 4][LD:P, :].rearrange("p (j n) -> p j n", j=HB)).then_inc(v_high, 1)
            wait_slot(dve, chunk_loaded, c, k, 48)
            for g in range(NB):
                dve.wait_ge(q_ready, c * NB + g + 1)
                dve.scalar_tensor_tensor(q[:, :, g * HB:(g + 1) * HB].rearrange("p n i -> p i n"),
                                         banks[4 + g % 4][:, :].rearrange("p (i n) -> p i n", i=HB), 0.0,
                                         ksc[k][:, :].unsqueeze(1).to_broadcast([P, HB, LHALF]),
                                         ALU.max, ALU.mult).then_inc(q_kept, 1)
            for g in range(NG):
                w = g % 2
                b0 = pair_view(w)
                dve.wait_ge(out_ready, c * NG + g + 1)
                dve.tensor_scalar(norm[w][:, :].rearrange("p (b m) -> p b m", b=2), b0[:, :, :, LH], 1e-6, None,
                                  ALU.add).then_inc(norm_ready, 1)
                dve.wait_ge(norm_ready, c * NG + g + 1)
                dve.reciprocal(rnorm[w][:, :], norm[w][:, :]).then_inc(rnorm_ready, 1)
                dve.wait_ge(rnorm_ready, c * NG + g + 1)
                dve.tensor_tensor(
                    out[:, 4 * g:4 * g + 4, :, :].rearrange("p (b m) a j -> p b (m a) j", b=2),
                    b0[:, :, :, 0:LH],
                    rnorm[w][:, :].rearrange("p (b m) -> p b m", b=2).unsqueeze(3).to_broadcast([P, 2, 4, LH]),
                    ALU.mult).then_inc(out_kept, 1)
            for par in range(2):
                dve.wait_ge(y_ready, 2 * c + par + 1)
                x = xc[k][:, :].rearrange("p (a m o) -> p m a o", a=2, o=2)[:, :, :, par]
                ins = dve.scalar_tensor_tensor(x, y_bank[par][:, 0:LHALF].rearrange("p (m a) -> p m a", a=2),
                                               core.vec("a_bo"), x, ALU.add, ALU.add)
            ins.then_inc(y_added, 1)

        def pair_view(w):
            both = core.all_banks[:, 2 * w:2 * w + 2, 0:4 * (LH + 1)]
            return both.rearrange("p b (m j) -> p b m j", j=LH + 1)

        run_steps(dve, step, NLC, 2)


def experts(core):
    nc, sem, banks, xT, ident, d = core.nc, core.sem, core.banks, core.xT, core.ident, core.d
    with ExitStack() as ctx:
        def sb(name, shape):
            return ctx.enter_context(nc.sbuf_tensor(f"e_{name}_sb", shape, F32))

        xn = sb("xn", [P, TOK])
        layer_norm(core, "e_ln", xT, xn, 1e-5)
        tile = [sb(f"tile{k}", [P, P]) for k in range(2)]
        w = sb("w", [P, E, D])
        gate = sb("gate", [P, E])
        gate_b = sb("gate_b", [P, E])
        bias = sb("bias", [E, D])
        logit = sb("logit", [P, E])
        negmax = sb("negmax", [P, 1])
        ex = sb("ex", [P, E])
        total = sb("total", [P, 1])
        rtotal = sb("rtotal", [P, 1])
        prob = sb("prob", [P, E])
        kept = sb("kept", [P, E])
        ksum = sb("ksum", [P, 1])
        guard = sb("guard", [P, 1])
        rksum = sb("rksum", [P, 1])
        weight = sb("weight", [P, E])
        weightT = sb("weightT", [E, P])
        acc = [sb(f"acc{k}", [P, D]) for k in range(2)]

        loaded = sem("e_loaded")
        tile_ready = sem("e_tile_ready")
        mm_ready = sem("e_mm_ready")
        small = sem("e_small")
        exp_ready = sem("e_exp_ready")
        weight_ready = sem("e_weight_ready")
        acc_step = sem("e_acc_step")
        wT_turned = sem("e_wT_turned")
        wT_ready = sem("e_wT_ready")
        y_ready = sem("e_y_ready")
        y_added = sem("e_y_added")
        guard_ready = sem("e_guard_ready")
        rksum_ready = sem("e_rksum_ready")
        N = TOK // P
        block = ctx.enter_context(nc.Block())

        @block.sync
        def _(sp):
            sp.dma_start(w[:, :, :], d["e_w"]).then_inc(loaded, 16)
            sp.dma_start(gate[:, :], d["e_gate"]).then_inc(loaded, 16)
            sp.dma_start(gate_b[:, :], d["e_gate_b"]).then_inc(loaded, 16)
            sp.dma_start(bias[:, :], d["e_bias"]).then_inc(loaded, 16)

        @block.scalar
        def _(act):
            def step(n, k):
                if inside(n + 1, N):
                    if inside(n - 1, N):
                        act.wait_ge(mm_ready, n)
                    act.copy(tile[1 - k][:, :], xn[:, bass.ds((n + 1) * P, P)]).then_inc(tile_ready, 1)
                act.wait_ge(small, 5 * n + 2)
                act.activation(ex[:, :], logit[:, :], ACT.Exp, bias=negmax[:, :],
                               accum_out=total[:, :]).then_inc(exp_ready, 1)
                act.wait_ge(wT_turned, n + 1)
                act.copy(weightT[:, :], banks[6][0:E, 0:P]).then_inc(wT_ready, 1)

            act.copy(tile[0][:, :], xn[:, 0:P]).then_inc(tile_ready, 1)
            run_steps(act, step, N, 2)

        @block.tensor
        def _(pe):
            pe.wait_ge(loaded, 64)

            def products(n, k):
                pe.wait_ge(tile_ready, n + 1)
                pe.matmul(banks[4 + k][:, 0:E], tile[k][:, :], gate[:, :], start=True, stop=True)
                for half in range(2):
                    last = pe.matmul(banks[2 * k + half][:, :], tile[k][:, :],
                                     w[:, 4 * half:4 * half + 4, :].rearrange("p e c -> p (e c)"), start=True, stop=True)
                last.then_inc(mm_ready, 1)

            def step(n, k):
                if inside(n + 1, N):
                    products(n + 1, 1 - k)
                pe.wait_ge(weight_ready, n + 1)
                pe.transpose(banks[6][0:E, 0:P], weight[:, :], ident[:, :]).then_inc(wT_turned, 1)
                pe.wait_ge(acc_step, (n + 1) * E)
                pe.wait_ge(wT_ready, n + 1)
                pe.matmul(banks[7][:, 0:P], acc[k][:, :], ident[:, :], start=True, stop=False)
                pe.matmul(banks[7][:, 0:P], bias[:, :], weightT[:, :], start=False, stop=True).then_inc(y_ready, 1)

            products(0, 0)
            run_steps(pe, step, N, 2)

        @block.vector
        def _(dve):
            dve.wait_ge(loaded, 64)

            def step(n, k):
                base = 5 * n
                dve.wait_ge(mm_ready, n + 1)
                dve.tensor_tensor(logit[:, :], banks[4 + k][:, 0:E], gate_b[:, :], ALU.add).then_inc(small, 1)
                dve.wait_ge(small, base + 1)
                dve.tensor_reduce(negmax[:, :], logit[:, :], AX, ALU.max, negate=True).then_inc(small, 1)
                dve.wait_ge(exp_ready, n + 1)
                dve.reciprocal(rtotal[:, :], total[:, :]).then_inc(small, 1)
                dve.wait_ge(small, base + 3)
                dve.tensor_scalar(prob[:, :], ex[:, :], rtotal[:, 0:1], None, ALU.mult).then_inc(small, 1)
                dve.wait_ge(small, base + 4)
                dve.scalar_tensor_tensor(kept[:, :], prob[:, :], 0.1, prob[:, :], ALU.is_ge, ALU.mult,
                                         accum_out=ksum[:, :]).then_inc(small, 1)
                dve.wait_ge(small, base + 5)
                dve.scalar_tensor_tensor(guard[:, :], ksum[:, :], 0.0, ksum[:, :], ALU.is_equal,
                                         ALU.add).then_inc(guard_ready, 1)
                dve.wait_ge(guard_ready, n + 1)
                dve.reciprocal(rksum[:, :], guard[:, :]).then_inc(rksum_ready, 1)
                dve.wait_ge(rksum_ready, n + 1)
                dve.tensor_scalar(weight[:, :], kept[:, :], rksum[:, 0:1], None, ALU.mult).then_inc(weight_ready, 1)
                dve.wait_ge(weight_ready, n + 1)
                for e in range(E):
                    bank = banks[2 * k + e // 4][:, (e % 4) * D:(e % 4 + 1) * D]
                    if e == 0:
                        dve.tensor_scalar(acc[k][:, :], bank, weight[:, 0:1], None, ALU.mult).then_inc(acc_step, 1)
                    else:
                        dve.wait_ge(acc_step, n * E + e)
                        dve.scalar_tensor_tensor(acc[k][:, :], bank, weight[:, e:e + 1], acc[k][:, :], ALU.mult,
                                                 ALU.add).then_inc(acc_step, 1)
                dve.wait_ge(acc_step, n * E + E)
                dve.wait_ge(y_ready, n + 1)
                x = xT[:, bass.ds(n * P, P)]
                dve.tensor_tensor(x, x, banks[7][:, 0:P], ALU.add).then_inc(y_added, 1)
                dve.wait_ge(y_added, n + 1)

            run_steps(dve, step, N, 2)


def slot_attention(core):
    nc, sem, banks, xT, d = core.nc, core.sem, core.banks, core.xT, core.d
    with ExitStack() as ctx:
        def sb(name, shape):
            return ctx.enter_context(nc.sbuf_tensor(f"s_{name}_sb", shape, F32))

        slots = sb("slots", [P, TOK])
        qk_w = sb("qk_w", [P, D])
        in_w = sb("in_w", [P, 3, D])
        hh_w = sb("hh_w", [P, 3, D])
        key_scale = sb("key_scale", [P, 1])
        half_b = sb("half_b", [P, 3])
        sum_b = sb("sum_b", [P, 2])

        w_loaded = sem("s_w_loaded")
        w_prod = sem("s_w_prod")
        sum_ready = sem("s_sum_ready")
        with ExitStack() as wctx:
            wq, wk, wv = [wctx.enter_context(nc.sbuf_tensor(f"s_w{n}_sb", [P, D], F32)) for n in "qkv"]
            ih = wctx.enter_context(nc.sbuf_tensor("s_ih_sb", [P, 3, D], F32))

            def load_weights(sp):
                for t, n in ((wq, "s_wq"), (wk, "s_wk"), (wv, "s_wv")):
                    sp.dma_start(t[:, :], d[n]).then_inc(w_loaded, 16)
                sp.dma_start(ih[:, :, :], d["s_ihT"]).then_inc(w_loaded, 16)
                sp.dma_start(hh_w[:, :, :], d["s_hhT"]).then_inc(w_loaded, 16)
                sp.wait_ge(w_loaded, 80)

            layer_norm(core, "s_ln", xT, slots, 1e-5, beside=load_weights)
            block = wctx.enter_context(nc.Block())

            @block.tensor
            def _(pe):
                pe.wait_ge(w_loaded, 80)
                pe.matmul(banks[0][:, 0:D], wq[:, :], wk[:, :], start=True, stop=True)
                pe.matmul(banks[1][:, 0:3 * D], wv[:, :], ih[:, :, :].rearrange("p g c -> p (g c)"),
                          start=True, stop=True).then_inc(w_prod, 1)

            @block.vector
            def _(dve):
                for g, n in enumerate("rz"):
                    ins = dve.tensor_tensor(sum_b[:, g:g + 1], core.vec(f"bih_{n}"), core.vec(f"bhh_{n}"), ALU.add)
                ins.then_inc(sum_ready, 1)
                dve.tensor_scalar(key_scale[:, :], core.vec("input_w"), float(D) ** -0.5, None, ALU.mult)
                dve.wait_ge(sum_ready, 1)
                dve.tensor_scalar(half_b[:, 0:2], sum_b[:, :], 0.5, None, ALU.mult)
                dve.tensor_scalar(half_b[:, 2:3], core.vec("bhh_n"), 0.5, None, ALU.mult)
                dve.wait_ge(w_prod, 1)
                dve.tensor_scalar(qk_w[:, :], banks[0][:, 0:D], core.vec("slot_w"), None, ALU.mult)
                dve.tensor_scalar(in_w[:, :, :], banks[1][:, 0:3 * D].rearrange("p (g c) -> p g c", g=3),
                                  core.vec("input_w"), None, ALU.mult)

        with ExitStack() as rctx:
            slot_rounds(core, rctx, slots, qk_w, in_w, hh_w, key_scale, half_b)
        x_added = sem("s_x_added")
        with nc.Block() as block:
            @block.vector
            def _(dve):
                dve.tensor_tensor(xT[:, :], xT[:, :], slots[:, :], ALU.add).then_inc(x_added, 1)


def slot_rounds(core, ctx, slots, qk_w, in_w, hh_w, key_scale, half_b):
    nc, sem, banks, ident, d = core.nc, core.sem, core.banks, core.ident, core.d
    GB = BPC
    HS = CH // 2
    UG = 2 * ITERS
    UN = NCH * UG
    R = 4
    SC = 3 * ST

    def sb(name, shape):
        return ctx.enter_context(nc.sbuf_tensor(f"s_{name}_sb", shape, F32))

    raw = [sb(f"raw{k}", [ST, 3, D]) for k in range(R)]
    junk = sb("junk", [ST, 3, D])
    sumsq = [sb(f"sumsq{k}", [ST, 3]) for k in range(R)]
    shifted = sb("shifted", [ST, 3])
    krstd = [sb(f"krstd{k}", [ST, 3]) for k in range(R)]
    minus_half = sb("minus_half", [P, 4])
    eps_sum = sb("eps_sum", [ST, 3])
    keys = [sb(f"keys{p}", [ST, GB, 3, D + 1]) for p in range(2)]
    keysT = [sb(f"keysT{p}", [P, GB, SC]) for p in range(2)]
    sq = sb("sq", [P, HS])
    mean_sq = sb("mean_sq", [P, 2])
    srstd = sb("srstd", [P, 2])
    query = sb("query", [P, HS])
    score = [sb(f"score{q}", [P, SC]) for q in range(2)]
    big = [sb(f"big{q}", [ST, 12]) for q in range(2)]
    less = [sb(f"less{q}", [ST, 12, S]) for q in range(2)]
    total = [sb(f"total{q}", [ST, 12]) for q in range(2)]
    rtotal = [sb(f"rtotal{q}", [ST, 12]) for q in range(2)]
    attn = [sb(f"attn{q}", [ST, 12, S]) for q in range(2)]
    mass = [sb(f"mass{q}", [P, 1]) for q in range(2)]
    rmass = [sb(f"rmass{q}", [P, 1]) for q in range(2)]
    update = [sb(f"update{q}", [P, D]) for q in range(2)]
    updT = sb("updT", [P, HS])
    half_hn = sb("half_hn", [P, HS])
    tanh_r = sb("tanh_r", [P, HS])
    tanh_z = sb("tanh_z", [P, HS])
    cand_in = sb("cand_in", [P, HS])
    cand = sb("cand", [P, HS])
    new_share = sb("new_share", [P, HS])
    old_twice = sb("old_twice", [P, HS])

    cleared = sem("s_cleared")
    raw_loaded = [sem(f"s_raw_loaded{k}") for k in range(R)]
    sumsq_ready = sem("s_sumsq_ready")
    shifted_ready = sem("s_shifted_ready")
    krstd_ready = sem("s_krstd_ready")
    keys_ready = sem("s_keys_ready")
    keys_turned = sem("s_keys_turned")
    keysT_ready = sem("s_keysT_ready")
    sq_ready = sem("s_sq_ready")
    msq_ready = sem("s_msq_ready")
    mean_kept = sem("s_mean_kept")
    srstd_ready = sem("s_srstd_ready")
    query_ready = sem("s_query_ready")
    query_kept = sem("s_query_kept")
    score_ready = sem("s_score_ready")
    score_kept = sem("s_score_kept")
    score_turned = sem("s_score_turned")
    big_ready = sem("s_big_ready")
    less_ready = sem("s_less_ready")
    exp_ready = sem("s_exp_ready")
    total_ready = sem("s_total_ready")
    rtotal_ready = sem("s_rtotal_ready")
    attn_ready = sem("s_attn_ready")
    mix_ready = sem("s_mix_ready")
    mass_ready = sem("s_mass_ready")
    rmass_ready = sem("s_rmass_ready")
    update_ready = sem("s_update_ready")
    update_turned = sem("s_update_turned")
    updT_ready = sem("s_updT_ready")
    hh_ready = sem("s_hh_ready")
    hn_kept = sem("s_hn_kept")
    r_ready = sem("s_r_ready")
    zn_ready = sem("s_zn_ready")
    tanh_r_ready = sem("s_tanh_r_ready")
    tanh_z_ready = sem("s_tanh_z_ready")
    reset_done = sem("s_reset_done")
    cand_in_ready = sem("s_cand_in_ready")
    cand_ready = sem("s_cand_ready")
    share_ready = sem("s_share_ready")
    new_ready = sem("s_new_ready")
    slots_ready = sem("s_slots_ready")

    r_bank, z_bank = banks[0][:, 0:HS], banks[1][:, 0:HS]
    hn_bank, xn_bank = banks[0][:, HS:], banks[6][:, HS:]
    turned_bank = [banks[5], banks[2]]
    key_bank, query_bank, score_bank = banks[3], banks[1][:, HS:], banks[4]
    mix_bank = [banks[6], banks[4][:, SC:]]
    update_bank, msq_bank = banks[7][:, 0:HS], banks[7][:, HS:HS + 2]

    def at(g, i):
        return g * CH + {-1: -HS, UG: CH, UG + 1: CH + HS}.get(i, i % 2 * HS)

    def coming(g, i):
        if i == UG:
            g, i = g + 1, 0
        if not inside(g + 1, NCH):
            return []
        return [((g + 1) * GB + b, b) for b in range(i * GB // UG, (i + 1) * GB // UG)]

    def run_units(eng, unit):
        def step(g, p):
            for i in range(UG):
                unit(g * UG + i, g, i, p)

        run_steps(eng, step, NCH, 2)
        unit(UN, NCH, 0, 0)

    def landed(eng, n, k):
        if isinstance(n, int):
            eng.wait_ge(raw_loaded[k], 32 * (n // R + 1))
        else:
            eng.wait_ge(raw_loaded[k], 32 * ((n - k) // R) + 32)

    block = ctx.enter_context(nc.Block())

    @block.sync
    def _(sp):
        sp.wait_ge(cleared, 1)

        def load(n, k):
            ctx_n = d["ctx"][bass.ds(n, 1), :, :]
            sp.dma_start(raw[k][:, 0:2, :],
                         ctx_n[:, 0:2 * ST, :].rearrange("b (t p) d -> p (b t) d", p=ST)).then_inc(raw_loaded[k], 16)
            sp.dma_start(raw[k][0:SK[2], 2, :],
                         ctx_n[:, 2 * ST:M, :].rearrange("b p d -> (b p) d")).then_inc(raw_loaded[k], 16)

        for k in range(R):
            load(k, k)
        with sp.Fori(0, B - 2 * R + 1, R) as base:
            for k in range(R):
                sp.wait_ge(keys_ready, base + k + 1)
                load(base + k + R, k)

    @block.gpsimd
    def _(pool):
        def key_norm(n, k):
            pool.wait_ge(krstd_ready, n)
            pool.wait_ge(sumsq_ready, n + 1)
            pool.tensor_tensor(shifted[:, :], sumsq[k % R][:, :], eps_sum[:, :], ALU.add).then_inc(shifted_ready, 1)
            pool.wait_ge(shifted_ready, n + 1)
            if inside(n - R, B):
                pool.wait_ge(keys_ready, n - R + 1)
            pool.tensor_tensor(krstd[k % R][:, :], shifted[:, :], minus_half[0:ST, 0:3], ALU.pow).then_inc(krstd_ready, 1)

        def unit(u, g, i, p):
            if inside(u, UN):
                pool.wait_ge(mean_kept, u + 1)
                if inside(u - 1, UN):
                    pool.wait_ge(score_kept, 2 * u)
                pool.tensor_tensor(srstd[:, :], mean_sq[:, :], minus_half[:, 0:2], ALU.pow).then_inc(srstd_ready, 1)
                for n, b in coming(g, i + 1):
                    key_norm(n, b)

        pool.wait_ge(cleared, 1)
        for b in range(GB):
            key_norm(b, b)
        for n, b in coming(0, 0):
            key_norm(n, b)
        run_units(pool, unit)

    @block.tensor
    def _(pe):
        def turn_keys(n, p, b):
            pe.wait_ge(keys_ready, n + 1)
            if inside(n - 1, B):
                pe.wait_ge(keysT_ready, n)
            for t in range(3):
                last = pe.transpose(key_bank[:, t * ST:(t + 1) * ST], keys[p][:, b, t, 0:D], ident[0:ST, 0:ST])
            last.then_inc(keys_turned, 1)

        def scores(u, i, p, q):
            if q == 1:
                pe.wait_ge(score_kept, 2 * u + 1)
            for j in range(4):
                b = i % 2 * 8 + 4 * q + j
                last = pe.matmul(score_bank[j * S:(j + 1) * S, 0:SC], query[:, (4 * q + j) * S:(4 * q + j + 1) * S],
                                 keysT[p][:, b, :], start=True, stop=True)
            last.then_inc(score_ready, 1)

        def turn_scores(u, q):
            pe.wait_ge(score_kept, 2 * u + q + 1)
            for t in range(3):
                last = pe.transpose(turned_bank[q][0:ST, t * P:(t + 1) * P], score[q][:, t * ST:(t + 1) * ST],
                                    ident[:, :])
            last.then_inc(score_turned, 1)

        def mix(u, i, p, q):
            pe.wait_ge(attn_ready, 2 * u + q + 1)
            if q == 1 or inside(u - 1, UN):
                pe.wait_ge(update_ready, 2 * u + q - 1)
            for t in range(3):
                for j in range(4):
                    last = pe.matmul(mix_bank[q][j * S:(j + 1) * S, 0:D + 1], attn[q][0:SK[t], t * 4 + j, :],
                                     keys[p][0:SK[t], i % 2 * 8 + 4 * q + j, t, :], start=(t == 0), stop=(t == 2))
            last.then_inc(mix_ready, 1)

        def turn_update(u, q):
            pe.wait_ge(update_ready, 2 * u + q + 1)
            pe.transpose(update_bank[:, q * P:(q + 1) * P], update[q][:, :], ident[:, :]).then_inc(update_turned, 1)

        def transform_slots(u, g, i):
            if inside(u - 2, UN):
                pe.wait_ge(slots_ready, u - 1)
            pe.matmul(query_bank, qk_w[:, :], slots[:, bass.ds(at(g, i), HS)], start=True, stop=True).then_inc(query_ready, 1)
            pe.wait_ge(sq_ready, u + 1)
            for q in range(2):
                last = pe.matmul(msq_bank[:, q:q + 1], sq[:, q * P:(q + 1) * P], core.mean_mat[:, 0:1],
                                 start=True, stop=True)
            last.then_inc(msq_ready, 1)

        def unit(u, g, i, p):
            news = coming(g, i) if inside(u, UN) else []
            if inside(u - 1, UN):
                pe.wait_ge(update_ready, 2 * u)
            if inside(u, UN):
                if i == 0:
                    pe.wait_ge(keysT_ready, g * GB + GB)
                pe.wait_ge(query_kept, u + 1)
                scores(u, i, p, 0)
            if inside(u - 1, UN):
                if inside(u, UN):
                    pe.wait_ge(mean_kept, u + 1)
                for q in range(2):
                    turn_update(u - 1, q)
                sl = slots[:, bass.ds(at(g, i - 1), HS)]
                pe.matmul(hn_bank, hh_w[:, 2, :], sl, start=True, stop=True)
                pe.matmul(r_bank, hh_w[:, 0, :], sl, start=True, stop=False).then_inc(hh_ready, 1)
            if inside(u, UN):
                turn_scores(u, 0)
                scores(u, i, p, 1)
                for n, b in news[:1]:
                    turn_keys(n, 1 - p, b)
                turn_scores(u, 1)
            if inside(u - 1, UN):
                pe.matmul(z_bank, hh_w[:, 1, :], sl, start=True, stop=False)
                pe.wait_ge(updT_ready, u)
                pe.wait_ge(hn_kept, u)
                pe.matmul(r_bank, in_w[:, 0, :], updT[:, :], start=False, stop=True).then_inc(r_ready, 1)
                pe.matmul(z_bank, in_w[:, 1, :], updT[:, :], start=False, stop=True)
                pe.matmul(xn_bank, in_w[:, 2, :], updT[:, :], start=True, stop=True).then_inc(zn_ready, 1)
            if inside(u, UN):
                for n, b in news[1:]:
                    turn_keys(n, 1 - p, b)
                if inside(u - 1, UN):
                    pe.wait_ge(cand_in_ready, u)
                mix(u, i, p, 0)
                mix(u, i, p, 1)
                if inside(u + 1, UN):
                    transform_slots(u + 1, g, i + 1)

        for b in range(GB):
            turn_keys(b, 0, b)
        transform_slots(0, 0, 0)
        run_units(pe, unit)

    @block.scalar
    def _(act):
        def squares(n, k):
            landed(act, n, k % R)
            for t in range(3):
                last = act.activation(junk[:, t, :], raw[k % R][:, t, :], ACT.Square,
                                      accum_out=sumsq[k % R][:, t:t + 1])
            last.then_inc(sumsq_ready, 1)
            act.wait_ge(sumsq_ready, n + 1)

        def keep_keysT(n, p, b):
            act.wait_ge(keys_turned, n + 1)
            act.copy(keysT[p][:, b, :], key_bank[:, 0:SC]).then_inc(keysT_ready, 1)

        def keep_scores(u, q):
            act.wait_ge(score_ready, 2 * u + q + 1)
            act.activation(score[q][:, :], score_bank[:, 0:SC], ACT.Copy, scale=srstd[:, q:q + 1]).then_inc(score_kept, 1)

        def exponentials(u, q):
            act.wait_ge(less_ready, 2 * u + q + 1)
            act.activation(less[q][:, :, :], less[q][:, :, :], ACT.Exp).then_inc(exp_ready, 1)

        def keep_query(u):
            act.wait_ge(query_ready, u + 1)
            act.activation(query[:, :], query_bank, ACT.Copy, scale=key_scale[:, 0:1]).then_inc(query_kept, 1)

        def unit(u, g, i, p):
            news = coming(g, i) if inside(u, UN) else []
            if inside(u, UN):
                act.wait_ge(srstd_ready, u + 1)
                keep_scores(u, 0)
            if inside(u - 1, UN):
                act.wait_ge(update_turned, 2 * u)
                act.copy(updT[:, :], update_bank).then_inc(updT_ready, 1)
                act.wait_ge(hh_ready, u)
                act.activation(half_hn[:, :], hn_bank, ACT.Identity, scale=0.5, bias=half_b[:, 2:3]).then_inc(hn_kept, 1)
            if inside(u, UN):
                keep_scores(u, 1)
                exponentials(u, 0)
            for n, b in news[:1]:
                keep_keysT(n, 1 - p, b)
            if inside(u - 1, UN):
                act.wait_ge(r_ready, u)
                act.activation(tanh_r[:, :], r_bank, ACT.Tanh, scale=0.5, bias=half_b[:, 0:1]).then_inc(tanh_r_ready, 1)
            if inside(u, UN):
                exponentials(u, 1)
            if inside(u - 1, UN):
                act.wait_ge(zn_ready, u)
                act.activation(tanh_z[:, :], z_bank, ACT.Tanh, scale=0.5, bias=half_b[:, 1:2]).then_inc(tanh_z_ready, 1)
            for n, b in news[1:]:
                keep_keysT(n, 1 - p, b)
            if inside(u - 1, UN):
                act.wait_ge(cand_in_ready, u)
                act.activation(cand[:, :], cand_in[:, :], ACT.Tanh, bias=core.vec("bih_n")).then_inc(cand_ready, 1)
            if inside(u, UN):
                for n, b in coming(g, i + 1):
                    squares(n, b)
            if inside(u + 1, UN):
                keep_query(u + 1)

        for b in range(GB):
            squares(b, b)
            keep_keysT(b, 0, b)
        for n, b in coming(0, 0):
            squares(n, b)
        keep_query(0)
        run_units(act, unit)

    @block.vector
    def _(dve):
        dve.memset(minus_half[:, :], -0.5)
        dve.memset(eps_sum[:, :], 1e-6 * D)
        for p in range(2):
            dve.memset(keys[p][:, :, :, D:D + 1], 1.0)
        for k in range(R):
            ins = dve.memset(raw[k][:, 2, :], 0.0)
        ins.then_inc(cleared, 1)

        def scale_keys(n, p, b):
            dve.wait_ge(krstd_ready, n + 1)
            for t in range(3):
                last = dve.tensor_scalar(keys[p][:, b, t, 0:D], raw[b % R][:, t, :], krstd[b % R][:, t:t + 1],
                                         float(D) ** 0.5, ALU.mult, ALU.mult)
            last.then_inc(keys_ready, 1)

        def take_update(u, q):
            n = 2 * u + q + 1
            dve.wait_ge(mix_ready, n)
            dve.tensor_scalar(mass[q][:, :], mix_bank[q][:, D:D + 1], 1e-6, None, ALU.add).then_inc(mass_ready, 1)
            dve.wait_ge(mass_ready, n)
            dve.reciprocal(rmass[q][:, :], mass[q][:, :]).then_inc(rmass_ready, 1)
            dve.wait_ge(rmass_ready, n)
            dve.tensor_scalar(update[q][:, :], mix_bank[q][:, 0:D], rmass[q][:, 0:1], None, ALU.mult).then_inc(update_ready, 1)

        def below_max(u, q):
            turned = turned_bank[q][0:ST, 0:3 * P].rearrange("p (g k) -> p g k", k=S)
            dve.wait_ge(score_turned, 2 * u + q + 1)
            dve.tensor_reduce(big[q][:, :], turned, AX, ALU.max).then_inc(big_ready, 1)
            dve.wait_ge(big_ready, 2 * u + q + 1)
            dve.tensor_tensor(less[q][:, :, :], turned, big[q][:, :].unsqueeze(2).to_broadcast([ST, 12, S]),
                              ALU.subtract).then_inc(less_ready, 1)

        def softmax(u, q):
            n = 2 * u + q + 1
            dve.wait_ge(exp_ready, n)
            dve.tensor_reduce(total[q][:, :], less[q][:, :, :], AX, ALU.add).then_inc(total_ready, 1)
            dve.wait_ge(total_ready, n)
            dve.reciprocal(rtotal[q][:, :], total[q][:, :]).then_inc(rtotal_ready, 1)
            dve.wait_ge(rtotal_ready, n)
            dve.tensor_tensor(attn[q][:, :, :], less[q][:, :, :], rtotal[q][:, :].unsqueeze(2).to_broadcast([ST, 12, S]),
                              ALU.mult).then_inc(attn_ready, 1)

        def square_slots(u, g, i):
            if inside(u - 2, UN):
                dve.wait_ge(slots_ready, u - 1)
            if inside(u - 1, UN):
                dve.wait_ge(msq_ready, u)
            sl = slots[:, bass.ds(at(g, i), HS)]
            dve.tensor_tensor(sq[:, :], sl, sl, ALU.mult).then_inc(sq_ready, 1)

        def keep_mean(u):
            dve.wait_ge(msq_ready, u + 1)
            dve.tensor_scalar(mean_sq[:, :], msq_bank, 1e-6, None, ALU.add).then_inc(mean_kept, 1)

        def unit(u, g, i, p):
            news = coming(g, i) if inside(u, UN) else []
            for n, b in news:
                scale_keys(n, 1 - p, b)
            if inside(u, UN):
                below_max(u, 0)
                below_max(u, 1)
                softmax(u, 0)
            if inside(u - 1, UN):
                dve.wait_ge(tanh_r_ready, u)
                dve.scalar_tensor_tensor(cand_in[:, :], tanh_r[:, :], 1.0, half_hn[:, :], ALU.add,
                                         ALU.mult).then_inc(reset_done, 1)
                dve.wait_ge(zn_ready, u)
                dve.wait_ge(reset_done, u)
                dve.tensor_tensor(cand_in[:, :], cand_in[:, :], xn_bank, ALU.add).then_inc(cand_in_ready, 1)
            if inside(u, UN):
                softmax(u, 1)
            if inside(u - 1, UN):
                sl = slots[:, bass.ds(at(g, i - 1), HS)]
                dve.wait_ge(tanh_z_ready, u)
                dve.tensor_scalar(new_share[:, :], tanh_z[:, :], -0.5, 0.5, ALU.mult, ALU.add)
                dve.scalar_tensor_tensor(old_twice[:, :], tanh_z[:, :], 1.0, sl, ALU.add, ALU.mult).then_inc(share_ready, 1)
                dve.wait_ge(share_ready, u)
                dve.wait_ge(cand_ready, u)
                dve.tensor_tensor(new_share[:, :], new_share[:, :], cand[:, :], ALU.mult).then_inc(new_ready, 1)
                dve.wait_ge(new_ready, u)
                dve.scalar_tensor_tensor(sl, old_twice[:, :], 0.5, new_share[:, :], ALU.mult, ALU.add).then_inc(slots_ready, 1)
            if inside(u + 1, UN):
                square_slots(u + 1, g, i + 1)
            if inside(u, UN):
                take_update(u, 0)
                take_update(u, 1)
            if inside(u + 1, UN):
                keep_mean(u + 1)

        for b in range(GB):
            scale_keys(b, 0, b)
        square_slots(0, 0, 0)
        keep_mean(0)
        run_units(dve, unit)


def rotary_attention(core):
    nc, sem, banks, xT, d = core.nc, core.sem, core.banks, core.xT, core.d
    with ExitStack() as ctx:
        def sb(name, shape):
            return ctx.enter_context(nc.sbuf_tensor(f"r_{name}_sb", shape, F32))

        xn = sb("xn", [P, TOK])
        layer_norm(core, "r_ln", xT, xn, 1e-5)
        w = sb("w", [P, 6, D])
        turn = sb("turn", [P, 4, S])
        own_head = sb("own_head", [P, RH])
        own_batch = sb("own_batch", [P, 4])
        own_quarter = sb("own_quarter", [P, 4])
        out_b = sb("out_b", [P, 1])
        xt = [sb(f"xt{p}", [P, CH]) for p in range(2)]
        part = [sb(f"part{u}", [P, BPC, S]) for u in range(2)]
        qT = [sb(f"qT{p}", [P, CH]) for p in range(2)]
        kT = [sb(f"kT{p}", [P, CH]) for p in range(2)]
        spread = [sb(f"spread{u}", [P, 4, RH, S]) for u in range(2)]
        big = [sb(f"big{u}", [P, RH]) for u in range(2)]
        less = [sb(f"less{u}", [P, RH, S]) for u in range(2)]
        total = [sb(f"total{u}", [P, RH]) for u in range(2)]
        rtotal = [sb(f"rtotal{u}", [P, RH]) for u in range(2)]
        attn = [sb(f"attn{u}", [P, RH * S]) for u in range(2)]
        attnT = [sb(f"attnT{u}", [P, RH * S]) for u in range(2)]
        vals = [sb(f"vals{u}", [P, 4, D]) for u in range(2)]
        own = [sb(f"own{u}", [P, 4, S, 4]) for u in range(2)]
        oT = sb("oT", [P, CH])

        loaded = sem("r_loaded")
        bias_prod = sem("r_bias_prod")
        bias_ready = sem("r_bias_ready")
        xt_ready = sem("r_xt_ready")
        proj_ready = sem("r_proj_ready")
        part_ready = sem("r_part_ready")
        turned_ready = sem("r_turned_ready")
        spread_ready = sem("r_spread_ready")
        score_ready = sem("r_score_ready")
        big_ready = sem("r_big_ready")
        less_ready = sem("r_less_ready")
        exp_ready = sem("r_exp_ready")
        total_ready = sem("r_total_ready")
        rtotal_ready = sem("r_rtotal_ready")
        attn_ready = sem("r_attn_ready")
        attnT_ready = sem("r_attnT_ready")
        v_ready = sem("r_v_ready")
        vals_ready = sem("r_vals_ready")
        mix_ready = sem("r_mix_ready")
        own_ready = sem("r_own_ready")
        o_ready = sem("r_o_ready")
        y_ready = sem("r_y_ready")
        y_added = sem("r_y_added")
        Q = 4

        def at_least(eng, s, count):
            if not isinstance(count, int) or count > 0:
                eng.wait_ge(s, count)

        block = ctx.enter_context(nc.Block())

        @block.sync
        def _(sp):
            sp.dma_start(w[:, :, :], d["r_w"]).then_inc(loaded, 16)
            sp.dma_start(turn[:, :, :], d["r_turn"]).then_inc(loaded, 16)
            sp.dma_start(own_head[:, :], d["r_own_head"]).then_inc(loaded, 16)
            sp.dma_start(own_batch[:, :], d["r_own_batch"]).then_inc(loaded, 16)
            sp.dma_start(own_quarter[:, :], d["r_own_quarter"]).then_inc(loaded, 16)

        @block.gpsimd
        def _(pool):
            pool.wait_ge(loaded, 80)

            def step(c, p):
                pool.wait_ge(turned_ready, 2 * c + 2)
                for q in range(Q):
                    at_least(pool, score_ready, c * Q + q - 1)
                    for j in range(4):
                        k = kT[p][:, (4 * q + j) * S:(4 * q + j + 1) * S].unsqueeze(1).to_broadcast([P, RH, S])
                        m = own_head[:, :].unsqueeze(2).to_broadcast([P, RH, S])
                        pool.tensor_tensor(spread[q % 2][:, j, :, :], k, m, ALU.mult).then_inc(spread_ready, 1)

            run_steps(pool, step, NCH, 2)

        @block.tensor
        def _(pe):
            pe.wait_ge(loaded, 80)
            pe.matmul(banks[7][:, 0:1], w[:, 5, :], core.vec("r_bv"), start=True, stop=True).then_inc(bias_prod, 1)

            def project(c, which):
                at_least(pe, turned_ready, 2 * c + which)
                for half in range(2):
                    last = pe.matmul(banks[5 + half][:, :], w[:, 2 * which + half, :], xn[:, bass.ds(c * CH, CH)],
                                     start=True, stop=True)
                last.then_inc(proj_ready, 1)

            def values(c, p):
                pe.wait_ge(xt_ready, c + 1)
                at_least(pe, vals_ready, c * Q)
                for q in range(Q):
                    last = pe.matmul(banks[4][:, q * P:(q + 1) * P], xt[p][:, q * P:(q + 1) * P], w[:, 4, :],
                                     start=True, stop=True)
                last.then_inc(v_ready, 1)

            def scores(c, p, q):
                n = c * Q + q
                at_least(pe, less_ready, n - 1)
                for j in range(4):
                    pe.wait_ge(spread_ready, 4 * n + j + 1)
                    last = pe.matmul(banks[q % 2][j * S:(j + 1) * S, :], qT[p][:, (4 * q + j) * S:(4 * q + j + 1) * S],
                                     spread[q % 2][:, j, :, :].rearrange("p h t -> p (h t)"), start=True, stop=True)
                last.then_inc(score_ready, 1)

            def mix(c, q):
                n = c * Q + q
                pe.wait_ge(attnT_ready, n + 1)
                pe.wait_ge(vals_ready, n + 1)
                for j in range(4):
                    for g in range(4):
                        last = pe.matmul(banks[2 + q % 2][g * S:(g + 1) * S, j * P:(j + 1) * P],
                                         vals[q % 2][:, j, g * S:(g + 1) * S], attnT[q % 2][:, g * P:(g + 1) * P],
                                         start=True, stop=True)
                last.then_inc(mix_ready, 1)

            def step(c, p):
                for q in range(Q + 1):
                    if q < Q:
                        scores(c, p, q)
                    if q >= 1:
                        mix(c, q - 1)
                    if inside(c + 1, NCH):
                        if q == 0:
                            project(c + 1, 0)
                        if q == 2:
                            project(c + 1, 1)
                        if q == 4:
                            values(c + 1, 1 - p)
                pe.wait_ge(o_ready, c * Q + Q)
                pe.wait_ge(bias_ready, 1)
                pe.matmul(banks[7][:, :], w[:, 5, :], oT[:, :], start=True, stop=True).then_inc(y_ready, 1)

            project(0, 0)
            project(0, 1)
            values(0, 0)
            run_steps(pe, step, NCH, 2)

        @block.scalar
        def _(act):
            def copy_tile(c, p):
                act.copy(xt[p][:, :], xn[:, bass.ds(c * CH, CH)]).then_inc(xt_ready, 1)

            def step(c, p):
                for q in range(Q):
                    act.wait_ge(less_ready, c * Q + q + 1)
                    act.activation(less[q % 2][:, :, :], less[q % 2][:, :, :], ACT.Exp).then_inc(exp_ready, 1)
                    if q == 0 and inside(c + 1, NCH):
                        act.wait_ge(v_ready, c + 1)
                        copy_tile(c + 1, 1 - p)

            copy_tile(0, 0)
            run_steps(act, step, NCH, 2)

        @block.vector
        def _(dve):
            dve.wait_ge(loaded, 80)
            dve.wait_ge(bias_prod, 1)
            dve.tensor_tensor(out_b[:, :], banks[7][:, 0:1], core.vec("r_bo"), ALU.add).then_inc(bias_ready, 1)

            def rotate(c, p, which):
                n = 2 * c + which
                dve.wait_ge(proj_ready, n + 1)
                at_least(dve, turned_ready, n)
                names = ("r_bqa", "r_bqb") if which == 0 else ("r_bka", "r_bkb")
                for half in range(2):
                    last = dve.scalar_tensor_tensor(
                        part[half][:, :, :], banks[5 + half][:, :].rearrange("p (b s) -> p b s", s=S),
                        core.vec(names[half]), turn[:, 2 * which + half, :].unsqueeze(1).to_broadcast([P, BPC, S]),
                        ALU.add, ALU.mult)
                last.then_inc(part_ready, 1)
                dve.wait_ge(part_ready, n + 1)
                dst = (qT, kT)[which][p]
                dve.tensor_tensor(dst[:, :].rearrange("p (b s) -> p b s", s=S), part[0][:, :, :], part[1][:, :, :],
                                  ALU.add).then_inc(turned_ready, 1)

            def take(c, q):
                n = c * Q + q
                u = q % 2
                dve.wait_ge(mix_ready, n + 1)
                dve.tensor_tensor(own[u][:, :, :, :].rearrange("p b s h -> p b h s"),
                                  banks[2 + u][:, :].rearrange("p (b h s) -> p b h s", b=4, h=4),
                                  own_quarter[:, :].unsqueeze(1).unsqueeze(3).to_broadcast([P, 4, 4, S]),
                                  ALU.mult).then_inc(own_ready, 1)
                if q == 0:
                    at_least(dve, y_ready, c)
                dve.wait_ge(own_ready, n + 1)
                dve.tensor_reduce(oT[:, q * P:(q + 1) * P].rearrange("p (b s) -> p b s", b=4), own[u][:, :, :, :], AX,
                                  ALU.add).then_inc(o_ready, 1)

            def step(c, p):
                for q in range(Q + 1):
                    n = c * Q + q
                    u = q % 2
                    if q < Q:
                        dve.wait_ge(score_ready, n + 1)
                        s = banks[u][:, :].rearrange("p (h t) -> p h t", t=S)
                        dve.tensor_reduce(big[u][:, :], s, AX, ALU.max).then_inc(big_ready, 1)
                        dve.wait_ge(big_ready, n + 1)
                        dve.tensor_tensor(less[u][:, :, :], s, big[u][:, :].unsqueeze(2).to_broadcast([P, RH, S]),
                                          ALU.subtract).then_inc(less_ready, 1)
                        dve.wait_ge(v_ready, c + 1)
                        dve.tensor_tensor(vals[u][:, :, :],
                                          banks[4][:, q * P:(q + 1) * P].unsqueeze(1).to_broadcast([P, 4, D]),
                                          own_batch[:, :].unsqueeze(2).to_broadcast([P, 4, D]),
                                          ALU.mult).then_inc(vals_ready, 1)
                    if q >= 1:
                        take(c, q - 1)
                    if q < Q:
                        dve.wait_ge(exp_ready, n + 1)
                        dve.tensor_reduce(total[u][:, :], less[u][:, :, :], AX, ALU.add).then_inc(total_ready, 1)
                        dve.wait_ge(total_ready, n + 1)
                        dve.reciprocal(rtotal[u][:, :], total[u][:, :]).then_inc(rtotal_ready, 1)
                        dve.wait_ge(rtotal_ready, n + 1)
                        dve.tensor_tensor(attn[u][:, :].rearrange("p (h t) -> p h t", t=S), less[u][:, :, :],
                                          rtotal[u][:, :].unsqueeze(2).to_broadcast([P, RH, S]),
                                          ALU.mult).then_inc(attn_ready, 1)
                        dve.wait_ge(attn_ready, n + 1)
                        dve.transpose(attnT[u][:, :], attn[u][:, :]).then_inc(attnT_ready, 1)
                    if inside(c + 1, NCH):
                        if q == 1:
                            rotate(c + 1, 1 - p, 0)
                        if q == 3:
                            rotate(c + 1, 1 - p, 1)
                dve.wait_ge(y_ready, c + 1)
                x = xT[:, bass.ds(c * CH, CH)]
                dve.scalar_tensor_tensor(x, banks[7][:, :], out_b[:, 0:1], x, ALU.add, ALU.add).then_inc(y_added, 1)
                dve.wait_ge(y_added, c + 1)

            rotate(0, 0, 0)
            rotate(0, 0, 1)
            run_steps(dve, step, NCH, 2)


def mlp(core):
    nc, sem, banks, xT, ident, d = core.nc, core.sem, core.banks, core.xT, core.ident, core.d
    T = CH // P
    FT = FF // P
    with ExitStack() as ctx:
        def sb(name, shape):
            return ctx.enter_context(nc.sbuf_tensor(f"f_{name}_sb", shape, F32))

        xn = sb("xn", [P, TOK])
        layer_norm(core, "f_ln", xT, xn, 1e-5)
        tile = sb("tile", [P, CH])
        w1 = sb("w1", [P, FF])
        w2 = sb("w2", [P, FT, D])
        router = sb("router", [P, E])
        hidden = sb("hidden", [P, FT, CH])
        shifted = sb("shifted", [P, T, E])
        top_ex = sb("top_ex", [P, T, E])
        top = sb("top", [P, T, 2])
        big = sb("big", [P, T])
        negmax = sb("negmax", [P, T])
        ex = sb("ex", [P, T, E])
        total = sb("total", [P, T])
        rtotal = sb("rtotal", [P, T])
        pair = sb("pair", [P, T])
        rpair = sb("rpair", [P, T])
        share = sb("share", [P, T, 2])
        factor = sb("factor", [P, T])
        rows = sb("rows", [P, T, P])
        ones = sb("ones", [P, P])
        factorT = sb("factorT", [P, CH])
        mixed = sb("mixed", [P, CH])

        loaded = sem("f_loaded")
        ones_set = sem("f_ones_set")
        tile_ready = sem("f_tile_ready")
        logit_ready = sem("f_logit_ready")
        small = sem("f_small")
        exp_ready = sem("f_exp_ready")
        rows_ready = sem("f_rows_ready")
        hidden_ready = sem("f_hidden_ready")
        gelu_ready = sem("f_gelu_ready")
        factor_turned = sem("f_factor_turned")
        factor_ready = sem("f_factor_ready")
        y_ready = sem("f_y_ready")
        y_scaled = sem("f_y_scaled")
        y_added = sem("f_y_added")
        factor_sum = sem("f_factor_sum")
        block = ctx.enter_context(nc.Block())

        @block.sync
        def _(sp):
            sp.dma_start(w1[:, :], d["f_w1"]).then_inc(loaded, 16)
            sp.dma_start(w2[:, :, :], d["f_w2"]).then_inc(loaded, 16)
            sp.dma_start(router[:, :], d["f_router"]).then_inc(loaded, 16)

        @block.gpsimd
        def _(pool):
            with pool.Fori(0, NCH) as c:
                pool.wait_ge(logit_ready, c)
                pool.tensor_copy(tile[:, :], xn[:, bass.ds(c * CH, CH)]).then_inc(tile_ready, 1)

        @block.tensor
        def _(pe):
            pe.wait_ge(loaded, 48)
            with pe.Fori(0, NCH) as c:
                pe.wait_ge(tile_ready, c + 1)
                for t in range(T):
                    last = pe.matmul(banks[0][:, t * E:(t + 1) * E], tile[:, t * P:(t + 1) * P], router[:, :],
                                     start=True, stop=True)
                last.then_inc(logit_ready, 1)
                for f in range(FT):
                    pe.matmul(banks[1 + f][:, :], w1[:, f * P:(f + 1) * P], xn[:, bass.ds(c * CH, CH)],
                              start=True, stop=True).then_inc(hidden_ready, 1)
                for f in range(FT):
                    pe.wait_ge(gelu_ready, c * FT + f + 1)
                    last = pe.matmul(banks[5][:, :], w2[:, f, :], hidden[:, f, :], start=(f == 0), stop=(f == FT - 1))
                last.then_inc(y_ready, 1)
                pe.wait_ge(rows_ready, c + 1)
                for t in range(T):
                    last = pe.transpose(banks[6][:, t * P:(t + 1) * P], rows[:, t, :], ident[:, :])
                last.then_inc(factor_turned, 1)
                pe.wait_ge(y_scaled, c + 1)

        @block.scalar
        def _(act):
            with act.Fori(0, NCH) as c:
                act.wait_ge(small, c * 9 + 3)
                act.activation(ex[:, :, :], shifted[:, :, :], ACT.Exp).then_inc(exp_ready, 1)
                for f in range(FT):
                    act.wait_ge(hidden_ready, c * FT + f + 1)
                    act.activation(hidden[:, f, :], banks[1 + f][:, :], ACT.Gelu_apprx_tanh,
                                   bias=core.vec(f"f_b1_{f}")).then_inc(gelu_ready, 1)
                act.wait_ge(factor_turned, c + 1)
                act.copy(factorT[:, :], banks[6][:, :]).then_inc(factor_ready, 1)

        @block.vector
        def _(dve):
            dve.memset(ones[:, :], 1.0).then_inc(ones_set, 1)
            dve.wait_ge(ones_set, 1)
            with dve.Fori(0, NCH) as c:
                count = [0]

                def after(ins):
                    count[0] += 1
                    ins.then_inc(small, 1)
                    dve.wait_ge(small, c * 9 + count[0])

                dve.wait_ge(logit_ready, c + 1)
                logits = banks[0][:, 0:T * E].rearrange("p (t e) -> p t e", t=T)
                after(dve.tensor_reduce(big[:, :], logits, AX, ALU.max))
                after(dve.tensor_scalar(negmax[:, :], big[:, :], -1.0, None, ALU.mult))
                after(dve.tensor_tensor(shifted[:, :, :], logits,
                                        negmax[:, :].unsqueeze(2).to_broadcast([P, T, E]), ALU.add))
                dve.wait_ge(exp_ready, c + 1)
                dve.tensor_reduce(total[:, :], ex[:, :, :], AX, ALU.add)
                for t in range(T):
                    last = dve.max(top_ex[:, t, :], ex[:, t, :])
                after(last)
                after(dve.reciprocal(rtotal[:, :], total[:, :]))
                after(dve.tensor_tensor(top[:, :, :], top_ex[:, :, 0:2],
                                        rtotal[:, :].unsqueeze(2).to_broadcast([P, T, 2]), ALU.mult))
                after(dve.tensor_reduce(pair[:, :], top[:, :, :], AX, ALU.add))
                after(dve.reciprocal(rpair[:, :], pair[:, :]))
                after(dve.tensor_tensor(share[:, :, :], top[:, :, :],
                                        rpair[:, :].unsqueeze(2).to_broadcast([P, T, 2]), ALU.mult))
                dve.tensor_reduce(factor[:, :], share[:, :, :], AX, ALU.add).then_inc(factor_sum, 1)
                dve.wait_ge(factor_sum, c + 1)
                for t in range(T):
                    last = dve.tensor_scalar(rows[:, t, :], ones[:, :], factor[:, t:t + 1], None, ALU.mult)
                last.then_inc(rows_ready, 1)
                dve.wait_ge(y_ready, c + 1)
                dve.wait_ge(factor_ready, c + 1)
                dve.scalar_tensor_tensor(mixed[:, :], banks[5][:, :], core.vec("f_b2"), factorT[:, :], ALU.add,
                                         ALU.mult).then_inc(y_scaled, 1)
                dve.wait_ge(y_scaled, c + 1)
                x = xT[:, bass.ds(c * CH, CH)]
                dve.tensor_tensor(x, x, mixed[:, :], ALU.add).then_inc(y_added, 1)
                dve.wait_ge(y_added, c + 1)


STAGES = [cross_attention, linear_attention, experts, slot_attention, rotary_attention, mlp]


def hold_residual(core, name):
    core.xT_guard = core.nc.sbuf_tensor(name, [P, TOK], F32)
    core.xT = core.xT_guard.__enter__()


def run_stage(core, stage):
    nc, used, outer = core.nc, [], core.sem
    with ExitStack() as ctx:
        def sem(name):
            used.append(ctx.enter_context(nc.semaphore(name)))
            return used[-1]

        core.sem = sem
        stage(core)
        core.sem = outer
        with nc.Block() as block:
            @block.sync
            def _(sp):
                for s in used:
                    sp.sem_clear(s)


def build(nc, d, stages):
    core = Core()
    core.nc, core.d = nc, d
    with ExitStack() as ctx:
        core.sem = lambda name: ctx.enter_context(nc.semaphore(name))
        core.norms = [0]
        core.norm_sems = {n: core.sem(f"ln_{n}") for n in (
            "mean_ready", "centred_ready", "square_ready", "var_ready", "log_ready", "rstd_ready", "normed")}
        core.all_banks = ctx.enter_context(nc.psum_tensor("banks", [P, 8, 512], F32))
        core.banks = [core.all_banks[:, i, :] for i in range(8)]
        core.ident = ctx.enter_context(nc.sbuf_tensor("ident_sb", [P, P], F32))
        core.mean_mat = ctx.enter_context(nc.sbuf_tensor("mean_mat_sb", [P, P], F32))
        core.vecs = ctx.enter_context(nc.sbuf_tensor("vecs_sb", [P, len(VECS)], F32))
        core.eps5 = ctx.enter_context(nc.sbuf_tensor("eps5", [P, 1], F32))
        core.eps6 = ctx.enter_context(nc.sbuf_tensor("eps6", [P, 1], F32))
        scratch = lambda name, cols: nc.dram_tensor(name, (P, cols), F32, kind="Internal").ap()
        d["a_x"], d["a_x2"], d["a_xn"] = scratch("a_x", TOK), scratch("a_x2", TOK), scratch("a_xn", TOK)
        d["a_ks"] = scratch("a_ks", TOK // 2)
        core.vec = lambda name: core.vecs[:, VCOL[name]:VCOL[name] + 1]
        core.eps_col = lambda eps: (core.eps5 if eps == 1e-5 else core.eps6)[:, 0:1]
        hold_residual(core, "xT_sb")
        load_residual(core)
        for stage in stages:
            run_stage(core, stage)
        store_residual(core)
        core.xT_guard.__exit__(None, None, None)


def lay_out(inputs):
    i = {k: np.asarray(v) for k, v in inputs.items()}
    c = np.ascontiguousarray
    wkv = i["L0_xattn_Wkv"]
    heads = lambda w: c(w.reshape(D, XH, D).transpose(2, 1, 0))
    even = np.array([RD * h + 2 * (r % (RD // 2)) for h in range(RH) for r in range(RD)])
    a = {
        "xT": c(i["x"].reshape(TOK, D).T),
        "ctx": i["ctx_1024"],
        "ident": np.eye(P, dtype=np.float32),
        "mean_mat": np.full((P, P), 1.0 / D, np.float32),
        "g_media_rows": c(np.broadcast_to(i["L0_xattn_gamma_media"], (XROWS, D))),
        "b_media_rows": c(np.broadcast_to(i["L0_xattn_beta_media"], (XROWS, D))),
        "x_wqT": heads(i["L0_xattn_Wq"]),
        "x_wkT": heads(wkv[:, :XH * D]),
        "x_wvT": heads(wkv[:, XH * D:]),
        "x_wo": c(i["L0_xattn_Wo"].reshape(XH, D, D).transpose(1, 0, 2)),
    }
    bih, bhh = i["L1_xattn_gru_bih"].reshape(3, D), i["L1_xattn_gru_bhh"].reshape(3, D)
    cols = [i["L0_xattn_gamma_media"], i["L0_xattn_beta_media"], i["L0_xattn_gamma_lat"], i["L0_xattn_beta_lat"]]
    cols += list(i["L0_xattn_bq"].reshape(XH, D)) + list(i["L0_xattn_bkv"][XH * D:].reshape(XH, D))
    cols += [i["L0_xattn_bo"], i["L0_attn_bo"], i["L1_xattn_slot_norm_w"], i["L1_xattn_input_norm_w"], *bih, *bhh]
    cols += [i["L1_attn_bq"][even], i["L1_attn_bq"][even + 1], i["L1_attn_bk"][even], i["L1_attn_bk"][even + 1]]
    cols += [i["L1_attn_bv"], i["L1_attn_bo"], *i["L1_ffn_b1"].reshape(4, D), i["L1_ffn_b2"]]
    a["vecs"] = c(np.stack(cols, axis=1))
    more_arrays(i, a, c, even)
    return a


def more_arrays(i, a, c, even):
    a["a_wq"], a["a_wk"], a["a_wv"] = i["L0_attn_Wq"], i["L0_attn_Wk"], i["L0_attn_Wv"]
    a["a_wo"] = c(i["L0_attn_Wo"].reshape(LH, LH, D))
    a["a_fold"] = c(np.tile(np.eye(LD, dtype=np.float32), (2, 1))) * np.float32(LD ** -0.5)
    a["e_w"] = c(i["L0_ffn_expert_w"].transpose(1, 0, 2))
    a["e_gate"] = i["L0_ffn_gate_w"]
    a["e_gate_b"] = c(np.broadcast_to(i["L0_ffn_gate_b"], (P, E)))
    a["e_bias"] = i["L0_ffn_expert_b"]
    a["f_w1"] = i["L1_ffn_w1"]
    a["f_w2"] = c(i["L1_ffn_w2"].reshape(FF // P, P, D).transpose(1, 0, 2))
    a["f_router"] = i["L1_ffn_router_w"]
    a["s_wq"], a["s_wk"], a["s_wv"] = i["L1_xattn_Wq"], i["L1_xattn_Wk"], i["L1_xattn_Wv"]
    a["s_ihT"] = c(i["L1_xattn_gru_wih"].reshape(3, D, D).transpose(2, 0, 1))
    a["s_hhT"] = c(i["L1_xattn_gru_whh"].reshape(3, D, D).transpose(2, 0, 1))
    w = [i["L1_attn_Wq"][even], i["L1_attn_Wq"][even + 1], i["L1_attn_Wk"][even], i["L1_attn_Wk"][even + 1]]
    a["r_w"] = c(np.stack([m.T for m in w + [i["L1_attn_Wv"], i["L1_attn_Wo"]]], axis=1))
    freq = (1.0 / 10000.0 ** (np.arange(0, RD, 2) / RD)).astype(np.float32)
    angle = np.outer(freq, np.arange(S, dtype=np.float32)).astype(np.float32)
    cos, sin = np.cos(angle), np.sin(angle)
    first, second = np.concatenate([cos, sin]), np.concatenate([-sin, cos])
    turn = np.stack([first * RD ** -0.5, second * RD ** -0.5, first, second], axis=1)
    a["r_turn"] = np.tile(turn, (RH, 1, 1)).astype(np.float32)
    rows = np.arange(P)
    a["r_own_head"] = (rows[:, None] // RD == np.arange(RH)).astype(np.float32)
    a["r_own_batch"] = (rows[:, None] // S == np.arange(4)).astype(np.float32)
    a["r_own_quarter"] = (rows[:, None] // RD % 4 == np.arange(4)).astype(np.float32)


def kernel(**inputs):
    import concourse.bacc as bacc
    from concourse.bass_utils import run_bass_kernel_spmd

    nc = bacc.Bacc("TRN2", target_bir_lowering=False, num_devices=1)
    arrays = lay_out(inputs)
    d = {n: nc.dram_tensor(n, a.shape, mybir.dt.from_np(a.dtype), kind="ExternalInput").ap() for n, a in arrays.items()}
    d["out"] = nc.dram_tensor("out", (D, TOK), F32, kind="ExternalOutput").ap()
    build(nc, d, STAGES)
    got = run_bass_kernel_spmd(nc, [arrays], core_ids=[0]).results[0]["out"]
    return np.ascontiguousarray(np.asarray(got).T).reshape(B, S, D)
```

```python
from contextlib import ExitStack

import numpy as np

import concourse.bass as bass
from concourse import mybir

F32 = mybir.dt.float32
ALU = mybir.AluOpType
ACT = mybir.ActivationFunctionType
AX = mybir.AxisListType.X

P = 128
D = 128
B = 128
S = 32
M = 257
TOK = B * S
CH = 512
NCH = TOK // CH
BPC = CH // S

XH = 8
XROWS = 97
XLAT = M - 2 * XROWS
XKEYS = M + S
XK = [XROWS, XROWS, S + XLAT]
LH = 64
LD = 64
LT = 256
LHALF = LT // 2
NLC = TOK // LT
E = 8
ITERS = 3
ST = 86
SK = [86, 86, 85]
RH = 16
RD = 8
FF = 512

VECS = ["g_media", "b_media", "g_lat", "b_lat"] + [f"bq{h}" for h in range(8)] + [f"bv{h}" for h in range(8)] + [
    "x_bo", "a_bo", "slot_w", "input_w", "bih_r", "bih_z", "bih_n", "bhh_r", "bhh_z", "bhh_n",
    "r_bqa", "r_bqb", "r_bka", "r_bkb", "r_bv", "r_bo", "f_b1_0", "f_b1_1", "f_b1_2", "f_b1_3", "f_b2",
]
VCOL = {n: i for i, n in enumerate(VECS)}


def run_steps(eng, step, total, unroll):
    for n in range(unroll):
        step(n, n % unroll)
    with eng.Fori(unroll, total - 2 * unroll + 1, unroll) as base:
        for k in range(unroll):
            step(base + k, k)
    for n in range(total - unroll, total):
        step(n, n % unroll)


def inside(n, total):
    return not isinstance(n, int) or 0 <= n < total


LN_EXP_SET = "natural_log_exp_and_others"


class Core:
    pass


def layer_norm(core, tag, src, dst, eps, gamma=None, beta=None, beside=None):
    nc = core.nc
    s = core.norm_sems
    mean_ready, centred_ready, square_ready = s["mean_ready"], s["centred_ready"], s["square_ready"]
    var_ready, log_ready, rstd_ready, normed = s["var_ready"], s["log_ready"], s["rstd_ready"], s["normed"]
    done = core.norms[0] * NCH
    core.norms[0] += 1
    banks = core.banks
    with ExitStack() as ctx:
        def sb(name, shape):
            return ctx.enter_context(nc.sbuf_tensor(f"{tag}_{name}", shape, F32))

        centred = sb("centred", [P, 2, CH])
        square = sb("square", [P, 2, CH])
        logvar = sb("logvar", [P, 2, CH])
        rstd = sb("rstd", [P, 2, CH])
        block = ctx.enter_context(nc.Block())

        if beside is not None:
            @block.sync
            def _(sp):
                beside(sp)

        @block.tensor
        def _(pe):
            def mean(c, u):
                if inside(c - 2, NCH):
                    pe.wait_ge(centred_ready, done + c - 1)
                pe.matmul(banks[u][:, :], core.mean_mat[:, :], src[:, bass.ds(c * CH, CH)],
                          start=True, stop=True).then_inc(mean_ready, 1)

            def step(c, u):
                if inside(c + 1, NCH):
                    mean(c + 1, 1 - u)
                pe.wait_ge(square_ready, done + c + 1)
                if inside(c - 2, NCH):
                    pe.wait_ge(log_ready, done + c - 1)
                pe.matmul(banks[2 + u][:, :], core.mean_mat[:, :], square[:, u, :],
                          start=True, stop=True).then_inc(var_ready, 1)

            mean(0, 0)
            run_steps(pe, step, NCH, 2)

        @block.vector
        def _(dve):
            def centre(c, u):
                dve.wait_ge(mean_ready, done + c + 1)
                if inside(c - 2, NCH):
                    dve.wait_ge(normed, done + c - 1)
                dve.tensor_tensor(centred[:, u, :], src[:, bass.ds(c * CH, CH)], banks[u][:, :],
                                  ALU.subtract).then_inc(centred_ready, 1)

            def step(c, u):
                if inside(c + 1, NCH):
                    centre(c + 1, 1 - u)
                out = dst[:, bass.ds(c * CH, CH)]
                dve.wait_ge(rstd_ready, done + c + 1)
                dve.tensor_tensor(out, centred[:, u, :], rstd[:, u, :], ALU.mult).then_inc(normed, 1)
                if gamma is not None:
                    dve.wait_ge(normed, done + c + 1)
                    dve.tensor_scalar(out, out, gamma, beta, ALU.mult, ALU.add)

            centre(0, 0)
            run_steps(dve, step, NCH, 2)

        @block.scalar
        def _(act):
            def squares(c, u):
                act.wait_ge(centred_ready, done + c + 1)
                if inside(c - 2, NCH):
                    act.wait_ge(var_ready, done + c - 1)
                act.activation(square[:, u, :], centred[:, u, :], ACT.Square).then_inc(square_ready, 1)

            def step(c, u):
                if inside(c + 1, NCH):
                    squares(c + 1, 1 - u)
                act.wait_ge(var_ready, done + c + 1)
                act.activation(logvar[:, u, :], banks[2 + u][:, :], ACT.Ln, bias=core.eps_col(eps)).then_inc(log_ready, 1)
                act.wait_ge(log_ready, done + c + 1)
                if inside(c - 2, NCH):
                    act.wait_ge(normed, done + c - 1)
                act.activation(rstd[:, u, :], logvar[:, u, :], ACT.Exp, scale=-0.5).then_inc(rstd_ready, 1)

            act.preload_act_table_set(LN_EXP_SET)
            squares(0, 0)
            run_steps(act, step, NCH, 2)


def load_residual(core):
    nc = core.nc
    loaded = core.sem("residual_loaded")
    eps_set = core.sem("eps_set")
    with nc.Block() as block:
        @block.sync
        def _(sp):
            sp.dma_start(core.ident[:, :], core.d["ident"]).then_inc(loaded, 16)
            sp.dma_start(core.mean_mat[:, :], core.d["mean_mat"]).then_inc(loaded, 16)
            sp.dma_start(core.vecs[:, :], core.d["vecs"]).then_inc(loaded, 16)
            sp.dma_start(core.xT[:, :], core.d["xT"]).then_inc(loaded, 16)
            sp.wait_ge(loaded, 64)

        @block.vector
        def _(dve):
            dve.memset(core.eps5[:, :], 1e-5)
            dve.memset(core.eps6[:, :], 1e-6).then_inc(eps_set, 1)


def store_residual(core):
    nc = core.nc
    stored = core.sem("residual_stored")
    with nc.Block() as block:
        @block.sync
        def _(sp):
            sp.dma_start(core.d["out"], core.xT[:, :]).then_inc(stored, 16)
            sp.wait_ge(stored, 16)


def cross_attention(core):
    nc, sem, banks, xT, ident = core.nc, core.sem, core.banks, core.xT, core.ident
    scale = float(D) ** -0.5
    CALL = XH * S

    with ExitStack() as ctx:
        def sb(name, shape):
            return ctx.enter_context(nc.sbuf_tensor(f"x_{name}_sb", shape, F32))

        latT = sb("latT", [P, TOK])
        qk_w = sb("qk_w", [P, XH, D])
        vo_w = sb("vo_w", [P, XH, D])
        qk_b = sb("qk_b", [P, XH])
        vo_b = sb("vo_b", [P, 1])

        w_loaded = sem("x_w_loaded")
        w_prod = sem("x_w_prod")
        w_done = sem("x_w_done")
        with ExitStack() as wctx:
            wq = wctx.enter_context(nc.sbuf_tensor("x_wq_sb", [P, XH, D], F32))
            wk = wctx.enter_context(nc.sbuf_tensor("x_wk_sb", [P, XH, D], F32))
            wv = wctx.enter_context(nc.sbuf_tensor("x_wv_sb", [P, XH, D], F32))
            wo = wctx.enter_context(nc.sbuf_tensor("x_wo_sb", [P, XH, D], F32))

            def load_weights(sp):
                for t, n in ((wq, "x_wqT"), (wk, "x_wkT"), (wv, "x_wvT"), (wo, "x_wo")):
                    sp.dma_start(t[:, :, :], core.d[n]).then_inc(w_loaded, 16)

            layer_norm(core, "x_ln0", xT, latT, 1e-5, beside=load_weights)
            layer_norm(core, "x_ln1", latT, latT, 1e-5, core.vec("g_lat"), core.vec("b_lat"))
            block = wctx.enter_context(nc.Block())

            @block.tensor
            def _(pe):
                pe.wait_ge(w_loaded, 64)
                for h in range(XH):
                    pe.matmul(banks[h // 4][:, (h % 4) * D:(h % 4 + 1) * D], wq[:, h, :], wk[:, h, :],
                              start=True, stop=True)
                    pe.matmul(banks[2 + h // 4][:, (h % 4) * D:(h % 4 + 1) * D], wv[:, h, :], wo[:, h, :],
                              start=True, stop=True)
                    pe.matmul(banks[4][:, h:h + 1], wk[:, h, :], core.vec(f"bq{h}"), start=True, stop=True)
                for h in range(XH):
                    last = pe.matmul(banks[5][:, 0:1], wo[:, h, :], core.vec(f"bv{h}"),
                                     start=(h == 0), stop=(h == XH - 1))
                last.then_inc(w_prod, 1)

            @block.vector
            def _(dve):
                dve.wait_ge(w_prod, 1)
                for g in range(2):
                    dve.tensor_scalar(qk_w[:, 4 * g:4 * g + 4, :],
                                      banks[g][:, :].rearrange("p (h d) -> p h d", h=4), scale, None, ALU.mult)
                    dve.tensor_copy(vo_w[:, 4 * g:4 * g + 4, :],
                                    banks[2 + g][:, :].rearrange("p (h d) -> p h d", h=4))
                dve.tensor_scalar(qk_b[:, :], banks[4][:, 0:XH], scale, None, ALU.mult)
                dve.tensor_tensor(vo_b[:, :], banks[5][:, 0:1], core.vec("x_bo"), ALU.add).then_inc(w_done, 1)

        G = sb("G", [P, B, XH, S])
        with ExitStack() as bctx:
            cross_attention_batches(core, bctx, latT, G, qk_w, qk_b, CALL)

        y_ready = sem("x_y_ready")
        y_added = sem("x_y_added")
        with nc.Block() as block:
            @block.tensor
            def _(pe):
                def step(c, k):
                    if inside(c - 2, NCH):
                        pe.wait_ge(y_added, c - 1)
                    for h in range(XH):
                        last = pe.matmul(banks[k][:, :], vo_w[:, h, :], G[:, bass.ds(c * BPC, BPC), h, :],
                                         start=(h == 0), stop=(h == XH - 1))
                    last.then_inc(y_ready, 1)

                run_steps(pe, step, NCH, 2)

            @block.vector
            def _(dve):
                def step(c, k):
                    dve.wait_ge(y_ready, c + 1)
                    x = xT[:, bass.ds(c * CH, CH)]
                    dve.scalar_tensor_tensor(x, banks[k][:, :], vo_b[:, 0:1], x, ALU.add, ALU.add).then_inc(y_added, 1)

                run_steps(dve, step, NCH, 2)


def cross_attention_batches(core, ctx, latT, G, qk_w, qk_b, CALL):
    nc, sem, banks, ident = core.nc, core.sem, core.banks, core.ident
    U = 4

    def sb(name, shape):
        return ctx.enter_context(nc.sbuf_tensor(f"x_{name}_sb", shape, F32))

    raw = [sb(f"raw{k}", [XROWS, 3, D]) for k in range(U)]
    xhat = sb("xhat", [XROWS, 3, D])
    scaled = sb("scaled", [XROWS, 3, D])
    keys = [sb(f"keys{k}", [XROWS, 3, D]) for k in range(U)]
    keysT = [sb(f"keysT{k}", [P, XKEYS]) for k in range(2)]
    lat = [sb(f"lat{k}", [P, S]) for k in range(2)]
    query = [sb(f"query{k}", [P, CALL]) for k in range(U)]
    probs = [sb(f"probs{k}", [P, 2, XKEYS]) for k in range(2)]
    probsT = sb("probsT", [P, 3, CALL])
    stats = sb("stats", [XROWS, 3, 6])
    meanvar = [sb(f"meanvar{k}", [XROWS, 3, 2]) for k in range(2)]
    vareps = sb("vareps", [XROWS, 3])
    rstd = [sb(f"rstd{k}", [XROWS, 3]) for k in range(2)]
    minus_half = sb("minus_half", [XROWS, 3])
    eps = sb("eps", [XROWS, 3])
    negmax = [sb(f"negmax{k}", [P, 2]) for k in range(2)]
    total = [sb(f"total{k}", [P, 2]) for k in range(2)]
    rtotal = [sb(f"rtotal{k}", [P, 2]) for k in range(2)]
    g_row = sb("g_row", [XROWS, D])
    b_row = sb("b_row", [XROWS, D])

    cleared = sem("x_cleared")
    rows_loaded = sem("x_rows_loaded")
    raw_loaded = [sem(f"x_raw_loaded{k}") for k in range(U)]
    query_loaded = [sem(f"x_query_loaded{k}") for k in range(U)]
    stats_ready = sem("x_stats_ready")
    meanvar_ready = sem("x_meanvar_ready")
    vareps_ready = sem("x_vareps_ready")
    rstd_ready = sem("x_rstd_ready")
    xhat_ready = sem("x_xhat_ready")
    scaled_ready = sem("x_scaled_ready")
    media_ready = sem("x_media_ready")
    lat_ready = sem("x_lat_ready")
    lat_turned = sem("x_lat_turned")
    keys_ready = sem("x_keys_ready")
    keys_turned = sem("x_keys_turned")
    keysT_ready = sem("x_keysT_ready")
    scores_ready = sem("x_scores_ready")
    max_ready = sem("x_max_ready")
    probs_ready = sem("x_probs_ready")
    rtotal_ready = sem("x_rtotal_ready")
    normp_ready = sem("x_normp_ready")
    probs_turned = sem("x_probs_turned")
    probsT_low = sem("x_probsT_low")
    probsT_high = sem("x_probsT_high")
    mix_ready = sem("x_mix_ready")
    mix_kept = sem("x_mix_kept")

    turn_bank = [banks[0], banks[1]]
    score_bank = [banks[2], banks[3]]
    pT_low, pT_high, mix_bank = banks[4], banks[5][:, 0:CALL], banks[6][:, 0:CALL]

    g_ready = sem("x_g_ready")
    g_kept = sem("x_g_kept")


    def load_media(sp, n, k):
        ctx_n = core.d["ctx"][bass.ds(n, 1), :, :]
        sp.dma_start(raw[k][:, 0:2, :],
                     ctx_n[:, 0:2 * XROWS, :].rearrange("b (t p) d -> p (b t) d", p=XROWS)).then_inc(raw_loaded[k], 16)
        sp.dma_start(raw[k][S:S + XLAT, 2, :],
                     ctx_n[:, 2 * XROWS:M, :].rearrange("b p d -> (b p) d")).then_inc(raw_loaded[k], 16)

    with nc.Block() as block:
        @block.vector
        def _(dve):
            for k in range(U):
                dve.memset(raw[k][:, 2, :], 0.0)
            dve.memset(minus_half[:, :], -0.5)
            dve.memset(eps[:, :], 1e-5).then_inc(cleared, 1)

        @block.sync
        def _(sp):
            sp.wait_ge(cleared, 1)
            for k in range(U):
                load_media(sp, k, k)
            sp.dma_start(g_row[:, :], core.d["g_media_rows"]).then_inc(rows_loaded, 16)
            sp.dma_start(b_row[:, :], core.d["b_media_rows"]).then_inc(rows_loaded, 16)

        @block.tensor
        def _(pe):
            def step(c, k):
                for h in range(XH):
                    if inside(c - 1, NCH):
                        pe.wait_ge(g_kept, (c - 1) * XH + h + 1)
                    pe.matmul(banks[h][:, :], qk_w[:, h, :], latT[:, bass.ds(c * CH, CH)],
                              start=True, stop=True).then_inc(g_ready, 1)

            run_steps(pe, step, NCH, 1)

        @block.scalar
        def _(act):
            def step(c, k):
                for h in range(XH):
                    act.wait_ge(g_ready, c * XH + h + 1)
                    act.activation(G[:, bass.ds(c * BPC, BPC), h, :],
                                   banks[h][:, :].rearrange("p (b i) -> p b i", i=S),
                                   ACT.Identity, bias=qk_b[:, h:h + 1]).then_inc(g_kept, 1)

            run_steps(act, step, NCH, 1)

    block = ctx.enter_context(nc.Block())

    @block.sync
    def _(sp):
        def load_query(n, k):
            sp.dma_start(query[k][:, :],
                         G[:, bass.ds(n, 1), :, :].rearrange("p b h i -> p (b h i)")).then_inc(query_loaded[k], 16)

        def step(n, k):
            if inside(n + U, B):
                sp.wait_ge(xhat_ready, n + 1)
                load_media(sp, n + U, k)
            if inside(n + U - 2, B):
                if inside(n - 2, B):
                    sp.wait_ge(scores_ready, 2 * (n - 2) + 2)
                load_query(n + U - 2, (k - 2) % U)

        for k in range(U - 2):
            load_query(k, k)
        run_steps(sp, step, B, U)

    @block.vector
    def _(dve):
        def moments(n, k):
            if isinstance(n, int):
                dve.wait_ge(raw_loaded[k], 32 * (n // U + 1))
            else:
                dve.wait_ge(raw_loaded[k], 32 * ((n - k) // U) + 32)
            if inside(n - 1, B):
                dve.wait_ge(meanvar_ready, n)
            for t in range(3):
                last = dve.bn_stats(stats[:, t, :], raw[k][:, t, :])
            last.then_inc(stats_ready, 1)

        def mean_variance(n, k):
            for t in range(3):
                last = dve.bn_aggr(meanvar[k % 2][:, t, :], stats[:, t, :])
            last.then_inc(meanvar_ready, 1)

        def normalise(n, k):
            dve.wait_ge(rstd_ready, n + 1)
            if inside(n - 1, B):
                dve.wait_ge(scaled_ready, n)
            for t in range(3):
                last = dve.tensor_scalar(xhat[:, t, :], raw[k][:, t, :], meanvar[k % 2][:, t, 0:1],
                                         rstd[k % 2][:, t:t + 1], ALU.subtract, ALU.mult)
            last.then_inc(xhat_ready, 1)

        def add_latents(n, k):
            dve.wait_ge(media_ready, n + 1)
            dve.wait_ge(lat_turned, n + 1)
            dve.tensor_copy(keys[k][0:S, 2, :], turn_bank[k % 2][0:S, 0:D]).then_inc(keys_ready, 1)

        def step(n, k):
            if inside(n + 2, B):
                normalise(n + 2, (k + 2) % U)
            if inside(n + 1, B):
                add_latents(n + 1, (k + 1) % U)
            if inside(n + 3, B):
                moments(n + 3, (k + 3) % U)
                dve.wait_ge(stats_ready, n + 4)
            if inside(n - 1, B):
                dve.wait_ge(probs_ready, 2 * n)
                dve.reciprocal(rtotal[(k - 1) % 2][:, :], total[(k - 1) % 2][:, :]).then_inc(rtotal_ready, 1)
            if inside(n + 3, B):
                mean_variance(n + 3, (k + 3) % U)
            if inside(n - 1, B):
                dve.wait_ge(rtotal_ready, n)
                for f in range(2):
                    dve.tensor_scalar(probs[(k - 1) % 2][:, f, :], probs[(k - 1) % 2][:, f, :],
                                      rtotal[(k - 1) % 2][:, f:f + 1], None, ALU.mult).then_inc(normp_ready, 1)
            if inside(n, B):
                for f in range(2):
                    dve.wait_ge(scores_ready, 2 * n + f + 1)
                    dve.tensor_reduce(negmax[k % 2][:, f:f + 1], score_bank[f][:, 0:XKEYS], AX, ALU.max,
                                      negate=True).then_inc(max_ready, 1)

        for n in range(3):
            moments(n, n)
            dve.wait_ge(stats_ready, n + 1)
            mean_variance(n, n)
            if n < 2:
                normalise(n, n)
        add_latents(0, 0)
        run_steps(dve, step, B, U)
        step(B, 0)

    @block.gpsimd
    def _(pool):
        def variance(n, k):
            pool.wait_ge(meanvar_ready, n + 1)
            pool.tensor_tensor(vareps[:, :], meanvar[k % 2][:, :, 1], eps[:, :], ALU.add).then_inc(vareps_ready, 1)
            pool.wait_ge(vareps_ready, n + 1)
            pool.tensor_tensor(rstd[k % 2][:, :], vareps[:, :], minus_half[:, :], ALU.pow).then_inc(rstd_ready, 1)

        def take_latents(n, k):
            if inside(n - 2, B):
                pool.wait_ge(lat_turned, n - 1)
            pool.tensor_copy(lat[k % 2][:, :], latT[:, bass.ds(n * S, S)]).then_inc(lat_ready, 1)

        def scale(n, k):
            pool.wait_ge(xhat_ready, n + 1)
            g = g_row[:, :].unsqueeze(1).to_broadcast([XROWS, 3, D])
            if inside(n - 1, B):
                pool.wait_ge(media_ready, n)
            pool.tensor_tensor(scaled[:, :, :], xhat[:, :, :], g, ALU.mult).then_inc(scaled_ready, 1)

        def shift(n, k):
            b = b_row[:, :].unsqueeze(1).to_broadcast([XROWS, 3, D])
            pool.wait_ge(scaled_ready, n + 1)
            if inside(n - U, B):
                pool.wait_ge(mix_ready, n - U + 1)
            pool.tensor_tensor(keys[k][:, :, :], scaled[:, :, :], b, ALU.add).then_inc(media_ready, 1)

        def step(n, k):
            if inside(n + 3, B):
                take_latents(n + 3, (k + 3) % U)
            if inside(n + 2, B):
                scale(n + 2, (k + 2) % U)
            if inside(n + 3, B):
                variance(n + 3, (k + 3) % U)
            if inside(n + 2, B):
                shift(n + 2, (k + 2) % U)

        pool.wait_ge(rows_loaded, 32)
        for n in range(3):
            take_latents(n, n)
        variance(0, 0)
        scale(0, 0)
        shift(0, 0)
        variance(1, 1)
        scale(1, 1)
        shift(1, 1)
        variance(2, 2)
        run_steps(pool, step, B, U)

    @block.tensor
    def _(pe):
        def turn_latents(n, k):
            pe.wait_ge(lat_ready, n + 1)
            pe.transpose(turn_bank[k % 2][0:S, 0:D], lat[k % 2][:, :], ident[:, :]).then_inc(lat_turned, 1)

        def turn_keys(n, k):
            pe.wait_ge(keys_ready, n + 1)
            for t in range(3):
                last = pe.transpose(turn_bank[k % 2][:, D + t * XROWS:D + t * XROWS + XK[t]],
                                    keys[k][0:XK[t], t, :], ident[0:XK[t], 0:XK[t]])
            last.then_inc(keys_turned, 1)

        def scores(n, k):
            pe.wait_ge(keysT_ready, n + 1)
            if isinstance(n, int):
                pe.wait_ge(query_loaded[k], 16 * (n // U + 1))
            else:
                pe.wait_ge(query_loaded[k], 16 * ((n - k) // U) + 16)
            if inside(n - 1, B):
                pe.wait_ge(probs_ready, 2 * n)
            for f in range(2):
                pe.matmul(score_bank[f][:, 0:XKEYS], query[k][:, f * P:(f + 1) * P], keysT[k % 2][:, :],
                          start=True, stop=True).then_inc(scores_ready, 1)

        def turn_probs(n, k):
            pe.wait_ge(normp_ready, 2 * n + 2)
            for t in range(3):
                for f in range(2):
                    out = pT_low[:, t * CALL:] if t < 2 else pT_high
                    last = pe.transpose(out[0:XK[t], f * P:(f + 1) * P],
                                        probs[k % 2][:, f, t * XROWS:t * XROWS + XK[t]], ident[:, :])
            last.then_inc(probs_turned, 1)

        def mix(n, k):
            pe.wait_ge(probsT_low, n + 1)
            pe.wait_ge(probsT_high, n + 1)
            if inside(n - 1, B):
                pe.wait_ge(mix_kept, n)
            for t in range(3):
                last = pe.matmul(mix_bank, keys[k][0:XK[t], t, :], probsT[0:XK[t], t, :],
                                 start=(t == 0), stop=(t == 2))
            last.then_inc(mix_ready, 1)

        def step(n, k):
            if inside(n, B):
                scores(n, k)
            if inside(n + 2, B):
                turn_latents(n + 2, (k + 2) % U)
            if inside(n + 1, B):
                turn_keys(n + 1, (k + 1) % U)
            if inside(n - 2, B):
                mix(n - 2, (k - 2) % U)
            if inside(n - 1, B):
                turn_probs(n - 1, (k - 1) % U)

        turn_latents(0, 0)
        turn_latents(1, 1)
        turn_keys(0, 0)
        run_steps(pe, step, B, U)
        step(B, 0)
        step(B + 1, 1)

    @block.scalar
    def _(act):
        def keep_keysT(n, k):
            act.wait_ge(keys_turned, n + 1)
            act.copy(keysT[k % 2][:, :], turn_bank[k % 2][:, D:D + XKEYS]).then_inc(keysT_ready, 1)

        def step(n, k):
            if inside(n + 1, B):
                keep_keysT(n + 1, (k + 1) % U)
            if inside(n, B):
                for f in range(2):
                    act.wait_ge(max_ready, 2 * n + f + 1)
                    act.activation(probs[k % 2][:, f, :], score_bank[f][:, 0:XKEYS], ACT.Exp,
                                   bias=negmax[k % 2][:, f:f + 1],
                                   accum_out=total[k % 2][:, f:f + 1]).then_inc(probs_ready, 1)
            if inside(n - 2, B):
                act.wait_ge(mix_ready, n - 1)
                act.copy(G[:, bass.ds(n - 2, 1), :, :].rearrange("p b h i -> p (b h i)"), mix_bank).then_inc(mix_kept, 1)
            if inside(n - 1, B):
                act.wait_ge(probs_turned, n)
                act.copy(probsT[0:XROWS, 0:2, :],
                         pT_low[0:XROWS, 0:2 * CALL].rearrange("p (t c) -> p t c", t=2)).then_inc(probsT_low, 1)
                act.copy(probsT[0:XK[2], 2, :], pT_high[0:XK[2], :]).then_inc(probsT_high, 1)

        keep_keysT(0, 0)
        run_steps(act, step, B, U)
        step(B, 0)
        step(B + 1, 1)


def linear_attention(core):
    nc, sem, d = core.nc, core.sem, core.d
    with ExitStack() as ctx:
        def sb(name, shape):
            return ctx.enter_context(nc.sbuf_tensor(f"a_{name}_sb", shape, F32))

        wq = core.xT
        wv = sb("wv", [P, LH * LD])
        wo = sb("wo", [P, LH, 2, D])
        w_loaded = sem("a_w_loaded")
        linear_attention_sums(core, wq, wv, wo, w_loaded)
        linear_attention_tokens(core, ctx, wq, wv, wo, w_loaded)


def linear_attention_sums(core, wq, wv, wo, w_loaded):
    nc, sem, banks = core.nc, core.sem, core.banks
    d = core.d
    PAIRS = LH // 2
    with ExitStack() as ctx:
        def sb(name, shape):
            return ctx.enter_context(nc.sbuf_tensor(f"a_{name}_sb", shape, F32))

        xn = sb("xn", [P, TOK])
        wk = sb("wk", [P, LH * LD])
        fold = sb("fold", [P, P])
        acc = [[sb(f"acc{k}{u}", [P, CH]) for u in range(2)] for k in range(2)]
        ksum = sb("ksum", [P, TOK])

        wk_loaded = sem("a_wk_loaded")
        cleared = sem("a_cleared")
        k_ready = sem("a_k_ready")
        k_added = sem("a_k_added")
        fold_ready = sem("a_fold_ready")
        ksum_kept = sem("a_ksum_kept")
        x_spilled = sem("a_x_spilled")
        spilled = sem("a_spilled")

        def load_and_spill(sp):
            sp.dma_start(wk[:, :], d["a_wk"]).then_inc(wk_loaded, 16)
            sp.dma_start(fold[:, :], d["a_fold"]).then_inc(wk_loaded, 16)
            sp.dma_start(d["a_x"], core.xT[:, :]).then_inc(x_spilled, 16)

        layer_norm(core, "a_ln", core.xT, xn, 1e-5, beside=load_and_spill)
        block = ctx.enter_context(nc.Block())

        @block.gpsimd
        def _(pool):
            pool.memset(wo[LD:P, :, 0, :], 0.0)
            pool.memset(wo[0:LD, :, 1, :], 0.0).then_inc(cleared, 1)

        @block.sync
        def _(sp):
            sp.dma_start(d["a_xn"], xn[:, :]).then_inc(spilled, 16)
            sp.wait_ge(x_spilled, 16)
            sp.dma_start(wq[:, :], d["a_wq"]).then_inc(w_loaded, 16)
            sp.dma_start(wv[:, :], d["a_wv"]).then_inc(w_loaded, 16)
            sp.wait_ge(cleared, 1)
            sp.dma_start(wo[0:LD, :, 0, :], d["a_wo"]).then_inc(w_loaded, 16)
            sp.dma_start(wo[LD:P, :, 1, :], d["a_wo"]).then_inc(w_loaded, 16)
            sp.wait_ge(ksum_kept, NCH)
            sp.dma_start(d["a_ks"], ksum[:, :]).then_inc(spilled, 16)
            sp.wait_ge(spilled, 32)

        @block.tensor
        def _(pe):
            pe.wait_ge(wk_loaded, 32)

            def fold_pairs(c, k):
                pe.wait_ge(k_added, c * PAIRS + PAIRS)
                if inside(c - 2, NCH):
                    pe.wait_ge(ksum_kept, c - 1)
                for u in range(2):
                    last = pe.matmul(banks[4 + k][:, :], fold[:, :], acc[k][u][:, :], start=(u == 0), stop=(u == 1))
                last.then_inc(fold_ready, 1)

            def step(c, k):
                for h in range(PAIRS):
                    if h >= 4 or inside(c - 1, NCH):
                        pe.wait_ge(k_added, c * PAIRS + h - 3)
                    pe.matmul(banks[h % 4][:, :], wk[:, h * P:(h + 1) * P], xn[:, bass.ds(c * CH, CH)],
                              start=True, stop=True).then_inc(k_ready, 1)
                    if h == 4 and inside(c - 1, NCH):
                        fold_pairs(c - 1, 1 - k)

            run_steps(pe, step, NCH, 2)
            fold_pairs(NCH - 1, 1)

        @block.vector
        def _(dve):
            def keep_sums(c, k):
                dve.wait_ge(fold_ready, c + 1)
                dve.tensor_copy(ksum[:, bass.ds(c * CH, CH)], banks[4 + k][:, :]).then_inc(ksum_kept, 1)

            def step(c, k):
                for h in range(PAIRS):
                    dve.wait_ge(k_ready, c * PAIRS + h + 1)
                    if h < 2:
                        if inside(c - 2, NCH):
                            dve.wait_ge(fold_ready, c - 1)
                        dve.tensor_scalar(acc[k][h][:, :], banks[h][:, :], 0.0, None, ALU.max).then_inc(k_added, 1)
                    else:
                        dve.wait_ge(k_added, c * PAIRS + h - 1)
                        dve.scalar_tensor_tensor(acc[k][h % 2][:, :], banks[h % 4][:, :], 0.0, acc[k][h % 2][:, :],
                                                 ALU.max, ALU.add).then_inc(k_added, 1)
                    if h == 8 and inside(c - 1, NCH):
                        keep_sums(c - 1, 1 - k)

            run_steps(dve, step, NCH, 2)
            keep_sums(NCH - 1, 1)


def linear_attention_tokens(core, ctx, wq, wv, wo, w_loaded):
    nc, sem, banks, d = core.nc, core.sem, core.banks, core.d

    def sb(name, shape):
        return ctx.enter_context(nc.sbuf_tensor(f"a_{name}_sb", shape, F32))

    q = sb("q", [P, LHALF, LH])
    v = sb("v", [P, LHALF, 2, LH + 1])
    xnc = [sb(f"xnc{k}", [P, LT]) for k in range(2)]
    xc = [sb(f"xc{k}", [P, LT]) for k in range(2)]
    ksc = [sb(f"ksc{k}", [P, LT]) for k in range(2)]
    norm = [sb(f"norm{k}", [P, 8]) for k in range(2)]
    rnorm = [sb(f"rnorm{k}", [P, 8]) for k in range(2)]
    out = q[:, :, :].rearrange("p (m a) j -> p m a j", a=2)

    HB = 4
    NB = LH // HB
    NG = LHALF // 8

    chunk_loaded = [sem(f"a_chunk_loaded{k}") for k in range(2)]
    zeros_set = sem("a_zeros_set")
    v_ready = sem("a_v_ready")
    v_kept = sem("a_v_kept")
    edge_kept = sem("a_edge_kept")
    q_ready = sem("a_q_ready")
    q_low = sem("a_q_low")
    q_high = sem("a_q_high")
    out_ready = sem("a_out_ready")
    norm_ready = sem("a_norm_ready")
    rnorm_ready = sem("a_rnorm_ready")
    out_kept = sem("a_out_kept")
    y_ready = sem("a_y_ready")
    y_added = sem("a_y_added")
    stored = [sem(f"a_stored{k}") for k in range(2)]
    reloaded = sem("a_x_reloaded")

    pair = [(banks[0], banks[1]), (banks[2], banks[3])]
    y_bank = [banks[4], banks[5]]
    v_bank = [banks[6], banks[7], banks[0], banks[1]]
    q_bank = [banks[6], banks[7], banks[2], banks[3]]
    block = ctx.enter_context(nc.Block())

    def wait_slot(eng, s, c, k, per):
        if isinstance(c, int):
            eng.wait_ge(s[k], per * (c // 2 + 1))
        else:
            eng.wait_ge(s[k], per * ((c - k) // 2) + per)

    @block.sync
    def _(sp):
        def load(c, k):
            sp.dma_start(xnc[k][:, :], d["a_xn"][:, bass.ds(c * LT, LT)]).then_inc(chunk_loaded[k], 16)
            sp.dma_start(xc[k][:, :], d["a_x"][:, bass.ds(c * LT, LT)]).then_inc(chunk_loaded[k], 16)
            sp.dma_start(ksc[k][:, :], d["a_ks"][:, bass.ds(c * LT, LT)]).then_inc(chunk_loaded[k], 16)

        def step(c, k):
            if inside(c + 1, NLC):
                if inside(c - 1, NLC):
                    wait_slot(sp, stored, c - 1, 1 - k, 16)
                load(c + 1, 1 - k)
            last = isinstance(c, int) and c == NLC - 1
            if last:
                sp.wait_ge(q_ready, NLC * NB)
                sp.wait_ge(stored[1 - k], 16 * (NLC // 2))
                sp.wait_ge(stored[k], 16 * (NLC // 2 - 1))
                sp.dma_start(core.xT[:, 0:c * LT], d["a_x2"][:, 0:c * LT]).then_inc(reloaded, 16)
            sp.wait_ge(y_added, c + 1)
            if last:
                sp.dma_start(core.xT[:, c * LT:TOK], xc[k][:, :]).then_inc(reloaded, 16)
            else:
                sp.dma_start(d["a_x2"][:, bass.ds(c * LT, LT)], xc[k][:, :]).then_inc(stored[k], 16)

        load(0, 0)
        run_steps(sp, step, NLC, 2)
        sp.wait_ge(reloaded, 32)

    @block.tensor
    def _(pe):
        pe.wait_ge(w_loaded, 64)

        def project(bank, w, g, k):
            for r in range(2):
                h = g * HB + 2 * r
                last = pe.matmul(bank[:, r * LT:(r + 1) * LT], w[:, h * LD:(h + 2) * LD], xnc[k][:, :],
                                 start=True, stop=True)
            return last

        def values(c, k, g):
            if g >= 4:
                pe.wait_ge(v_kept, c * NB + g - 3)
            elif g == 2 and inside(c - 1, NLC):
                pe.wait_ge(out_kept, c * NG - 1)
            project(v_bank[g % 4], wv, g, k).then_inc(v_ready, 1)

        def outputs(c, first, last_j, par):
            for j in range(first, last_j):
                last = pe.matmul(y_bank[par][:, 0:LHALF], wo[:, j, par, :], out[:, :, :, j],
                                 start=(j == 0), stop=(j == LH - 1))
            if last_j == LH:
                last.then_inc(y_ready, 1)

        def step(c, k):
            for g in range(NB):
                if g >= 4:
                    pe.wait_ge(q_low, c * NB + g - 3)
                    pe.wait_ge(q_high, c * NB + g - 3)
                elif g == 0:
                    pe.wait_ge(v_kept, c * NB + NB)
                project(q_bank[g % 4], wq, g, k).then_inc(q_ready, 1)
            if isinstance(c, int) and c == 0:
                pe.wait_ge(zeros_set, 2)
            pe.wait_ge(edge_kept, 2 * c + 2)
            pe.wait_ge(q_low, c * NB + NB)
            pe.wait_ge(q_high, c * NB + NB)
            for g in range(NG):
                if g >= 2:
                    pe.wait_ge(out_kept, c * NG + g - 1)
                for m in range(4):
                    for par in range(2):
                        n = 8 * g + 2 * m + par
                        bank = pair[g % 2][m // 2]
                        at = (m % 2) * 2 * (LH + 1)
                        last = pe.matmul(bank[par * LH:par * LH + LH, at:at + 2 * (LH + 1)],
                                         q[:, n, :], v[:, n, :, :].rearrange("p a j -> p (a j)"), start=True, stop=True)
                last.then_inc(out_ready, 1)
            more = inside(c + 1, NLC)
            if more:
                wait_slot(pe, chunk_loaded, c + 1, 1 - k, 48)
                for g in range(4):
                    values(c + 1, 1 - k, g)
            pe.wait_ge(out_kept, c * NG + NG)
            if inside(c - 1, NLC):
                pe.wait_ge(y_added, c)
            for part in range(16):
                per = 2 * LH // 16
                outputs(c, part % 8 * per, part % 8 * per + per, part // 8)
                if more and part < NB - 4:
                    values(c + 1, 1 - k, part + 4)

        wait_slot(pe, chunk_loaded, 0, 0, 48)
        for g in range(NB):
            values(0, 0, g)
        run_steps(pe, step, NLC, 2)

    @block.gpsimd
    def _(pool):
        for half in range(2):
            pool.memset(v[half * LD:half * LD + LD, :, 1 - half, :], 0.0).then_inc(zeros_set, 1)

    @block.scalar
    def _(act):
        def keep(c, k):
            wait_slot(act, chunk_loaded, c, k, 48)
            act.wait_ge(v_ready, c * NB + 1)
            for half in range(2):
                rows = slice(half * LD, half * LD + LD)
                act.copy(v[rows, :, half, LH], ksc[k][rows, half * LHALF:(half + 1) * LHALF]).then_inc(edge_kept, 1)
            for g in range(NB):
                act.wait_ge(q_ready, c * NB + g + 1)
                for half in range(2):
                    ins = act.activation(q[half * LD:half * LD + LD, :, g * HB:(g + 1) * HB:2].rearrange("p n r -> p r n"),
                                         q_bank[g % 4][0:LD, :].rearrange("p (r a n) -> p r a n", r=2, a=2)[:, :, half, :],
                                         ACT.Relu)
                ins.then_inc(q_low, 1)

        run_steps(act, keep, NLC, 2)

    @block.vector
    def _(dve):
        def keep_values(c, k):
            wait_slot(dve, chunk_loaded, c, k, 48)
            for g in range(NB):
                dve.wait_ge(v_ready, c * NB + g + 1)
                for head in range(2):
                    for half in range(2):
                        rows = slice(half * LD, half * LD + LD)
                        dest = v[rows, :, half, g * HB + head:(g + 1) * HB:2].rearrange("p n r -> p r n")
                        src = v_bank[g % 4][head * LD:head * LD + LD, :].rearrange("p (r a n) -> p r a n", r=2, a=2)
                        ks = ksc[k][head * LD:head * LD + LD, half * LHALF:(half + 1) * LHALF]
                        ins = dve.tensor_tensor(dest, src[:, :, half, :],
                                                ks.unsqueeze(1).to_broadcast([LD, 2, LHALF]), ALU.mult)
                ins.then_inc(v_kept, 1)

        def step(c, k):
            for g in range(NB):
                dve.wait_ge(q_ready, c * NB + g + 1)
                for half in range(2):
                    ins = dve.tensor_scalar(q[half * LD:half * LD + LD, :, g * HB + 1:(g + 1) * HB:2].rearrange("p n r -> p r n"),
                                            q_bank[g % 4][LD:P, :].rearrange("p (r a n) -> p r a n", r=2, a=2)[:, :, half, :],
                                            0.0, None, ALU.max)
                ins.then_inc(q_high, 1)
            for g in range(NG):
                w = g % 2
                b0 = pair_view(w)
                dve.wait_ge(out_ready, c * NG + g + 1)
                dve.tensor_scalar(norm[w][:, :].rearrange("p (b m) -> p b m", b=2), b0[:, :, :, LH], 1e-6, None,
                                  ALU.add).then_inc(norm_ready, 1)
                dve.wait_ge(norm_ready, c * NG + g + 1)
                dve.reciprocal(rnorm[w][:, :], norm[w][:, :]).then_inc(rnorm_ready, 1)
                dve.wait_ge(rnorm_ready, c * NG + g + 1)
                dve.tensor_tensor(
                    out[:, 4 * g:4 * g + 4, :, :].rearrange("p (b m) a j -> p b (m a) j", b=2),
                    b0[:, :, :, 0:LH],
                    rnorm[w][:, :].rearrange("p (b m) -> p b m", b=2).unsqueeze(3).to_broadcast([P, 2, 4, LH]),
                    ALU.mult).then_inc(out_kept, 1)
            if inside(c + 1, NLC):
                keep_values(c + 1, 1 - k)
            for par in range(2):
                dve.wait_ge(y_ready, 2 * c + par + 1)
                x = xc[k][:, :].rearrange("p (a m o) -> p m a o", a=2, o=2)[:, :, :, par]
                ins = dve.scalar_tensor_tensor(x, y_bank[par][:, 0:LHALF].rearrange("p (m a) -> p m a", a=2),
                                               core.vec("a_bo"), x, ALU.add, ALU.add)
            ins.then_inc(y_added, 1)

        def pair_view(w):
            both = core.all_banks[:, 2 * w:2 * w + 2, 0:4 * (LH + 1)]
            return both.rearrange("p b (m j) -> p b m j", j=LH + 1)

        keep_values(0, 0)
        run_steps(dve, step, NLC, 2)


def experts(core):
    nc, sem, banks, xT, ident, d = core.nc, core.sem, core.banks, core.xT, core.ident, core.d
    TC = CH // P
    NT = TOK // P
    with ExitStack() as ctx:
        def sb(name, shape):
            return ctx.enter_context(nc.sbuf_tensor(f"e_{name}_sb", shape, F32))

        xn = sb("xn", [P, TOK])
        w = sb("w", [P, E, D])
        gate = sb("gate", [P, E])
        gate_b = sb("gate_b", [E, 1])
        bias = sb("bias", [E, D])
        weight = sb("weight", [P, NT, E])

        loaded = sem("e_loaded")

        def load_weights(sp):
            sp.dma_start(w[:, :, :], d["e_w"]).then_inc(loaded, 16)
            sp.dma_start(gate[:, :], d["e_gate"]).then_inc(loaded, 16)
            sp.dma_start(gate_b[:, :], d["e_gate_b"]).then_inc(loaded, 16)
            sp.dma_start(bias[:, :], d["e_bias"]).then_inc(loaded, 16)
            sp.wait_ge(loaded, 64)

        layer_norm(core, "e_ln", xT, xn, 1e-5, beside=load_weights)
        expert_weights(core, xn, gate, gate_b, weight)

        tile = [sb(f"tile{k}", [P, CH]) for k in range(2)]
        share = [sb(f"share{k}", [P, TC, E]) for k in range(2)]
        shareT = sb("shareT", [E, CH])
        acc = [[sb(f"acc{j}{t}", [P, D]) for t in range(2)] for j in range(2)]

        tile_ready = sem("e_tile_ready")
        share_ready = sem("e_share_ready")
        share_turned = sem("e_share_turned")
        shareT_ready = sem("e_shareT_ready")
        mm_ready = sem("e_mm_ready")
        mm_used = sem("e_mm_used")
        acc_step = [sem(f"e_acc_step{t}") for t in range(2)]
        pair_turned = sem("e_pair_turned")
        y_added = sem("e_y_added")
        block = ctx.enter_context(nc.Block())

        @block.gpsimd
        def _(pool):
            def step(c, k):
                if inside(c - 2, NCH):
                    pool.wait_ge(mm_used, 4 * (c - 1))
                    pool.wait_ge(share_turned, c - 1)
                pool.tensor_copy(share[k][:, :, :], weight[:, bass.ds(c * TC, TC), :]).then_inc(share_ready, 1)

            run_steps(pool, step, NCH, 2)

        @block.scalar
        def _(act):
            def copy_tile(c, k):
                if inside(c - 2, NCH):
                    act.wait_ge(mm_ready, 4 * (c - 1))
                act.copy(tile[k][:, :], xn[:, bass.ds(c * CH, CH)]).then_inc(tile_ready, 1)

            def step(c, k):
                act.wait_ge(share_turned, c + 1)
                if inside(c - 1, NCH):
                    act.wait_ge(pair_turned, 2 * c)
                act.copy(shareT[:, :], banks[6][0:E, :]).then_inc(shareT_ready, 1)
                if inside(c + 1, NCH):
                    copy_tile(c + 1, 1 - k)

            copy_tile(0, 0)
            run_steps(act, step, NCH, 2)

        @block.tensor
        def _(pe):
            def products(c, k, s):
                j, h = s // 2, s % 2
                if s == 0:
                    pe.wait_ge(tile_ready, c + 1)
                if s >= 2 or inside(c - 1, NCH):
                    pe.wait_ge(mm_used, 4 * c + s - 1)
                for t in range(2):
                    at = (2 * j + t) * P
                    last = pe.matmul(banks[2 * h + t][:, :], tile[k][:, at:at + P],
                                     w[:, 4 * h:4 * h + 4, :].rearrange("p e c -> p (e c)"), start=True, stop=True)
                last.then_inc(mm_ready, 1)

            def turn_pair(c, k, j):
                for t in range(2):
                    pe.wait_ge(acc_step[t], (2 * c + j + 1) * E)
                for t in range(2):
                    at = (2 * j + t) * P
                    last = pe.matmul(banks[4 + k][:, at:at + P], acc[j][t][:, :], ident[:, :], start=False,
                                     stop=(j == 1 and t == 1))
                last.then_inc(pair_turned, 1)

            def step(c, k):
                products(c, k, 0)
                pe.wait_ge(share_ready, c + 1)
                if inside(c - 1, NCH):
                    turn_pair(c - 1, 1 - k, 1)
                    pe.wait_ge(shareT_ready, c)
                for t in range(TC):
                    last = pe.transpose(banks[6][0:E, t * P:(t + 1) * P], share[k][:, t, :], ident[:, :])
                last.then_inc(share_turned, 1)
                products(c, k, 1)
                products(c, k, 2)
                pe.wait_ge(shareT_ready, c + 1)
                if inside(c - 2, NCH):
                    pe.wait_ge(y_added, c - 1)
                pe.matmul(banks[4 + k][:, :], bias[:, :], shareT[:, :], start=True, stop=False)
                turn_pair(c, k, 0)
                products(c, k, 3)

            run_steps(pe, step, NCH, 2)
            turn_pair(NCH - 1, 1, 1)

        @block.vector
        def _(dve):
            def add_y(c, k):
                dve.wait_ge(pair_turned, 2 * c + 2)
                x = xT[:, bass.ds(c * CH, CH)]
                dve.tensor_tensor(x, x, banks[4 + k][:, :], ALU.add).then_inc(y_added, 1)

            def step(c, k):
                dve.wait_ge(share_ready, c + 1)
                for s in range(4):
                    j, h = s // 2, s % 2
                    dve.wait_ge(mm_ready, 4 * c + s + 1)
                    if h == 0 and inside(c - 1, NCH):
                        dve.wait_ge(pair_turned, 2 * c - 1 + j)
                    for e in range(4 * h, 4 * h + 4):
                        for t in range(2):
                            done = (2 * c + j) * E + e
                            part = banks[2 * h + t][:, (e % 4) * D:(e % 4 + 1) * D]
                            share_e = share[k][:, 2 * j + t, e:e + 1]
                            if e == 0:
                                last = dve.tensor_scalar(acc[j][t][:, :], part, share_e, None, ALU.mult)
                            else:
                                dve.wait_ge(acc_step[t], done)
                                last = dve.scalar_tensor_tensor(acc[j][t][:, :], part, share_e, acc[j][t][:, :],
                                                                ALU.mult, ALU.add)
                            last.then_inc(acc_step[t], 1)
                    for t in range(2):
                        dve.wait_ge(acc_step[t], (2 * c + j) * E + 4 * h + 4)
                    dve.nop().then_inc(mm_used, 1)
                    if s == 1 and inside(c - 1, NCH):
                        add_y(c - 1, 1 - k)

            run_steps(dve, step, NCH, 2)
            add_y(NCH - 1, 1)


def expert_weights(core, xn, gate, gate_b, weight):
    nc, sem, banks, ident = core.nc, core.sem, core.banks, core.ident
    TC = CH // P
    NT = TOK // P
    with ExitStack() as ctx:
        def sb(name, shape):
            return ctx.enter_context(nc.sbuf_tensor(f"g_{name}_sb", shape, F32))

        logitT = [sb(f"logitT{k}", [E, CH]) for k in range(2)]
        logit = sb("logit", [P, NT, E])
        big = sb("big", [P, NT])
        ex = sb("ex", [P, NT, E])
        total = sb("total", [P, NT])
        rtotal = sb("rtotal", [P, NT])
        kept = sb("kept", [P, NT, E])
        ksum = sb("ksum", [P, NT])
        guard = sb("guard", [P, NT])
        rksum = sb("rksum", [P, NT])

        gate_ready = sem("g_gate_ready")
        logitT_ready = sem("g_logitT_ready")
        logit_turned = sem("g_logit_turned")
        logit_kept = sem("g_logit_kept")
        small = sem("g_small")
        exp_ready = sem("g_exp_ready")
        block = ctx.enter_context(nc.Block())

        @block.tensor
        def _(pe):
            def gates(c, k):
                pe.matmul(banks[k][0:E, :], gate[:, :], xn[:, bass.ds(c * CH, CH)], start=True, stop=True).then_inc(gate_ready, 1)

            def step(c, k):
                if inside(c - 2, NCH):
                    pe.wait_ge(logit_kept, c - 1)
                pe.wait_ge(logitT_ready, c + 1)
                if inside(c + 1, NCH):
                    gates(c + 1, 1 - k)
                for t in range(TC):
                    last = pe.transpose(banks[2 + k][:, t * E:(t + 1) * E], logitT[k][:, t * P:(t + 1) * P],
                                        ident[0:E, 0:E])
                last.then_inc(logit_turned, 1)

            gates(0, 0)
            run_steps(pe, step, NCH, 2)

        @block.scalar
        def _(act):
            def step(c, k):
                act.wait_ge(gate_ready, c + 1)
                if inside(c - 2, NCH):
                    act.wait_ge(logit_turned, c - 1)
                act.activation(logitT[k][:, :], banks[k][0:E, :], ACT.Identity, bias=gate_b[:, 0:1]).then_inc(logitT_ready, 1)

            run_steps(act, step, NCH, 2)
            act.wait_ge(small, 2)
            act.activation(ex[:, :, :], logit[:, :, :], ACT.Exp).then_inc(exp_ready, 1)

        @block.vector
        def _(dve):
            def step(c, k):
                dve.wait_ge(logit_turned, c + 1)
                dve.tensor_copy(logit[:, bass.ds(c * TC, TC), :],
                                banks[2 + k][:, 0:TC * E].rearrange("p (t e) -> p t e", e=E)).then_inc(logit_kept, 1)

            run_steps(dve, step, NCH, 2)
            dve.wait_ge(logit_kept, NCH)
            count = [0]

            def after(ins):
                count[0] += 1
                ins.then_inc(small, 1)
                dve.wait_ge(small, count[0])

            def wide(t):
                return t[:, :].unsqueeze(2).to_broadcast([P, NT, E])

            after(dve.tensor_reduce(big[:, :], logit[:, :, :], AX, ALU.max))
            after(dve.tensor_tensor(logit[:, :, :], logit[:, :, :], wide(big), ALU.subtract))
            dve.wait_ge(exp_ready, 1)
            after(dve.tensor_reduce(total[:, :], ex[:, :, :], AX, ALU.add))
            after(dve.reciprocal(rtotal[:, :], total[:, :]))
            after(dve.tensor_tensor(ex[:, :, :], ex[:, :, :], wide(rtotal), ALU.mult))
            after(dve.scalar_tensor_tensor(kept[:, :, :], ex[:, :, :], 0.1, ex[:, :, :], ALU.is_ge, ALU.mult))
            after(dve.tensor_reduce(ksum[:, :], kept[:, :, :], AX, ALU.add))
            after(dve.scalar_tensor_tensor(guard[:, :], ksum[:, :], 0.0, ksum[:, :], ALU.is_equal, ALU.add))
            after(dve.reciprocal(rksum[:, :], guard[:, :]))
            after(dve.tensor_tensor(weight[:, :, :], kept[:, :, :], wide(rksum), ALU.mult))


def slot_attention(core):
    nc, sem, banks, xT, d = core.nc, core.sem, core.banks, core.xT, core.d
    with ExitStack() as ctx:
        def sb(name, shape):
            return ctx.enter_context(nc.sbuf_tensor(f"s_{name}_sb", shape, F32))

        slots = sb("slots", [P, TOK])
        qk_w = sb("qk_w", [P, D])
        in_w = sb("in_w", [P, 3, D])
        hh_w = sb("hh_w", [P, 3, D])
        key_scale = sb("key_scale", [P, 1])
        half_b = sb("half_b", [P, 3])
        sum_b = sb("sum_b", [P, 2])

        w_loaded = sem("s_w_loaded")
        w_prod = sem("s_w_prod")
        sum_ready = sem("s_sum_ready")
        with ExitStack() as wctx:
            wq, wk, wv = [wctx.enter_context(nc.sbuf_tensor(f"s_w{n}_sb", [P, D], F32)) for n in "qkv"]
            ih = wctx.enter_context(nc.sbuf_tensor("s_ih_sb", [P, 3, D], F32))

            def load_weights(sp):
                for t, n in ((wq, "s_wq"), (wk, "s_wk"), (wv, "s_wv")):
                    sp.dma_start(t[:, :], d[n]).then_inc(w_loaded, 16)
                sp.dma_start(ih[:, :, :], d["s_ihT"]).then_inc(w_loaded, 16)
                sp.dma_start(hh_w[:, :, :], d["s_hhT"]).then_inc(w_loaded, 16)
                sp.wait_ge(w_loaded, 80)

            layer_norm(core, "s_ln", xT, slots, 1e-5, beside=load_weights)
            block = wctx.enter_context(nc.Block())

            @block.tensor
            def _(pe):
                pe.wait_ge(w_loaded, 80)
                pe.matmul(banks[0][:, 0:D], wq[:, :], wk[:, :], start=True, stop=True)
                pe.matmul(banks[1][:, 0:3 * D], wv[:, :], ih[:, :, :].rearrange("p g c -> p (g c)"),
                          start=True, stop=True).then_inc(w_prod, 1)

            @block.vector
            def _(dve):
                for g, n in enumerate("rz"):
                    ins = dve.tensor_tensor(sum_b[:, g:g + 1], core.vec(f"bih_{n}"), core.vec(f"bhh_{n}"), ALU.add)
                ins.then_inc(sum_ready, 1)
                dve.tensor_scalar(key_scale[:, :], core.vec("input_w"), float(D) ** -0.5, None, ALU.mult)
                dve.wait_ge(sum_ready, 1)
                dve.tensor_scalar(half_b[:, 0:2], sum_b[:, :], 0.5, None, ALU.mult)
                dve.tensor_scalar(half_b[:, 2:3], core.vec("bhh_n"), 0.5, None, ALU.mult)
                dve.wait_ge(w_prod, 1)
                dve.tensor_scalar(qk_w[:, :], banks[0][:, 0:D], core.vec("slot_w"), None, ALU.mult)
                dve.tensor_scalar(in_w[:, :, :], banks[1][:, 0:3 * D].rearrange("p (g c) -> p g c", g=3),
                                  core.vec("input_w"), None, ALU.mult)

        with ExitStack() as rctx:
            slot_rounds(core, rctx, slots, qk_w, in_w, hh_w, key_scale, half_b)
        x_added = sem("s_x_added")
        with nc.Block() as block:
            @block.vector
            def _(dve):
                dve.tensor_tensor(xT[:, :], xT[:, :], slots[:, :], ALU.add).then_inc(x_added, 1)


def slot_rounds(core, ctx, slots, qk_w, in_w, hh_w, key_scale, half_b):
    nc, sem, banks, ident, d = core.nc, core.sem, core.banks, core.ident, core.d
    GB = BPC
    HS = CH // 2
    UG = 2 * ITERS
    UN = NCH * UG
    R = 4
    SC = 3 * ST

    def sb(name, shape):
        return ctx.enter_context(nc.sbuf_tensor(f"s_{name}_sb", shape, F32))

    raw = [sb(f"raw{k}", [ST, 3, D]) for k in range(R)]
    junk = sb("junk", [ST, 3, D])
    sumsq = [sb(f"sumsq{k}", [ST, 3]) for k in range(R)]
    shifted = sb("shifted", [ST, 3])
    krstd = [sb(f"krstd{k}", [ST, 3]) for k in range(R)]
    minus_half = sb("minus_half", [P, 4])
    eps_sum = sb("eps_sum", [ST, 3])
    keys = [sb(f"keys{p}", [ST, GB, 3, D + 1]) for p in range(2)]
    keysT = [sb(f"keysT{p}", [P, GB, SC]) for p in range(2)]
    sq = sb("sq", [P, HS])
    mean_sq = sb("mean_sq", [P, 2])
    srstd = sb("srstd", [P, 2])
    query = sb("query", [P, HS])
    score = [sb(f"score{q}", [P, SC]) for q in range(2)]
    big = [sb(f"big{q}", [ST, 12]) for q in range(2)]
    less = [sb(f"less{q}", [ST, 12, S]) for q in range(2)]
    total = [sb(f"total{q}", [ST, 12]) for q in range(2)]
    rtotal = [sb(f"rtotal{q}", [ST, 12]) for q in range(2)]
    attn = [sb(f"attn{q}", [ST, 12, S]) for q in range(2)]
    mass = sb("mass", [P, 2])
    rmass = sb("rmass", [P, 2])
    update = sb("update", [P, 2, D])
    updT = sb("updT", [P, HS])
    half_hn = sb("half_hn", [P, HS])
    tanh_r = sb("tanh_r", [P, HS])
    tanh_z = sb("tanh_z", [P, HS])
    cand_in = sb("cand_in", [P, HS])
    cand = sb("cand", [P, HS])
    new_share = sb("new_share", [P, HS])
    old_twice = sb("old_twice", [P, HS])

    cleared = sem("s_cleared")
    raw_loaded = [sem(f"s_raw_loaded{k}") for k in range(R)]
    sumsq_ready = sem("s_sumsq_ready")
    shifted_ready = sem("s_shifted_ready")
    krstd_ready = sem("s_krstd_ready")
    keys_ready = sem("s_keys_ready")
    keys_turned = sem("s_keys_turned")
    keysT_ready = sem("s_keysT_ready")
    sq_ready = sem("s_sq_ready")
    msq_ready = sem("s_msq_ready")
    mean_kept = sem("s_mean_kept")
    srstd_ready = sem("s_srstd_ready")
    query_ready = sem("s_query_ready")
    query_kept = sem("s_query_kept")
    score_ready = sem("s_score_ready")
    score_kept = sem("s_score_kept")
    score_turned = sem("s_score_turned")
    big_ready = sem("s_big_ready")
    less_ready = sem("s_less_ready")
    exp_ready = sem("s_exp_ready")
    total_ready = sem("s_total_ready")
    rtotal_ready = sem("s_rtotal_ready")
    attn_ready = sem("s_attn_ready")
    mix_ready = sem("s_mix_ready")
    mass_ready = sem("s_mass_ready")
    rmass_ready = sem("s_rmass_ready")
    update_ready = sem("s_update_ready")
    update_turned = sem("s_update_turned")
    updT_ready = sem("s_updT_ready")
    hn_ready = sem("s_hn_ready")
    hn_kept = sem("s_hn_kept")
    r_ready = sem("s_r_ready")
    z_ready = sem("s_z_ready")
    xn_ready = sem("s_xn_ready")
    tanh_r_ready = sem("s_tanh_r_ready")
    tanh_z_ready = sem("s_tanh_z_ready")
    reset_done = sem("s_reset_done")
    cand_in_ready = sem("s_cand_in_ready")
    cand_ready = sem("s_cand_ready")
    share_ready = sem("s_share_ready")
    new_ready = sem("s_new_ready")
    slots_ready = sem("s_slots_ready")

    r_bank, z_bank = banks[0][:, 0:HS], banks[1][:, 0:HS]
    hn_bank, xn_bank = banks[0][:, HS:], banks[7][:, HS:]
    turned_bank = [banks[5], banks[2]]
    key_bank, query_bank, score_bank = banks[3], banks[1][:, HS:], banks[4]
    mix_bank = [banks[6][:, 0:D + 1], banks[6][:, HS:HS + D + 1]]
    both_mixes = banks[6][:, :].rearrange("p (q c) -> p q c", q=2)
    update_bank, msq_bank = banks[7][:, 0:HS], banks[3][:, 3 * P:3 * P + 2]

    def at(g, i):
        return g * CH + {-1: -HS, UG: CH, UG + 1: CH + HS}.get(i, i % 2 * HS)

    def coming(g, i):
        if i == UG:
            g, i = g + 1, 0
        if not inside(g + 1, NCH):
            return []
        return [((g + 1) * GB + b, b) for b in range(i * GB // UG, (i + 1) * GB // UG)]

    def run_units(eng, unit):
        def step(g, p):
            for i in range(UG):
                unit(g * UG + i, g, i, p)

        run_steps(eng, step, NCH, 2)
        unit(UN, NCH, 0, 0)

    def landed(eng, n, k):
        if isinstance(n, int):
            eng.wait_ge(raw_loaded[k], 32 * (n // R + 1))
        else:
            eng.wait_ge(raw_loaded[k], 32 * ((n - k) // R) + 32)

    block = ctx.enter_context(nc.Block())

    @block.sync
    def _(sp):
        sp.wait_ge(cleared, 1)

        def load(n, k):
            ctx_n = d["ctx"][bass.ds(n, 1), :, :]
            sp.dma_start(raw[k][:, 0:2, :],
                         ctx_n[:, 0:2 * ST, :].rearrange("b (t p) d -> p (b t) d", p=ST)).then_inc(raw_loaded[k], 16)
            sp.dma_start(raw[k][0:SK[2], 2, :],
                         ctx_n[:, 2 * ST:M, :].rearrange("b p d -> (b p) d")).then_inc(raw_loaded[k], 16)

        for k in range(R):
            load(k, k)
        with sp.Fori(0, B - 2 * R + 1, R) as base:
            for k in range(R):
                sp.wait_ge(keys_ready, base + k + 1)
                load(base + k + R, k)

    @block.gpsimd
    def _(pool):
        def key_norm(n, k):
            pool.wait_ge(krstd_ready, n)
            pool.wait_ge(sumsq_ready, n + 1)
            pool.tensor_tensor(shifted[:, :], sumsq[k % R][:, :], eps_sum[:, :], ALU.add).then_inc(shifted_ready, 1)
            pool.wait_ge(shifted_ready, n + 1)
            if inside(n - R, B):
                pool.wait_ge(keys_ready, n - R + 1)
            pool.tensor_tensor(krstd[k % R][:, :], shifted[:, :], minus_half[0:ST, 0:3], ALU.pow).then_inc(krstd_ready, 1)

        def unit(u, g, i, p):
            if inside(u, UN):
                pool.wait_ge(mean_kept, u + 1)
                if inside(u - 1, UN):
                    pool.wait_ge(score_kept, 2 * u)
                pool.tensor_tensor(srstd[:, :], mean_sq[:, :], minus_half[:, 0:2], ALU.pow).then_inc(srstd_ready, 1)
                for n, b in coming(g, i)[-1:] + coming(g, i + 1)[:-1]:
                    key_norm(n, b)

        pool.wait_ge(cleared, 1)
        for b in range(GB):
            key_norm(b, b)
        for n, b in coming(0, 0)[:-1]:
            key_norm(n, b)
        run_units(pool, unit)

    @block.tensor
    def _(pe):
        def turn_keys(n, p, b):
            pe.wait_ge(keys_ready, n + 1)
            if inside(n - 1, B):
                pe.wait_ge(keysT_ready, n)
            for t in range(3):
                last = pe.transpose(key_bank[:, t * ST:(t + 1) * ST], keys[p][:, b, t, 0:D], ident[0:ST, 0:ST])
            last.then_inc(keys_turned, 1)

        def scores(u, i, p, q):
            if q == 1 or inside(u - 1, UN):
                pe.wait_ge(score_kept, 2 * u + q)
            for j in range(4):
                b = i % 2 * 8 + 4 * q + j
                last = pe.matmul(score_bank[j * S:(j + 1) * S, 0:SC], query[:, (4 * q + j) * S:(4 * q + j + 1) * S],
                                 keysT[p][:, b, :], start=True, stop=True)
            last.then_inc(score_ready, 1)

        def turn_scores(u, q):
            pe.wait_ge(score_kept, 2 * u + q + 1)
            for t in range(3):
                last = pe.transpose(turned_bank[q][0:ST, t * P:(t + 1) * P], score[q][:, t * ST:(t + 1) * ST],
                                    ident[:, :])
            last.then_inc(score_turned, 1)

        def mix(u, i, p, q):
            pe.wait_ge(attn_ready, 2 * u + q + 1)
            if q == 0 and inside(u - 1, UN):
                pe.wait_ge(update_ready, u)
            for t in range(3):
                for j in range(4):
                    last = pe.matmul(mix_bank[q][j * S:(j + 1) * S, 0:D + 1], attn[q][0:SK[t], t * 4 + j, :],
                                     keys[p][0:SK[t], i % 2 * 8 + 4 * q + j, t, :], start=(t == 0), stop=(t == 2))
            last.then_inc(mix_ready, 1)

        def turn_update(u):
            pe.wait_ge(update_ready, u + 1)
            for q in range(2):
                last = pe.transpose(update_bank[:, q * P:(q + 1) * P], update[:, q, :], ident[:, :])
            last.then_inc(update_turned, 1)

        def transform_slots(u, g, i, turned):
            if inside(u - 2, UN):
                pe.wait_ge(slots_ready, u - 1)
            pe.matmul(query_bank, qk_w[:, :], slots[:, bass.ds(at(g, i), HS)], start=True, stop=True).then_inc(query_ready, 1)
            pe.wait_ge(sq_ready, u + 1)
            pe.wait_ge(keysT_ready, turned)
            for q in range(2):
                last = pe.matmul(msq_bank[:, q:q + 1], sq[:, q * P:(q + 1) * P], core.mean_mat[:, 0:1],
                                 start=True, stop=True)
            last.then_inc(msq_ready, 1)

        def unit(u, g, i, p):
            news = coming(g, i) if inside(u, UN) else []
            if inside(u, UN):
                if i == 0:
                    pe.wait_ge(keysT_ready, g * GB + GB)
                pe.wait_ge(query_kept, u + 1)
                scores(u, i, p, 0)
            if inside(u - 1, UN):
                if inside(u - 2, UN):
                    pe.wait_ge(cand_in_ready, u - 1)
                turn_update(u - 1)
            if inside(u, UN):
                turn_scores(u, 0)
                scores(u, i, p, 1)
            if inside(u - 1, UN):
                pe.wait_ge(updT_ready, u)
                pe.matmul(r_bank, in_w[:, 0, :], updT[:, :], start=False, stop=True).then_inc(r_ready, 1)
            if inside(u, UN):
                turn_scores(u, 1)
                pe.wait_ge(mean_kept, u + 1)
                for n, b in news[:1]:
                    turn_keys(n, 1 - p, b)
            if inside(u - 1, UN):
                pe.matmul(z_bank, hh_w[:, 1, :], slots[:, bass.ds(at(g, i - 1), HS)], start=True, stop=False)
                pe.matmul(z_bank, in_w[:, 1, :], updT[:, :], start=False, stop=True).then_inc(z_ready, 1)
                pe.matmul(xn_bank, in_w[:, 2, :], updT[:, :], start=True, stop=True).then_inc(xn_ready, 1)
            if inside(u, UN):
                for n, b in news[1:2]:
                    turn_keys(n, 1 - p, b)
                mix(u, i, p, 0)
                sl = slots[:, bass.ds(at(g, i), HS)]
                if inside(u - 1, UN):
                    pe.wait_ge(tanh_r_ready, u)
                pe.matmul(hn_bank, hh_w[:, 2, :], sl, start=True, stop=True).then_inc(hn_ready, 1)
                for n, b in news[2:]:
                    turn_keys(n, 1 - p, b)
                pe.wait_ge(hn_kept, u + 1)
                pe.matmul(r_bank, hh_w[:, 0, :], sl, start=True, stop=False)
                mix(u, i, p, 1)
                if inside(u + 1, UN):
                    transform_slots(u + 1, g, i + 1, news[-1][0] + 1 if news else B)

        for b in range(GB):
            turn_keys(b, 0, b)
        transform_slots(0, 0, 0, GB)
        run_units(pe, unit)

    @block.scalar
    def _(act):
        def squares(n, k):
            landed(act, n, k % R)
            for t in range(3):
                last = act.activation(junk[:, t, :], raw[k % R][:, t, :], ACT.Square,
                                      accum_out=sumsq[k % R][:, t:t + 1])
            last.then_inc(sumsq_ready, 1)
            act.wait_ge(sumsq_ready, n + 1)

        def keep_keysT(n, p, b):
            act.wait_ge(keys_turned, n + 1)
            act.copy(keysT[p][:, b, :], key_bank[:, 0:SC]).then_inc(keysT_ready, 1)

        def keep_scores(u, q):
            act.wait_ge(score_ready, 2 * u + q + 1)
            act.activation(score[q][:, :], score_bank[:, 0:SC], ACT.Copy, scale=srstd[:, q:q + 1]).then_inc(score_kept, 1)

        def exponentials(u, q):
            act.wait_ge(less_ready, 2 * u + q + 1)
            act.activation(less[q][:, :, :], less[q][:, :, :], ACT.Exp).then_inc(exp_ready, 1)

        def keep_query(u):
            act.wait_ge(query_ready, u + 1)
            act.activation(query[:, :], query_bank, ACT.Copy, scale=key_scale[:, 0:1]).then_inc(query_kept, 1)

        def unit(u, g, i, p):
            news = coming(g, i) if inside(u, UN) else []
            if inside(u, UN):
                act.wait_ge(srstd_ready, u + 1)
                keep_scores(u, 0)
            if inside(u - 1, UN):
                act.wait_ge(update_turned, u)
                act.copy(updT[:, :], update_bank).then_inc(updT_ready, 1)
            if inside(u, UN):
                keep_scores(u, 1)
                exponentials(u, 0)
            for n, b in news[:1]:
                keep_keysT(n, 1 - p, b)
            if inside(u - 1, UN):
                act.wait_ge(r_ready, u)
                act.activation(tanh_r[:, :], r_bank, ACT.Tanh, scale=0.5, bias=half_b[:, 0:1]).then_inc(tanh_r_ready, 1)
            if inside(u, UN):
                exponentials(u, 1)
            if inside(u - 1, UN):
                act.wait_ge(z_ready, u)
                act.activation(tanh_z[:, :], z_bank, ACT.Tanh, scale=0.5, bias=half_b[:, 1:2]).then_inc(tanh_z_ready, 1)
            for n, b in news[1:2]:
                keep_keysT(n, 1 - p, b)
            if inside(u - 1, UN):
                act.wait_ge(cand_in_ready, u)
                act.activation(cand[:, :], cand_in[:, :], ACT.Tanh, bias=core.vec("bih_n")).then_inc(cand_ready, 1)
            if inside(u, UN):
                act.wait_ge(hn_ready, u + 1)
                if inside(u - 1, UN):
                    act.wait_ge(reset_done, u)
                act.activation(half_hn[:, :], hn_bank, ACT.Identity, scale=0.5, bias=half_b[:, 2:3]).then_inc(hn_kept, 1)
            for n, b in news[2:]:
                keep_keysT(n, 1 - p, b)
            if inside(u, UN):
                for n, b in coming(g, i + 1)[:-1]:
                    squares(n, b)
            if inside(u + 1, UN):
                keep_query(u + 1)
            if inside(u, UN):
                for n, b in coming(g, i + 1)[-1:]:
                    squares(n, b)

        for b in range(GB):
            squares(b, b)
            if b >= 2:
                keep_keysT(b - 2, 0, b - 2)
        for b in range(GB - 2, GB):
            keep_keysT(b, 0, b)
        for n, b in coming(0, 0):
            squares(n, b)
        keep_query(0)
        run_units(act, unit)

    @block.vector
    def _(dve):
        dve.memset(minus_half[:, :], -0.5)
        dve.memset(eps_sum[:, :], 1e-6 * D)
        for p in range(2):
            dve.memset(keys[p][:, :, :, D:D + 1], 1.0)
        for k in range(R):
            ins = dve.memset(raw[k][:, 2, :], 0.0)
        ins.then_inc(cleared, 1)

        def scale_keys(n, p, b):
            dve.wait_ge(krstd_ready, n + 1)
            for t in range(3):
                last = dve.tensor_scalar(keys[p][:, b, t, 0:D], raw[b % R][:, t, :], krstd[b % R][:, t:t + 1],
                                         float(D) ** 0.5, ALU.mult, ALU.mult)
            last.then_inc(keys_ready, 1)

        def take_update(u):
            dve.wait_ge(mix_ready, 2 * u + 2)
            dve.tensor_scalar(mass[:, :], both_mixes[:, :, D], 1e-6, None, ALU.add).then_inc(mass_ready, 1)
            dve.wait_ge(mass_ready, u + 1)
            dve.reciprocal(rmass[:, :], mass[:, :]).then_inc(rmass_ready, 1)
            dve.wait_ge(rmass_ready, u + 1)
            dve.tensor_tensor(update[:, :, :], both_mixes[:, :, 0:D], rmass[:, :].unsqueeze(2).to_broadcast([P, 2, D]),
                              ALU.mult).then_inc(update_ready, 1)

        def below_max(u, q):
            turned = turned_bank[q][0:ST, 0:3 * P].rearrange("p (g k) -> p g k", k=S)
            dve.wait_ge(score_turned, 2 * u + q + 1)
            dve.tensor_reduce(big[q][:, :], turned, AX, ALU.max).then_inc(big_ready, 1)
            dve.wait_ge(big_ready, 2 * u + q + 1)
            dve.tensor_tensor(less[q][:, :, :], turned, big[q][:, :].unsqueeze(2).to_broadcast([ST, 12, S]),
                              ALU.subtract).then_inc(less_ready, 1)

        def softmax_sum(u, q):
            n = 2 * u + q + 1
            dve.wait_ge(exp_ready, n)
            dve.tensor_reduce(total[q][:, :], less[q][:, :, :], AX, ALU.add).then_inc(total_ready, 1)
            dve.wait_ge(total_ready, n)
            dve.reciprocal(rtotal[q][:, :], total[q][:, :]).then_inc(rtotal_ready, 1)

        def softmax_share(u, q):
            n = 2 * u + q + 1
            dve.wait_ge(rtotal_ready, n)
            dve.tensor_tensor(attn[q][:, :, :], less[q][:, :, :], rtotal[q][:, :].unsqueeze(2).to_broadcast([ST, 12, S]),
                              ALU.mult).then_inc(attn_ready, 1)

        def square_slots(u, g, i):
            if inside(u - 2, UN):
                dve.wait_ge(slots_ready, u - 1)
            if inside(u - 1, UN):
                dve.wait_ge(msq_ready, u)
            sl = slots[:, bass.ds(at(g, i), HS)]
            dve.tensor_tensor(sq[:, :], sl, sl, ALU.mult).then_inc(sq_ready, 1)

        def keep_mean(u):
            dve.wait_ge(msq_ready, u + 1)
            dve.tensor_scalar(mean_sq[:, :], msq_bank, 1e-6, None, ALU.add).then_inc(mean_kept, 1)

        def unit(u, g, i, p):
            news = coming(g, i) if inside(u, UN) else []
            for n, b in news[:-1]:
                scale_keys(n, 1 - p, b)
            if inside(u, UN):
                below_max(u, 0)
                for n, b in news[-1:]:
                    scale_keys(n, 1 - p, b)
                below_max(u, 1)
                softmax_sum(u, 0)
                softmax_share(u, 0)
            if inside(u - 1, UN):
                dve.wait_ge(tanh_r_ready, u)
                dve.scalar_tensor_tensor(cand_in[:, :], tanh_r[:, :], 1.0, half_hn[:, :], ALU.add,
                                         ALU.mult).then_inc(reset_done, 1)
                sl = slots[:, bass.ds(at(g, i - 1), HS)]
                dve.wait_ge(tanh_z_ready, u)
                dve.tensor_scalar(new_share[:, :], tanh_z[:, :], -0.5, 0.5, ALU.mult, ALU.add)
                dve.wait_ge(reset_done, u)
                dve.wait_ge(xn_ready, u)
                dve.tensor_tensor(cand_in[:, :], cand_in[:, :], xn_bank, ALU.add).then_inc(cand_in_ready, 1)
                dve.scalar_tensor_tensor(old_twice[:, :], tanh_z[:, :], 1.0, sl, ALU.add, ALU.mult).then_inc(share_ready, 1)
            if inside(u, UN):
                softmax_sum(u, 1)
            if inside(u - 1, UN):
                dve.wait_ge(share_ready, u)
                dve.wait_ge(cand_ready, u)
                dve.tensor_tensor(new_share[:, :], new_share[:, :], cand[:, :], ALU.mult).then_inc(new_ready, 1)
            if inside(u, UN):
                softmax_share(u, 1)
            if inside(u - 1, UN):
                dve.wait_ge(new_ready, u)
                dve.scalar_tensor_tensor(sl, old_twice[:, :], 0.5, new_share[:, :], ALU.mult, ALU.add).then_inc(slots_ready, 1)
            if inside(u + 1, UN):
                square_slots(u + 1, g, i + 1)
            if inside(u, UN):
                take_update(u)
            if inside(u + 1, UN):
                keep_mean(u + 1)

        for b in range(GB):
            scale_keys(b, 0, b)
        square_slots(0, 0, 0)
        keep_mean(0)
        run_units(dve, unit)


def rotary_attention(core):
    nc, sem, banks, xT, d = core.nc, core.sem, core.banks, core.xT, core.d
    with ExitStack() as ctx:
        def sb(name, shape):
            return ctx.enter_context(nc.sbuf_tensor(f"r_{name}_sb", shape, F32))

        xn = sb("xn", [P, TOK])
        w = sb("w", [P, 6, D])
        turn = sb("turn", [P, 4, S])
        own_head = sb("own_head", [P, RH])
        own_batch = sb("own_batch", [P, 4])
        own_quarter = sb("own_quarter", [P, 4])
        out_b = sb("out_b", [P, 1])
        xt = [sb(f"xt{p}", [P, CH]) for p in range(2)]
        part = [sb(f"part{u}", [P, BPC, S]) for u in range(2)]
        qT = [sb(f"qT{p}", [P, CH]) for p in range(2)]
        kT = [sb(f"kT{p}", [P, CH]) for p in range(2)]
        spread = [sb(f"spread{u}", [P, 4, RH, S]) for u in range(2)]
        big = [sb(f"big{u}", [P, RH]) for u in range(2)]
        less = [sb(f"less{u}", [P, RH, S]) for u in range(2)]
        total = [sb(f"total{u}", [P, RH]) for u in range(2)]
        rtotal = [sb(f"rtotal{u}", [P, RH]) for u in range(2)]
        attn = [sb(f"attn{u}", [P, RH * S]) for u in range(2)]
        attnT = [sb(f"attnT{u}", [P, RH * S]) for u in range(2)]
        vals = [sb(f"vals{u}", [P, 4, D]) for u in range(2)]
        own = [sb(f"own{u}", [P, 4, S, 4]) for u in range(2)]
        oT = sb("oT", [P, CH])

        loaded = sem("r_loaded")
        bias_prod = sem("r_bias_prod")
        bias_ready = sem("r_bias_ready")
        xt_ready = sem("r_xt_ready")
        proj_ready = sem("r_proj_ready")
        part_ready = sem("r_part_ready")
        turned_ready = sem("r_turned_ready")
        spread_ready = sem("r_spread_ready")
        score_ready = sem("r_score_ready")
        big_ready = sem("r_big_ready")
        less_ready = sem("r_less_ready")
        exp_ready = sem("r_exp_ready")
        total_ready = sem("r_total_ready")
        rtotal_ready = sem("r_rtotal_ready")
        attn_ready = sem("r_attn_ready")
        attnT_ready = sem("r_attnT_ready")
        v_ready = sem("r_v_ready")
        vals_ready = sem("r_vals_ready")
        mix_ready = sem("r_mix_ready")
        own_ready = sem("r_own_ready")
        o_ready = sem("r_o_ready")
        y_ready = sem("r_y_ready")
        y_added = sem("r_y_added")
        Q = 4

        def at_least(eng, s, count):
            if not isinstance(count, int) or count > 0:
                eng.wait_ge(s, count)

        def load_weights(sp):
            sp.dma_start(w[:, :, :], d["r_w"]).then_inc(loaded, 16)
            sp.dma_start(turn[:, :, :], d["r_turn"]).then_inc(loaded, 16)
            sp.dma_start(own_head[:, :], d["r_own_head"]).then_inc(loaded, 16)
            sp.dma_start(own_batch[:, :], d["r_own_batch"]).then_inc(loaded, 16)
            sp.dma_start(own_quarter[:, :], d["r_own_quarter"]).then_inc(loaded, 16)

        layer_norm(core, "r_ln", xT, xn, 1e-5, beside=load_weights)
        block = ctx.enter_context(nc.Block())

        @block.gpsimd
        def _(pool):
            pool.wait_ge(loaded, 80)

            def step(c, p):
                pool.wait_ge(turned_ready, 2 * c + 1)
                for q in range(Q):
                    at_least(pool, score_ready, c * Q + q - 1)
                    for j in range(4):
                        k = kT[p][:, (4 * q + j) * S:(4 * q + j + 1) * S].unsqueeze(1).to_broadcast([P, RH, S])
                        m = own_head[:, :].unsqueeze(2).to_broadcast([P, RH, S])
                        pool.tensor_tensor(spread[q % 2][:, j, :, :], k, m, ALU.mult).then_inc(spread_ready, 1)

            run_steps(pool, step, NCH, 2)

        @block.tensor
        def _(pe):
            pe.wait_ge(loaded, 80)
            pe.matmul(banks[7][:, 0:1], w[:, 5, :], core.vec("r_bv"), start=True, stop=True).then_inc(bias_prod, 1)

            def project(c, which):
                at_least(pe, turned_ready, 2 * c + 1 - which)
                for half in range(2):
                    last = pe.matmul(banks[5 + half][:, :], w[:, 2 * which + half, :], xn[:, bass.ds(c * CH, CH)],
                                     start=True, stop=True)
                last.then_inc(proj_ready, 1)

            def values(c, p):
                pe.wait_ge(xt_ready, c + 1)
                at_least(pe, vals_ready, c * Q)
                for q in range(Q):
                    last = pe.matmul(banks[4][:, q * P:(q + 1) * P], xt[p][:, q * P:(q + 1) * P], w[:, 4, :],
                                     start=True, stop=True)
                last.then_inc(v_ready, 1)

            def scores(c, p, q):
                n = c * Q + q
                at_least(pe, less_ready, n - 1)
                if q == 0:
                    pe.wait_ge(turned_ready, 2 * c + 2)
                for j in range(4):
                    pe.wait_ge(spread_ready, 4 * n + j + 1)
                    last = pe.matmul(banks[q % 2][j * S:(j + 1) * S, :], qT[p][:, (4 * q + j) * S:(4 * q + j + 1) * S],
                                     spread[q % 2][:, j, :, :].rearrange("p h t -> p (h t)"), start=True, stop=True)
                last.then_inc(score_ready, 1)

            def mix(c, q):
                n = c * Q + q
                pe.wait_ge(attnT_ready, n + 1)
                pe.wait_ge(vals_ready, n + 1)
                for j in range(4):
                    for g in range(4):
                        last = pe.matmul(banks[2 + q % 2][g * S:(g + 1) * S, j * P:(j + 1) * P],
                                         vals[q % 2][:, j, g * S:(g + 1) * S], attnT[q % 2][:, g * P:(g + 1) * P],
                                         start=True, stop=True)
                last.then_inc(mix_ready, 1)

            def output(c):
                pe.wait_ge(o_ready, c * Q + Q)
                pe.wait_ge(bias_ready, 1)
                at_least(pe, y_added, c)
                pe.matmul(banks[7][:, :], w[:, 5, :], oT[:, :], start=True, stop=True).then_inc(y_ready, 1)

            def step(c, p):
                for q in range(Q):
                    scores(c, p, q)
                    if q == 0:
                        values(c, p)
                        if inside(c - 1, NCH):
                            mix(c - 1, Q - 1)
                        if inside(c + 1, NCH):
                            project(c + 1, 1)
                    else:
                        if q == 1 and inside(c - 1, NCH):
                            output(c - 1)
                        mix(c, q - 1)
                        if q == 2 and inside(c + 1, NCH):
                            project(c + 1, 0)

            project(0, 1)
            project(0, 0)
            run_steps(pe, step, NCH, 2)
            mix(NCH - 1, Q - 1)
            output(NCH - 1)

        @block.scalar
        def _(act):
            def copy_tile(c, p):
                act.copy(xt[p][:, :], xn[:, bass.ds(c * CH, CH)]).then_inc(xt_ready, 1)

            def step(c, p):
                for q in range(Q):
                    act.wait_ge(less_ready, c * Q + q + 1)
                    act.activation(less[q % 2][:, :, :], less[q % 2][:, :, :], ACT.Exp).then_inc(exp_ready, 1)
                    n = c * Q + q
                    act.wait_ge(v_ready, c + 1)
                    at_least(act, mix_ready, n - 1)
                    for j in range(4):
                        ins = act.activation(vals[q % 2][:, j, :], banks[4][:, q * P:(q + 1) * P], ACT.Copy,
                                             scale=own_batch[:, j:j + 1])
                    ins.then_inc(vals_ready, 1)
                    if q == 0 and inside(c + 1, NCH):
                        act.wait_ge(v_ready, c + 1)
                        copy_tile(c + 1, 1 - p)

            act.wait_ge(loaded, 80)
            copy_tile(0, 0)
            run_steps(act, step, NCH, 2)

        @block.vector
        def _(dve):
            dve.wait_ge(loaded, 80)
            dve.wait_ge(bias_prod, 1)
            dve.tensor_tensor(out_b[:, :], banks[7][:, 0:1], core.vec("r_bo"), ALU.add).then_inc(bias_ready, 1)

            def rotate(c, p, which):
                n = 2 * c + 1 - which
                dve.wait_ge(proj_ready, n + 1)
                at_least(dve, turned_ready, n)
                names = ("r_bqa", "r_bqb") if which == 0 else ("r_bka", "r_bkb")
                for half in range(2):
                    last = dve.scalar_tensor_tensor(
                        part[half][:, :, :], banks[5 + half][:, :].rearrange("p (b s) -> p b s", s=S),
                        core.vec(names[half]), turn[:, 2 * which + half, :].unsqueeze(1).to_broadcast([P, BPC, S]),
                        ALU.add, ALU.mult)
                last.then_inc(part_ready, 1)
                dve.wait_ge(part_ready, n + 1)
                dst = (qT, kT)[which][p]
                dve.tensor_tensor(dst[:, :].rearrange("p (b s) -> p b s", s=S), part[0][:, :, :], part[1][:, :, :],
                                  ALU.add).then_inc(turned_ready, 1)

            def take(c, q):
                n = c * Q + q
                u = q % 2
                dve.wait_ge(mix_ready, n + 1)
                dve.tensor_tensor(own[u][:, :, :, :].rearrange("p b s h -> p b h s"),
                                  banks[2 + u][:, :].rearrange("p (b h s) -> p b h s", b=4, h=4),
                                  own_quarter[:, :].unsqueeze(1).unsqueeze(3).to_broadcast([P, 4, 4, S]),
                                  ALU.mult).then_inc(own_ready, 1)
                if q == 0:
                    at_least(dve, y_ready, c)
                dve.wait_ge(own_ready, n + 1)
                dve.tensor_reduce(oT[:, q * P:(q + 1) * P].rearrange("p (b s) -> p b s", b=4), own[u][:, :, :, :], AX,
                                  ALU.add).then_inc(o_ready, 1)

            def add_output(c):
                dve.wait_ge(y_ready, c + 1)
                x = xT[:, bass.ds(c * CH, CH)]
                dve.scalar_tensor_tensor(x, banks[7][:, :], out_b[:, 0:1], x, ALU.add, ALU.add).then_inc(y_added, 1)

            def step(c, p):
                for q in range(Q):
                    n = c * Q + q
                    u = q % 2
                    dve.wait_ge(score_ready, n + 1)
                    s = banks[u][:, :].rearrange("p (h t) -> p h t", t=S)
                    dve.tensor_reduce(big[u][:, :], s, AX, ALU.max).then_inc(big_ready, 1)
                    dve.wait_ge(big_ready, n + 1)
                    dve.tensor_tensor(less[u][:, :, :], s, big[u][:, :].unsqueeze(2).to_broadcast([P, RH, S]),
                                      ALU.subtract).then_inc(less_ready, 1)
                    if q >= 1:
                        take(c, q - 1)
                    elif inside(c - 1, NCH):
                        take(c - 1, Q - 1)
                    if q == 1 and inside(c - 1, NCH):
                        add_output(c - 1)
                    dve.wait_ge(exp_ready, n + 1)
                    dve.tensor_reduce(total[u][:, :], less[u][:, :, :], AX, ALU.add).then_inc(total_ready, 1)
                    dve.wait_ge(total_ready, n + 1)
                    dve.reciprocal(rtotal[u][:, :], total[u][:, :]).then_inc(rtotal_ready, 1)
                    dve.wait_ge(rtotal_ready, n + 1)
                    dve.tensor_tensor(attn[u][:, :].rearrange("p (h t) -> p h t", t=S), less[u][:, :, :],
                                      rtotal[u][:, :].unsqueeze(2).to_broadcast([P, RH, S]),
                                      ALU.mult).then_inc(attn_ready, 1)
                    dve.wait_ge(attn_ready, n + 1)
                    dve.transpose(attnT[u][:, :], attn[u][:, :]).then_inc(attnT_ready, 1)
                    if inside(c + 1, NCH):
                        if q == 0:
                            rotate(c + 1, 1 - p, 1)
                        if q == 2:
                            rotate(c + 1, 1 - p, 0)

            rotate(0, 0, 1)
            rotate(0, 0, 0)
            run_steps(dve, step, NCH, 2)
            take(NCH - 1, Q - 1)
            add_output(NCH - 1)


def mlp(core):
    nc, sem, banks, xT, ident, d = core.nc, core.sem, core.banks, core.xT, core.ident, core.d
    T = CH // P
    FT = FF // P
    with ExitStack() as ctx:
        def sb(name, shape):
            return ctx.enter_context(nc.sbuf_tensor(f"f_{name}_sb", shape, F32))

        xn = sb("xn", [P, TOK])
        tile = [sb(f"tile{k}", [P, CH]) for k in range(2)]
        w1 = sb("w1", [P, FF])
        w2 = sb("w2", [P, FT, D])
        router = sb("router", [P, E])
        hidden = sb("hidden", [P, FT, CH])
        shifted = sb("shifted", [P, T, E])
        top_ex = sb("top_ex", [P, T, E])
        top = sb("top", [P, T, 2])
        big = sb("big", [P, T])
        negmax = sb("negmax", [P, T])
        ex = sb("ex", [P, T, E])
        total = sb("total", [P, T])
        rtotal = sb("rtotal", [P, T])
        pair = sb("pair", [P, T])
        rpair = sb("rpair", [P, T])
        share = sb("share", [P, T, 2])
        factor = sb("factor", [P, T])
        rows = sb("rows", [P, T, P])
        ones = sb("ones", [P, P])
        factorT = sb("factorT", [P, CH])
        mixed = sb("mixed", [P, CH])

        loaded = sem("f_loaded")
        ones_set = sem("f_ones_set")
        tile_ready = sem("f_tile_ready")
        logit_ready = sem("f_logit_ready")
        small = sem("f_small")
        exp_ready = sem("f_exp_ready")
        rows_ready = sem("f_rows_ready")
        hidden_ready = sem("f_hidden_ready")
        gelu_ready = sem("f_gelu_ready")
        factor_turned = sem("f_factor_turned")
        factor_ready = sem("f_factor_ready")
        y_ready = sem("f_y_ready")
        y_scaled = sem("f_y_scaled")
        y_added = sem("f_y_added")
        factor_sum = sem("f_factor_sum")
        NS = 9

        def load_weights(sp):
            sp.dma_start(w1[:, :], d["f_w1"]).then_inc(loaded, 16)
            sp.dma_start(w2[:, :, :], d["f_w2"]).then_inc(loaded, 16)
            sp.dma_start(router[:, :], d["f_router"]).then_inc(loaded, 16)

        layer_norm(core, "f_ln", xT, xn, 1e-5, beside=load_weights)
        block = ctx.enter_context(nc.Block())

        @block.gpsimd
        def _(pool):
            def step(c, k):
                if inside(c - 2, NCH):
                    pool.wait_ge(logit_ready, c - 1)
                pool.tensor_copy(tile[k][:, :], xn[:, bass.ds(c * CH, CH)]).then_inc(tile_ready, 1)

            run_steps(pool, step, NCH, 2)

        @block.tensor
        def _(pe):
            pe.wait_ge(loaded, 48)

            def route(c, k):
                pe.wait_ge(tile_ready, c + 1)
                if inside(c - 1, NCH):
                    pe.wait_ge(small, NS * (c - 1) + 3)
                for t in range(T):
                    last = pe.matmul(banks[0][:, t * E:(t + 1) * E], tile[k][:, t * P:(t + 1) * P], router[:, :],
                                     start=True, stop=True)
                last.then_inc(logit_ready, 1)

            def hide(c, f):
                pe.matmul(banks[1 + f][:, :], w1[:, f * P:(f + 1) * P], xn[:, bass.ds(c * CH, CH)],
                          start=True, stop=True).then_inc(hidden_ready, 1)

            def step(c, k):
                if inside(c + 1, NCH):
                    route(c + 1, 1 - k)
                pe.wait_ge(rows_ready, c + 1)
                if inside(c - 1, NCH):
                    pe.wait_ge(factor_ready, c)
                for t in range(T):
                    last = pe.transpose(banks[6][:, t * P:(t + 1) * P], rows[:, t, :], ident[:, :])
                last.then_inc(factor_turned, 1)
                if inside(c - 2, NCH):
                    pe.wait_ge(y_scaled, c - 1)
                for f in range(FT):
                    pe.wait_ge(gelu_ready, c * FT + f + 1)
                    last = pe.matmul(banks[(5, 7)[k]][:, :], w2[:, f, :], hidden[:, f, :], start=(f == 0),
                                     stop=(f == FT - 1))
                    if f == FT - 1:
                        last.then_inc(y_ready, 1)
                    if inside(c + 1, NCH):
                        hide(c + 1, f)

            route(0, 0)
            for f in range(FT):
                hide(0, f)
            run_steps(pe, step, NCH, 2)

        @block.scalar
        def _(act):
            def exponentials(c):
                act.wait_ge(small, c * NS + 3)
                act.activation(ex[:, :, :], shifted[:, :, :], ACT.Exp).then_inc(exp_ready, 1)

            def gelus(c):
                for f in range(FT):
                    act.wait_ge(hidden_ready, c * FT + f + 1)
                    act.activation(hidden[:, f, :], banks[1 + f][:, :], ACT.Gelu_apprx_tanh,
                                   bias=core.vec(f"f_b1_{f}")).then_inc(gelu_ready, 1)

            def step(c, k):
                if inside(c + 1, NCH):
                    exponentials(c + 1)
                act.wait_ge(factor_turned, c + 1)
                if inside(c - 1, NCH):
                    act.wait_ge(y_scaled, c)
                act.copy(factorT[:, :], banks[6][:, :]).then_inc(factor_ready, 1)
                if inside(c + 1, NCH):
                    gelus(c + 1)

            exponentials(0)
            gelus(0)
            run_steps(act, step, NCH, 2)

        @block.vector
        def _(dve):
            dve.memset(ones[:, :], 1.0).then_inc(ones_set, 1)
            dve.wait_ge(ones_set, 1)

            def choose(c):
                count = [0]

                def after(ins):
                    count[0] += 1
                    ins.then_inc(small, 1)
                    dve.wait_ge(small, c * NS + count[0])

                dve.wait_ge(logit_ready, c + 1)
                logits = banks[0][:, 0:T * E].rearrange("p (t e) -> p t e", t=T)
                after(dve.tensor_reduce(big[:, :], logits, AX, ALU.max))
                after(dve.tensor_scalar(negmax[:, :], big[:, :], -1.0, None, ALU.mult))
                after(dve.tensor_tensor(shifted[:, :, :], logits,
                                        negmax[:, :].unsqueeze(2).to_broadcast([P, T, E]), ALU.add))
                dve.wait_ge(exp_ready, c + 1)
                dve.tensor_reduce(total[:, :], ex[:, :, :], AX, ALU.add)
                for t in range(T):
                    last = dve.max(top_ex[:, t, :], ex[:, t, :])
                after(last)
                after(dve.reciprocal(rtotal[:, :], total[:, :]))
                after(dve.tensor_tensor(top[:, :, :], top_ex[:, :, 0:2],
                                        rtotal[:, :].unsqueeze(2).to_broadcast([P, T, 2]), ALU.mult))
                after(dve.tensor_reduce(pair[:, :], top[:, :, :], AX, ALU.add))
                after(dve.reciprocal(rpair[:, :], pair[:, :]))
                after(dve.tensor_tensor(share[:, :, :], top[:, :, :],
                                        rpair[:, :].unsqueeze(2).to_broadcast([P, T, 2]), ALU.mult))
                dve.tensor_reduce(factor[:, :], share[:, :, :], AX, ALU.add).then_inc(factor_sum, 1)

            def spread(c):
                dve.wait_ge(factor_sum, c + 1)
                if inside(c - 1, NCH):
                    dve.wait_ge(factor_turned, c)
                for t in range(T):
                    last = dve.tensor_scalar(rows[:, t, :], ones[:, :], factor[:, t:t + 1], None, ALU.mult)
                last.then_inc(rows_ready, 1)

            def step(c, k):
                if inside(c + 1, NCH):
                    choose(c + 1)
                    spread(c + 1)
                dve.wait_ge(factor_ready, c + 1)
                dve.wait_ge(y_ready, c + 1)
                if inside(c - 1, NCH):
                    dve.wait_ge(y_added, c)
                dve.scalar_tensor_tensor(mixed[:, :], banks[(5, 7)[k]][:, :], core.vec("f_b2"), factorT[:, :], ALU.add,
                                         ALU.mult).then_inc(y_scaled, 1)
                dve.wait_ge(y_scaled, c + 1)
                x = xT[:, bass.ds(c * CH, CH)]
                dve.tensor_tensor(x, x, mixed[:, :], ALU.add).then_inc(y_added, 1)

            choose(0)
            spread(0)
            run_steps(dve, step, NCH, 2)


STAGES = [cross_attention, linear_attention, experts, slot_attention, rotary_attention, mlp]


def hold_residual(core, name):
    core.xT_guard = core.nc.sbuf_tensor(name, [P, TOK], F32)
    core.xT = core.xT_guard.__enter__()


def run_stage(core, stage):
    nc, used, outer = core.nc, [], core.sem
    with ExitStack() as ctx:
        def sem(name):
            used.append(ctx.enter_context(nc.semaphore(name)))
            return used[-1]

        core.sem = sem
        stage(core)
        core.sem = outer
        with nc.Block() as block:
            @block.sync
            def _(sp):
                for s in used:
                    sp.sem_clear(s)


def build(nc, d, stages):
    core = Core()
    core.nc, core.d = nc, d
    with ExitStack() as ctx:
        core.sem = lambda name: ctx.enter_context(nc.semaphore(name))
        core.norms = [0]
        core.norm_sems = {n: core.sem(f"ln_{n}") for n in (
            "mean_ready", "centred_ready", "square_ready", "var_ready", "log_ready", "rstd_ready", "normed")}
        core.all_banks = ctx.enter_context(nc.psum_tensor("banks", [P, 8, 512], F32))
        core.banks = [core.all_banks[:, i, :] for i in range(8)]
        core.ident = ctx.enter_context(nc.sbuf_tensor("ident_sb", [P, P], F32))
        core.mean_mat = ctx.enter_context(nc.sbuf_tensor("mean_mat_sb", [P, P], F32))
        core.vecs = ctx.enter_context(nc.sbuf_tensor("vecs_sb", [P, len(VECS)], F32))
        core.eps5 = ctx.enter_context(nc.sbuf_tensor("eps5", [P, 1], F32))
        core.eps6 = ctx.enter_context(nc.sbuf_tensor("eps6", [P, 1], F32))
        scratch = lambda name, cols: nc.dram_tensor(name, (P, cols), F32, kind="Internal").ap()
        d["a_x"], d["a_x2"], d["a_xn"] = scratch("a_x", TOK), scratch("a_x2", TOK), scratch("a_xn", TOK)
        d["a_ks"] = scratch("a_ks", TOK)
        core.vec = lambda name: core.vecs[:, VCOL[name]:VCOL[name] + 1]
        core.eps_col = lambda eps: (core.eps5 if eps == 1e-5 else core.eps6)[:, 0:1]
        hold_residual(core, "xT_sb")
        load_residual(core)
        for stage in stages:
            run_stage(core, stage)
        store_residual(core)
        core.xT_guard.__exit__(None, None, None)


def lay_out(inputs):
    i = {k: np.asarray(v) for k, v in inputs.items()}
    c = np.ascontiguousarray
    wkv = i["L0_xattn_Wkv"]
    heads = lambda w: c(w.reshape(D, XH, D).transpose(2, 1, 0))
    even = np.array([RD * h + 2 * (r % (RD // 2)) for h in range(RH) for r in range(RD)])
    a = {
        "xT": c(i["x"].reshape(TOK, D).T),
        "ctx": i["ctx_1024"],
        "ident": np.eye(P, dtype=np.float32),
        "mean_mat": np.full((P, P), 1.0 / D, np.float32),
        "g_media_rows": c(np.broadcast_to(i["L0_xattn_gamma_media"], (XROWS, D))),
        "b_media_rows": c(np.broadcast_to(i["L0_xattn_beta_media"], (XROWS, D))),
        "x_wqT": heads(i["L0_xattn_Wq"]),
        "x_wkT": heads(wkv[:, :XH * D]),
        "x_wvT": heads(wkv[:, XH * D:]),
        "x_wo": c(i["L0_xattn_Wo"].reshape(XH, D, D).transpose(1, 0, 2)),
    }
    bih, bhh = i["L1_xattn_gru_bih"].reshape(3, D), i["L1_xattn_gru_bhh"].reshape(3, D)
    cols = [i["L0_xattn_gamma_media"], i["L0_xattn_beta_media"], i["L0_xattn_gamma_lat"], i["L0_xattn_beta_lat"]]
    cols += list(i["L0_xattn_bq"].reshape(XH, D)) + list(i["L0_xattn_bkv"][XH * D:].reshape(XH, D))
    cols += [i["L0_xattn_bo"], i["L0_attn_bo"], i["L1_xattn_slot_norm_w"], i["L1_xattn_input_norm_w"], *bih, *bhh]
    cols += [i["L1_attn_bq"][even], i["L1_attn_bq"][even + 1], i["L1_attn_bk"][even], i["L1_attn_bk"][even + 1]]
    cols += [i["L1_attn_bv"], i["L1_attn_bo"], *i["L1_ffn_b1"].reshape(4, D), i["L1_ffn_b2"]]
    a["vecs"] = c(np.stack(cols, axis=1))
    more_arrays(i, a, c, even)
    return a


def more_arrays(i, a, c, even):
    a["a_wq"], a["a_wk"], a["a_wv"] = i["L0_attn_Wq"], i["L0_attn_Wk"], i["L0_attn_Wv"]
    a["a_wo"] = c(i["L0_attn_Wo"].reshape(LH, LH, D))
    a["a_fold"] = c(np.tile(np.eye(LD, dtype=np.float32), (2, 2))) * np.float32(LD ** -0.5)
    a["e_w"] = c(i["L0_ffn_expert_w"].transpose(1, 0, 2))
    a["e_gate"] = i["L0_ffn_gate_w"]
    a["e_gate_b"] = i["L0_ffn_gate_b"].reshape(E, 1)
    a["e_bias"] = i["L0_ffn_expert_b"]
    a["f_w1"] = i["L1_ffn_w1"]
    a["f_w2"] = c(i["L1_ffn_w2"].reshape(FF // P, P, D).transpose(1, 0, 2))
    a["f_router"] = i["L1_ffn_router_w"]
    a["s_wq"], a["s_wk"], a["s_wv"] = i["L1_xattn_Wq"], i["L1_xattn_Wk"], i["L1_xattn_Wv"]
    a["s_ihT"] = c(i["L1_xattn_gru_wih"].reshape(3, D, D).transpose(2, 0, 1))
    a["s_hhT"] = c(i["L1_xattn_gru_whh"].reshape(3, D, D).transpose(2, 0, 1))
    w = [i["L1_attn_Wq"][even], i["L1_attn_Wq"][even + 1], i["L1_attn_Wk"][even], i["L1_attn_Wk"][even + 1]]
    a["r_w"] = c(np.stack([m.T for m in w + [i["L1_attn_Wv"], i["L1_attn_Wo"]]], axis=1))
    freq = (1.0 / 10000.0 ** (np.arange(0, RD, 2) / RD)).astype(np.float32)
    angle = np.outer(freq, np.arange(S, dtype=np.float32)).astype(np.float32)
    cos, sin = np.cos(angle), np.sin(angle)
    first, second = np.concatenate([cos, sin]), np.concatenate([-sin, cos])
    turn = np.stack([first * RD ** -0.5, second * RD ** -0.5, first, second], axis=1)
    a["r_turn"] = np.tile(turn, (RH, 1, 1)).astype(np.float32)
    rows = np.arange(P)
    a["r_own_head"] = (rows[:, None] // RD == np.arange(RH)).astype(np.float32)
    a["r_own_batch"] = (rows[:, None] // S == np.arange(4)).astype(np.float32)
    a["r_own_quarter"] = (rows[:, None] // RD % 4 == np.arange(4)).astype(np.float32)


def kernel(**inputs):
    import concourse.bacc as bacc
    from concourse.bass_utils import run_bass_kernel_spmd

    nc = bacc.Bacc("TRN2", target_bir_lowering=False, num_devices=1)
    arrays = lay_out(inputs)
    d = {n: nc.dram_tensor(n, a.shape, mybir.dt.from_np(a.dtype), kind="ExternalInput").ap() for n, a in arrays.items()}
    d["out"] = nc.dram_tensor("out", (D, TOK), F32, kind="ExternalOutput").ap()
    build(nc, d, STAGES)
    got = run_bass_kernel_spmd(nc, [arrays], core_ids=[0]).results[0]["out"]
    return np.ascontiguousarray(np.asarray(got).T).reshape(B, S, D)
```
